# Optimizing a Trainium2 kernel written in Bass

```python
import numpy as np
import jax
import jax.numpy as jnp

def _softmax(x, axis=-1):
    return jax.nn.softmax(x, axis=axis)

def _gelu(x):
    return jax.nn.gelu(x, approximate=True)

def _silu(x):
    return jax.nn.silu(x)

def _sigmoid(x):
    return jax.nn.sigmoid(x)

def _layernorm(x, axis=-1, eps=1e-05):
    m = jnp.mean(x, axis=axis, keepdims=True)
    v = jnp.var(x, axis=axis, keepdims=True)
    return (x - m) / jnp.sqrt(v + eps)

def _scatter_add(tgt, idx, src, axis=0):
    return tgt.at[idx].add(src)

def _segment_sum(src, seg, n):
    return jax.ops.segment_sum(src, seg, n)
kernel_name = 'mk_adaln_d2_jaxref_r4_a4570c'

def setup_inputs(seed: int=0):
    np.random.seed(seed)
    _w = jnp.asarray

    def _L0_attn_setup():
        import jax, jax.numpy as jnp
        import numpy as np
        B, S, QD = (2, 1024, 512)
        H, D = (32, 64)
        INNER = H * D
        key = jax.random.key(seed)
        ks = jax.random.split(key, 6)
        scale = 1.0 / np.sqrt(QD)
        return {'hidden_states': jax.random.normal(ks[0], (B, S, QD), dtype=jnp.float32), 'Wq': jax.random.normal(ks[1], (QD, INNER), dtype=jnp.float32) * scale, 'Wk': jax.random.normal(ks[2], (QD, INNER), dtype=jnp.float32) * scale, 'Wv': jax.random.normal(ks[3], (QD, INNER), dtype=jnp.float32) * scale, 'Wo': jax.random.normal(ks[4], (INNER, QD), dtype=jnp.float32) * (1.0 / np.sqrt(INNER)), 'bo': jax.random.normal(ks[5], (QD,), dtype=jnp.float32) * 0.01}
    _L0_attn_in = _L0_attn_setup()

    def _L0_ffn_setup():
        import jax, jax.numpy as jnp
        import numpy as np
        NUM_EXPERTS = 8
        TOP_K = 2
        HIDDEN = 512
        INTER = 256
        B, S = (4, 256)

        def _moe_forward(x, gate_w, gate_proj_w, up_proj_w, down_proj_w):
            Bx, Sx, H = x.shape
            T = Bx * Sx
            h = x.reshape(T, H)
            router_logits = h @ gate_w.T
            probs = jax.nn.softmax(router_logits.astype(jnp.float32), axis=-1)
            top_vals, top_idx = jax.lax.top_k(probs, TOP_K)
            top_vals = top_vals / jnp.sum(top_vals, axis=-1, keepdims=True)
            rw = jnp.zeros((T, NUM_EXPERTS), dtype=jnp.float32)
            rw = rw.at[jnp.arange(T)[:, None], top_idx].add(top_vals)
            rw = rw.astype(h.dtype)
            g = jnp.einsum('th,eih->tei', h, gate_proj_w)
            u = jnp.einsum('th,eih->tei', h, up_proj_w)
            a = jax.nn.silu(g) * u
            out_e = jnp.einsum('tei,ehi->teh', a, down_proj_w)
            out = jnp.einsum('te,teh->th', rw, out_e)
            return out.reshape(Bx, Sx, H)
        key = jax.random.key(seed)
        ks = jax.random.split(key, 5)
        sx = 1.0 / np.sqrt(HIDDEN)
        si = 1.0 / np.sqrt(INTER)
        return {'x': jax.random.normal(ks[0], (B, S, HIDDEN), dtype=jnp.float32), 'gate_w': jax.random.normal(ks[1], (NUM_EXPERTS, HIDDEN), dtype=jnp.float32) * sx, 'gate_proj_w': jax.random.normal(ks[2], (NUM_EXPERTS, INTER, HIDDEN), dtype=jnp.float32) * sx, 'up_proj_w': jax.random.normal(ks[3], (NUM_EXPERTS, INTER, HIDDEN), dtype=jnp.float32) * sx, 'down_proj_w': jax.random.normal(ks[4], (NUM_EXPERTS, HIDDEN, INTER), dtype=jnp.float32) * si}
    _L0_ffn_in = _L0_ffn_setup()
    _L0_c = _w((lambda *s: np.random.randn(*s).astype(np.float32) * 0.05)(4, 512))
    _L0_wmod = _w((lambda *s: np.random.randn(*s).astype(np.float32) * 0.05)(512, 6 * 512) * 512 ** (-0.5))

    def _L1_attn_setup():
        import jax, jax.numpy as jnp
        import numpy as np
        D, NC, DS = (512, 2, 16)
        B, L = (2, 128)

        def _rmsnorm(x, w):
            eps = jnp.asarray(jnp.finfo(x.dtype).eps, x.dtype)
            ms = jnp.mean(jnp.square(x), axis=-1, keepdims=True)
            return x * jax.lax.rsqrt(ms + eps) * w

        def _reference_tuple_inner(x, W_in, W_out, A_theta, B_real, B_imag, C_real, C_imag, norm_w):
            b, l, _ = x.shape
            xi = (x @ W_in.T).reshape(b, l, NC, D)[..., None]
            ct = jnp.cos(A_theta)
            st = jnp.sin(A_theta)
            rs = jnp.zeros((b, l, NC, D, DS), dtype=x.dtype)
            is_ = jnp.zeros_like(rs)
            bxr = B_real * xi
            bxi = B_imag * xi
            nr = ct * rs - st * is_ + bxr
            ni = st * rs + ct * is_ + bxi
            y = jnp.sum(C_real * nr - C_imag * ni, axis=-1)
            out = y.reshape(b, l, NC * D) @ W_out.T
            return (x + _rmsnorm(out, norm_w), nr, ni)
        key = jax.random.key(seed)
        ks = jax.random.split(key, 9)
        x = jax.random.normal(ks[0], (B, L, D), dtype=jnp.float32)
        W_in = jax.random.normal(ks[1], (NC * D, D), dtype=jnp.float32) * 0.02
        W_out = jax.random.normal(ks[2], (D, NC * D), dtype=jnp.float32) * 0.02
        A_theta = jax.random.normal(ks[3], (NC, D, DS), dtype=jnp.float32) * 0.1
        B_real = jax.random.normal(ks[4], (NC, D, DS), dtype=jnp.float32) * 0.1
        B_imag = jax.random.normal(ks[5], (NC, D, DS), dtype=jnp.float32) * 0.1
        C_real = jax.random.normal(ks[6], (NC, D, DS), dtype=jnp.float32) * 0.1
        C_imag = jax.random.normal(ks[7], (NC, D, DS), dtype=jnp.float32) * 0.1
        norm_w = jnp.ones((D,), dtype=jnp.float32)
        return {'x': x, 'W_in': W_in, 'W_out': W_out, 'A_theta': A_theta, 'B_real': B_real, 'B_imag': B_imag, 'C_real': C_real, 'C_imag': C_imag, 'norm_w': norm_w}
    _L1_attn_in = _L1_attn_setup()

    def _L1_ffn_setup():
        import jax, jax.numpy as jnp
        import numpy as np

        def _sparsify_2to4(h):
            B, S, I = h.shape
            g = h.reshape(B, S, I // 4, 4)
            a = jnp.abs(g)
            _, idx = jax.lax.top_k(a, 2)
            pos = jnp.arange(4)
            mask = (pos == idx[..., 0:1]) | (pos == idx[..., 1:2])
            return (g * mask.astype(g.dtype)).reshape(B, S, I)
        key = jax.random.key(seed)
        k1, k2, k3, k4 = jax.random.split(key, 4)
        B, S, H, I = (4, 512, 512, 2048)
        x = jax.random.normal(k1, (B, S, H), dtype=jnp.float32)
        w_gate = jax.random.normal(k2, (H, I), dtype=jnp.float32) / np.sqrt(H)
        w_up = jax.random.normal(k3, (H, I), dtype=jnp.float32) / np.sqrt(H)
        w_down = jax.random.normal(k4, (I, H), dtype=jnp.float32) / np.sqrt(I)
        return {'x': x, 'w_gate': w_gate, 'w_up': w_up, 'w_down': w_down}
    _L1_ffn_in = _L1_ffn_setup()
    _L1_c = _w((lambda *s: np.random.randn(*s).astype(np.float32) * 0.05)(4, 512))
    _L1_wmod = _w((lambda *s: np.random.randn(*s).astype(np.float32) * 0.05)(512, 6 * 512) * 512 ** (-0.5))
    _d = {'L0_attn_hidden_states': _L0_attn_in['hidden_states'], 'L0_attn_Wq': _L0_attn_in['Wq'], 'L0_attn_Wk': _L0_attn_in['Wk'], 'L0_attn_Wv': _L0_attn_in['Wv'], 'L0_attn_Wo': _L0_attn_in['Wo'], 'L0_attn_bo': _L0_attn_in['bo'], 'L0_ffn_gate_w': _L0_ffn_in['gate_w'], 'L0_ffn_gate_proj_w': _L0_ffn_in['gate_proj_w'], 'L0_ffn_up_proj_w': _L0_ffn_in['up_proj_w'], 'L0_ffn_down_proj_w': _L0_ffn_in['down_proj_w'], 'L0_c': _L0_c, 'L0_wmod': _L0_wmod, 'L1_attn_W_in': _L1_attn_in['W_in'], 'L1_attn_W_out': _L1_attn_in['W_out'], 'L1_attn_A_theta': _L1_attn_in['A_theta'], 'L1_attn_B_real': _L1_attn_in['B_real'], 'L1_attn_B_imag': _L1_attn_in['B_imag'], 'L1_attn_C_real': _L1_attn_in['C_real'], 'L1_attn_C_imag': _L1_attn_in['C_imag'], 'L1_attn_norm_w': _L1_attn_in['norm_w'], 'L1_ffn_w_gate': _L1_ffn_in['w_gate'], 'L1_ffn_w_up': _L1_ffn_in['w_up'], 'L1_ffn_w_down': _L1_ffn_in['w_down'], 'L1_c': _L1_c, 'L1_wmod': _L1_wmod}
    _x0 = _d['L0_attn_hidden_states']
    _d['L0_attn_hidden_states'] = jax.random.normal(jax.random.fold_in(jax.random.key(seed), 1), (4, 512, 512), dtype=_x0.dtype)
    del _x0
    return _d

def reference(L0_attn_hidden_states, L0_attn_Wq, L0_attn_Wk, L0_attn_Wv, L0_attn_Wo, L0_attn_bo, L0_ffn_gate_w, L0_ffn_gate_proj_w, L0_ffn_up_proj_w, L0_ffn_down_proj_w, L0_c, L0_wmod, L1_attn_W_in, L1_attn_W_out, L1_attn_A_theta, L1_attn_B_real, L1_attn_B_imag, L1_attn_C_real, L1_attn_C_imag, L1_attn_norm_w, L1_ffn_w_gate, L1_ffn_w_up, L1_ffn_w_down, L1_c, L1_wmod):

    def _L0_attn_ref(hidden_states, Wq, Wk, Wv, Wo, bo):
        import jax, jax.numpy as jnp
        import numpy as np
        B, S, QD = (2, 1024, 512)
        H, D = (32, 64)
        INNER = H * D
        b, s, _ = hidden_states.shape

        def proj(W):
            return (hidden_states @ W).reshape(b, s, H, D).transpose(0, 2, 1, 3)
        q = jax.nn.relu(proj(Wq))
        k = jax.nn.relu(proj(Wk))
        v = proj(Wv)
        kv = jnp.einsum('bhsd,bhse->bhde', k, v)
        qkv = jnp.einsum('bhsd,bhde->bhse', q, kv)
        key_sum = k.sum(axis=2)
        normalizer = jnp.einsum('bhsd,bhd->bhs', q, key_sum)
        normalizer = jnp.clip(normalizer, 1e-06, None)[..., None]
        out = qkv / normalizer
        out = out.transpose(0, 2, 1, 3).reshape(b, s, INNER)
        return out @ Wo + bo

    def _L0_ffn_ref(x, gate_w, gate_proj_w, up_proj_w, down_proj_w):
        import jax, jax.numpy as jnp
        import numpy as np
        NUM_EXPERTS = 8
        TOP_K = 2
        HIDDEN = 512
        INTER = 256
        B, S = (4, 256)

        def _moe_forward(x, gate_w, gate_proj_w, up_proj_w, down_proj_w):
            Bx, Sx, H = x.shape
            T = Bx * Sx
            h = x.reshape(T, H)
            router_logits = h @ gate_w.T
            probs = jax.nn.softmax(router_logits.astype(jnp.float32), axis=-1)
            top_vals, top_idx = jax.lax.top_k(probs, TOP_K)
            top_vals = top_vals / jnp.sum(top_vals, axis=-1, keepdims=True)
            rw = jnp.zeros((T, NUM_EXPERTS), dtype=jnp.float32)
            rw = rw.at[jnp.arange(T)[:, None], top_idx].add(top_vals)
            rw = rw.astype(h.dtype)
            g = jnp.einsum('th,eih->tei', h, gate_proj_w)
            u = jnp.einsum('th,eih->tei', h, up_proj_w)
            a = jax.nn.silu(g) * u
            out_e = jnp.einsum('tei,ehi->teh', a, down_proj_w)
            out = jnp.einsum('te,teh->th', rw, out_e)
            return out.reshape(Bx, Sx, H)
        return _moe_forward(x, gate_w, gate_proj_w, up_proj_w, down_proj_w)

    def _L1_attn_ref(x, W_in, W_out, A_theta, B_real, B_imag, C_real, C_imag, norm_w):
        import jax, jax.numpy as jnp
        import numpy as np
        D, NC, DS = (512, 2, 16)
        B, L = (2, 128)

        def _rmsnorm(x, w):
            eps = jnp.asarray(jnp.finfo(x.dtype).eps, x.dtype)
            ms = jnp.mean(jnp.square(x), axis=-1, keepdims=True)
            return x * jax.lax.rsqrt(ms + eps) * w

        def _reference_tuple_inner(x, W_in, W_out, A_theta, B_real, B_imag, C_real, C_imag, norm_w):
            b, l, _ = x.shape
            xi = (x @ W_in.T).reshape(b, l, NC, D)[..., None]
            ct = jnp.cos(A_theta)
            st = jnp.sin(A_theta)
            rs = jnp.zeros((b, l, NC, D, DS), dtype=x.dtype)
            is_ = jnp.zeros_like(rs)
            bxr = B_real * xi
            bxi = B_imag * xi
            nr = ct * rs - st * is_ + bxr
            ni = st * rs + ct * is_ + bxi
            y = jnp.sum(C_real * nr - C_imag * ni, axis=-1)
            out = y.reshape(b, l, NC * D) @ W_out.T
            return (x + _rmsnorm(out, norm_w), nr, ni)
        return _reference_tuple_inner(x, W_in, W_out, A_theta, B_real, B_imag, C_real, C_imag, norm_w)[0]

    def _L1_ffn_ref(x, w_gate, w_up, w_down):
        import jax, jax.numpy as jnp
        import numpy as np

        def _sparsify_2to4(h):
            B, S, I = h.shape
            g = h.reshape(B, S, I // 4, 4)
            a = jnp.abs(g)
            _, idx = jax.lax.top_k(a, 2)
            pos = jnp.arange(4)
            mask = (pos == idx[..., 0:1]) | (pos == idx[..., 1:2])
            return (g * mask.astype(g.dtype)).reshape(B, S, I)
        h = jax.nn.silu(jnp.einsum('bsh,hi->bsi', x, w_gate)) * jnp.einsum('bsh,hi->bsi', x, w_up)
        h_sparse = _sparsify_2to4(h)
        return jnp.einsum('bsi,ih->bsh', h_sparse, w_down)
    x = L0_attn_hidden_states
    mod = (_silu(L0_c) @ L0_wmod).reshape(L0_c.shape[0], 6, 1, -1)
    sa, ca, ga, sb, cb, gb = (mod[:, 0], mod[:, 1], mod[:, 2], mod[:, 3], mod[:, 4], mod[:, 5])
    ga = (2 * (ga >= 0) - 1) * jnp.maximum(jnp.abs(ga), 0.25)
    gb = (2 * (gb >= 0) - 1) * jnp.maximum(jnp.abs(gb), 0.25)
    h = _layernorm(x, axis=-1) * (1 + ca) + sa
    x = x + ga * _L0_attn_ref(h, L0_attn_Wq, L0_attn_Wk, L0_attn_Wv, L0_attn_Wo, L0_attn_bo)
    h = _layernorm(x, axis=-1) * (1 + cb) + sb
    x = x + gb * _L0_ffn_ref(h, L0_ffn_gate_w, L0_ffn_gate_proj_w, L0_ffn_up_proj_w, L0_ffn_down_proj_w)
    mod = (_silu(L1_c) @ L1_wmod).reshape(L1_c.shape[0], 6, 1, -1)
    sa, ca, ga, sb, cb, gb = (mod[:, 0], mod[:, 1], mod[:, 2], mod[:, 3], mod[:, 4], mod[:, 5])
    ga = (2 * (ga >= 0) - 1) * jnp.maximum(jnp.abs(ga), 0.25)
    gb = (2 * (gb >= 0) - 1) * jnp.maximum(jnp.abs(gb), 0.25)
    h = _layernorm(x, axis=-1) * (1 + ca) + sa
    x = x + ga * _L1_attn_ref(h, L1_attn_W_in, L1_attn_W_out, L1_attn_A_theta, L1_attn_B_real, L1_attn_B_imag, L1_attn_C_real, L1_attn_C_imag, L1_attn_norm_w)
    h = _layernorm(x, axis=-1) * (1 + cb) + sb
    x = x + gb * _L1_ffn_ref(h, L1_ffn_w_gate, L1_ffn_w_up, L1_ffn_w_down)
    return x

_drawn_inputs = setup_inputs


def setup_inputs(seed=0):
    import zlib

    import numpy as np

    out = dict(_drawn_inputs(seed))
    spreads = {'L1_attn_norm_w': (1.0, 0.2)}
    factors = {'L0_attn_Wq': 8.0,
     'L0_attn_Wk': 7.073,
     'L0_attn_Wv': 3.811,
     'L0_attn_Wo': 3.729,
     'L0_attn_bo': 8.0}
    for name, (base, spread) in spreads.items():
        noise = np.random.default_rng([zlib.crc32(name.encode()), seed]).standard_normal(out[name].shape)
        drawn = base * np.exp(spread * noise) if base else spread * noise
        out[name] = jnp.asarray(drawn.astype(out[name].dtype))
    for name, factor in factors.items():
        out[name] = (out[name] * factor).astype(out[name].dtype)
    return out
```

```python
from contextlib import ExitStack

import concourse.bass as bass
from concourse import mybir

F32 = mybir.dt.float32
F32R = mybir.dt.float32r
BF16 = mybir.dt.bfloat16
I32 = mybir.dt.int32
U32 = mybir.dt.uint32
ALU = mybir.AluOpType
ACT = mybir.ActivationFunctionType
AX_X = mybir.AxisListType.X

P = 128
NB = 4
S = 512
H = 512
NT = S // P
NC = H // P
GA = 8
GE = 8
GD = 4
HD = 64
VW = 2 * HD + 2
DS = 16
EPS = 1e-5
EPS_RMS = float(2.0 ** -23)
MAGIC = 1597463007.0
HI, LO = 0, 1
R_GA0, R_GB0, R_P1, R_Q1, R_R1, R_GB1 = range(6)
SA, CA, GAT, SB, CB, GBT = range(6)
COL_KIND = {SA: 0, CA: 1, SB: 2, CB: 3}
ROW_PART = [(0, GAT), (0, GBT), (1, SA), (1, CA), (1, GAT), (1, GBT)]
NSA, NSB, NSD = 4, 4, 6
BASE_B = NSA * GA
BASE_D = BASE_B + NSB * GE


def layernorms(stage, g, b):
    nxt = {"A": 1, "B": 2}.get(stage)
    if stage == "C":
        return (2, b + 2) if b < 2 else (3, b - 2)
    if isinstance(g, int) and g == 0 and b < 2:
        return {"A": 0, "B": 1, "D": 3}[stage], b + 2
    if nxt and isinstance(g, int) and g == 7 and b >= 2:
        return nxt, b - 2
    return None


def ln_index(k, b):
    return k * NB + b


def routed(stage, g, b):
    if stage == "A" and isinstance(g, int) and g == GA - 1 and b == 3:
        return 0
    if stage == "B" and isinstance(g, int) and g == 0 and b < 3:
        return b + 1
    return None


def tail_of(stage, g, b):
    if b > 0:
        return (stage, g, b - 1) if stage != "C" else None
    if isinstance(g, int) and g == 0:
        return {"A": None, "B": ("A", GA - 1, 3), "C": ("B", GE - 1, 3), "D": None}[stage]
    return stage, g - 1, 3


def plan_ring():
    at, n = {("ln", 0, 0): 0, ("ln", 0, 1): NT}, 2 * NT
    for stage, groups in (("A", GA), ("B", GE), ("C", 1), ("D", GD)):
        for g in range(groups):
            for b in range(NB):
                tail = tail_of(stage, g, b)
                if tail:
                    at[("tail", *tail)] = n
                    n += NT
                ln = layernorms(stage, g, b)
                if ln:
                    at[("ln", *ln)] = n
                    n += NC
                rt = routed(stage, g, b)
                if rt is not None:
                    at[("rt", rt)] = n
                    n += 1
    at[("tail", "D", GD - 1, 3)] = n
    return at


RING = plan_ring()


def ring_at(stage, g, b):
    if isinstance(g, int):
        return RING[("tail", stage, g, b)]
    return g * (NB * NT) + (RING[("tail", stage, 1, b)] - NB * NT)


def ring_before(stage, g, b):
    tail = tail_of(stage, g, b)
    if tail is None:
        return None
    if isinstance(g, int):
        return RING[("tail", *tail)]
    if b > 0:
        return ring_at(stage, g, b - 1)
    return g * (NB * NT) + (RING[("tail", stage, 0, 3)] - NB * NT)


def walk(eng, pro, step_a, step_b, step_c, step_d, epi):
    pro()
    for step, groups in ((step_a, GA), (step_b, GE), (step_c, 0), (step_d, GD)):
        if groups == 0:
            for b in range(NB):
                step(b)
            continue
        for b in range(NB):
            step(0, b)
        with eng.Fori(1, groups - 1) as g:
            for b in range(NB):
                step(g, b)
        for b in range(NB):
            step(groups - 1, b)
    epi()


def build(nc, x_in, wa, wbe, wdn, winout, coef, cT, wmod0, wmod1, gwT, bo, norm_w, out, rows_d):
    with ExitStack() as ctx:
        def sb(name, shape, dt=F32):
            return ctx.enter_context(nc.sbuf_tensor(name, shape, dt))

        def sem(name):
            return ctx.enter_context(nc.semaphore(name))

        x = sb("x", [P, NB * NT, H])
        hT = sb("hT", [P, 2, NC, NB * S], F32R)
        stage = sb("stage", [P, 2, 1024])
        tmp = sb("tmp", [P, 2, S])
        row = sb("row", [P, 2, H])
        xn = sb("xn", [P, NT, H])
        ident = sb("ident", [P, P])
        modc = sb("modc", [P, 4, 2, NC, NB])
        scT = sb("scT", [P, 2, NC, NB])
        cTs = sb("cTs", [P, 2, NC, NB])
        kcoef = sb("kcoef", [P, 8])
        st6 = sb("st6", [P, NT, 6])
        mv = sb("mv", [P, NT, 2])
        ve = sb("ve", [P, NT])
        na = sb("na", [P, NT])
        rstd = sb("rstd", [P, NT])
        ssum = sb("ssum", [P, NT])
        gw = sb("gw", [P, 2, NC, 8], F32R)
        rw = sb("rw", [P, NB * NT, 8])
        rwe = sb("rwe", [P, NB * NT])
        iota8 = sb("iota8", [P, 8])
        gwr = sb("gwr", [P, NC, 8])
        lg = sb("lg", [P, NT, 8])
        pe8 = sb("pe8", [P, NT, 8])
        m4 = sb("m4", [P, 2, NT])
        v8 = sb("v8", [P, NT, 8])
        i8 = sb("i8", [P, NT, 8], U32)
        sel = sb("sel", [P, 2, NT, 8])

        def shared(makers):
            outs = []
            for maker in makers:
                with ExitStack() as part:
                    outs.append(maker(lambda name, shape, dt=F32: part.enter_context(
                        nc.sbuf_tensor(name, shape, dt))))
            return outs

        (W1a, mstage) = shared([lambda a: a("W1a", [P, 4096], F32R), lambda a: a("mstage", [P, 4, 1024])])
        hold1 = sb("hold1", [P, 4096])
        W1b = sb("W1b", [P, 4096], F32R)
        (W2, (prow, ptmp)) = shared([lambda a: a("W2", [P, 4096], F32R),
                                     lambda a: (a("prow", [NB, 6, H]), a("ptmp", [NB, 2, H]))])
        hold2 = sb("hold2", [P, 4096])

        def over_pro(a):
            return a("wm", [P, 4, NC * H]), a("cin", [P, 5, 8, DS])

        def over_a(a):
            return (a("kt", [P, 2, 2, 256], F32R), a("vt", [P, 2, 2, 2, VW], F32R), a("qt", [P, 2, 2, S], F32R),
                    a("ot", [P, 2, 2, S], F32R), a("kvb", [P, 2, 2, 2, P], F32R), a("rr", [P, 2, S]),
                    a("bor", [P, H]))

        def over_b(a):
            return (a("sg", [P, 2, S]), a("pr", [P, 2, S]), a("ab", [P, 2, 2, S], F32R),
                    a("Wd", [P, 2, 2, 512], F32R), a("crow", [P, 3, H]), a("sqj", [P, S], BF16),
                    a("ct", [P, 2, S]))

        def over_d(a):
            return (a("hh", [P, 4, S]), a("mx", [P, S]), a("fl", [P, 6, S], BF16), a("ad", [P, 4, 2, S], F32R))

        ((wm, cin), (kt, vt, qt, ot, kvb, rr, bor), (sg, pr, ab, Wd, crow, sqj, ct),
         (hh, mx, fl, ad)) = shared([over_pro, over_a, over_b, over_d])
        hold3 = sb("hold3", [P, 9000])

        wkv = W1a[:, :].rearrange("p (s c n) -> p s c n", s=2, c=NC)
        wq = W1b[:, 0:2048].rearrange("p (s c n) -> p s c n", s=2, c=NC)
        wo = W1b[:, 2048:4096].rearrange("p (s c n) -> p s c n", s=2, c=2)
        gu = W2[:, :].rearrange("p (i s u c n) -> p i s u c n", i=2, s=2, u=2, c=NC)
        M = W1b[:, :].rearrange("p (s c n) -> p s c n", s=2, c=NC)
        gud = [w[:, :].rearrange("p (r s u c n) -> p r s u c n", r=2, s=2, u=2, c=NC) for w in (W1a, W1b)]
        wdd = W2[:, :].rearrange("p (s r n) -> p s r n", s=2, r=4)
        ab4 = xn

        bank = [ctx.enter_context(nc.psum_tensor(f"bank{i}", [P, 512], F32)) for i in range(8)]
        TAIL = bank[2:4]
        YB = [0, 1, 4, 5, 6, 7]

        x_in_s = [sem(f"x_loaded{b}") for b in range(NB)]
        small_loaded = sem("small_loaded")
        bo_loaded = sem("bo_loaded")
        wm_loaded = [sem(f"wmod_loaded{i}") for i in range(4)]
        nw_loaded = sem("norm_w_loaded")
        gw_loaded = sem("router_weights_loaded")
        zeroed = sem("identity_zeroed")
        silu_c = sem("silu_c_done")
        col_full = sem("mod_columns_full")
        col_done = sem("mod_columns_done")
        rowp_full = sem("mod_row_full")
        rowp_done = sem("mod_row_done")
        rows_ready = sem("rows_ready")
        rows_stored = sem("rows_stored")
        const_ready = sem("constants_ready")
        gw_hi_s = sem("router_weights_hi")
        gw_ready = sem("router_weights_ready")
        aconst = sem("stage_a_constants")
        pchain = sem("prologue_chain")
        stage_full = [sem(f"stage_full{i}") for i in range(2)]
        split_hi = sem("split_hi")
        split_done = sem("split_done")
        row_full = [sem(f"row_full{i}") for i in range(2)]
        crow_full = [sem(f"crow_full{i}") for i in range(3)]
        ring_full = sem("ring_full")
        ring_read = sem("ring_read")
        ring_done = sem("ring_done")
        ln_chain = sem("ln_chain")
        xn_ready = sem("xn_ready")
        h_hi = sem("h_hi")
        pq_mul = sem("pq_mul")
        pq_sum = sem("pq_sum")
        pq_add = sem("pq_added")
        pj_full = sem("a_proj_full")
        pj_hi = sem("a_proj_hi")
        pj_lo = sem("a_proj_lo")
        kvmm = sem("a_kv_accumulated")
        kvb_hi = sem("a_kvb_hi")
        kvb_lo = sem("a_kvb_lo")
        nn_full = sem("a_norm_num_full")
        r_max = sem("a_norm_clipped")
        r_rec = sem("a_norm_inverted")
        o_num = sem("a_out_normalised")
        o_hi = sem("a_out_hi")
        o_lo = sem("a_out_lo")
        bo_add = sem("a_bias_added")
        bg_full = sem("b_gate_full")
        bu_full = sem("b_up_full")
        b_silu = sem("b_silu_done")
        b_p = sem("b_product_done")
        b_hi = sem("b_act_hi")
        b_lo = sem("b_act_lo")
        rwe_done = sem("b_rwe_done")
        m_loaded = [sem(f"m_loaded{i}") for i in range(4)]
        m_scaled = sem("m_scaled")
        m_used = sem("m_used")
        m_hi = sem("m_hi")
        m_lo = sem("m_lo")
        rt_chain = sem("router_chain")
        rt_sub = sem("router_shifted")
        rt_exp = sem("router_exp")
        y_full = sem("c_y_full")
        y_sq = sem("c_y_squared")
        y_read = sem("c_y_read")
        c_add = sem("c_x_added")
        dg_full = sem("d_gate_full")
        du_full = sem("d_up_full")
        d_silu = sem("d_silu_done")
        d_h = sem("d_h_done")
        d_abs = sem("d_abs_done")
        d_sp = sem("d_sparsify_chain")
        d_hi = sem("d_act_hi")
        d_lo = sem("d_act_lo")
        out_stored = sem("out_stored")

        block = ctx.enter_context(nc.Block())
        NSP = 17

        @block.sync
        def _(sp):
            sp.dma_start(cTs[:, :, :, :], cT).then_inc(small_loaded, 16)
            sp.dma_start(cin[:, :, :, :], coef).then_inc(small_loaded, 16)

            def wmod_part(n):
                src = (wmod0, wmod1)[n // 6][n % 6]
                if n >= 4:
                    sp.wait_ge(col_full, sum(m % 6 in COL_KIND for m in range(n - 3)))
                    if any((m // 6, m % 6) in ROW_PART for m in range(n - 3)):
                        sp.wait_ge(rowp_full, sum((m // 6, m % 6) in ROW_PART for m in range(n - 3)))
                sp.dma_start(wm[:, n % 4, :], src).then_inc(wm_loaded[n % 4], 16)

            def raw(n, j, src, size):
                if not (isinstance(n, int) and n < 2):
                    sp.wait_ge(split_done, n - 1)
                sp.dma_start(stage[:, j % 2, 0:size], src).then_inc(stage_full[j % 2], 16)

            def wa_slice(g, j):
                raw(g * NSA + j, j, wa[bass.ds(g, 1), :, j, :].rearrange("a p n -> p (a n)"), 1024)

            def wb_slice(e, j):
                n = e * NSB + (BASE_B + j)
                off, size = ((0, 1024), (1024, 1024), (2048, 512), (2560, 512))[j]
                raw(n, j, wbe[bass.ds(e, 1), :, off:off + size].rearrange("a p n -> p (a n)"), size)

            def wd_slice(g, j):
                raw(g * NSD + (BASE_D + j), j, wdn[bass.ds(g, 1), :, j, :].rearrange("a p n -> p (a n)"), 1024)

            def pro():
                wmod_part(0)
                wmod_part(1)
                wa_slice(0, 0)
                wa_slice(0, 1)
                wmod_part(2)
                wmod_part(3)
                wa_slice(0, 2)
                wa_slice(0, 3)
                for n in range(4, 12):
                    wmod_part(n)
                sp.wait_ge(rows_ready, 1)
                sp.dma_start(rows_d.rearrange("k b n -> b k n"), prow[:, :, :]).then_inc(rows_stored, 16)

            def step_a(g, b):
                if isinstance(g, int) and g == 0 and b == 0:
                    sp.wait_ge(aconst, 1)
                    sp.dma_start(bor[:, :], bo.partition_broadcast(P)).then_inc(bo_loaded, 16)
                if b == 2 and not (isinstance(g, int) and g == GA - 1):
                    for j in range(3):
                        wa_slice(g + 1, j)
                if b == 0 and not (isinstance(g, int) and g == 0):
                    wa_slice(g, 3)
                if b == 2 and isinstance(g, int) and g == GA - 1:
                    wb_slice(0, 0)
                    wb_slice(0, 1)

            def m_load(n):
                if n >= 4:
                    sp.wait_ge(m_used, n - 3)
                else:
                    sp.wait_ge(pj_full, 6 * NB * GA)
                sp.dma_start(mstage[:, n % 4, :], winout[n % 8]).then_inc(m_loaded[n % 4], 16)

            def step_b(e, b):
                if b == 0:
                    wb_slice(e, 2)
                    wb_slice(e, 3)
                if isinstance(e, int) and e == 0:
                    for n in range(4 * b, 4 * b + 4):
                        m_load(n)
                if b == 2 and not (isinstance(e, int) and e == GE - 1):
                    wb_slice(e + 1, 0)
                    wb_slice(e + 1, 1)
                if b == 3 and isinstance(e, int) and e == GE - 1:
                    wd_slice(0, 0)
                    wd_slice(0, 1)

            def step_c(b):
                if b == 3:
                    wd_slice(0, 2)
                    wd_slice(0, 3)

            def step_d(g, b):
                if b == 0:
                    wd_slice(g, 4)
                    wd_slice(g, 5)
                if b == 2 and not (isinstance(g, int) and g == GD - 1):
                    for j in range(4):
                        wd_slice(g + 1, j)
                if isinstance(g, int) and g == GD - 1 and b >= 1:
                    store(b - 1)

            def store(b):
                sp.wait_ge(ring_done, RING[("tail", "D", GD - 1, b)] + NT)
                sp.dma_start(out[b].rearrange("(t p) n -> p t n", p=P),
                             x[:, b * NT:(b + 1) * NT, :]).then_inc(out_stored, 16)

            def epi():
                store(3)
                sp.wait_ge(out_stored, 16 * NB)
                sp.wait_ge(rows_stored, 16)

            walk(sp, pro, step_a, step_b, step_c, step_d, epi)

        @block.tensor
        def _(pe):
            def mm3(o, lhs, rhs, start, stop, **kw):
                pe.matmul(o, lhs(HI), rhs(HI), start=start, stop=False, **kw)
                pe.matmul(o, lhs(HI), rhs(LO), start=False, stop=False, **kw)
                return pe.matmul(o, lhs(LO), rhs(HI), start=False, stop=stop, **kw)

            def hcol(c, b, t):
                return lambda s: hT[:, s, c, b * S + t * P:b * S + (t + 1) * P]

            def hrow(c, b):
                return lambda s: hT[:, s, c, b * S:(b + 1) * S]

            def ring_slot(n, par):
                if not (isinstance(n, int) and n < 2):
                    pe.wait_ge(ring_read, n - 1)
                return TAIL[par]

            def par_of(stage, g, b, t):
                base = RING[("tail", stage, g if isinstance(g, int) else 1, b)]
                return (base + t) % 2

            def ln_transposes(k, b):
                n0 = RING[("ln", k, b)]
                pe.wait_ge(xn_ready, ln_index(k, b) + 1)
                for c in range(NC):
                    o = ring_slot(n0 + c, (n0 + c) % 2)
                    for t in range(NT):
                        last = pe.transpose(o[:, t * P:(t + 1) * P], xn[:, t, c * P:(c + 1) * P], ident[:, :])
                    last.then_inc(ring_full, 1)

            def need_h(k, b):
                pe.wait_ge(ring_done, RING[("ln", k, b)] + NC)

            def router(b):
                n = RING[("rt", b)]
                need_h(1, b)
                pe.wait_ge(gw_ready, 1)
                o = ring_slot(n, n % 2)
                for t in range(NT):
                    for c in range(NC):
                        last = mm3(o[:, t * 8:(t + 1) * 8], hcol(c, b, t), lambda s, c=c: gw[:, s, c, :],
                                   c == 0, c == NC - 1)
                last.then_inc(ring_full, 1)

            def extras(stage_, g, b):
                ln = layernorms(stage_, g, b)
                if ln:
                    ln_transposes(*ln)
                rt = routed(stage_, g, b)
                if rt is not None:
                    router(rt)

            def pro():
                pe.wait_ge(silu_c, 1)
                cols, rows = COL_KIND, ROW_PART
                for n in range(12):
                    layer, kind = n // 6, n % 6
                    w = wm[:, n % 4, :].rearrange("p (c n) -> p c n", c=NC)
                    pe.wait_ge(wm_loaded[n % 4], 16 * (n // 4 + 1))
                    if kind in cols:
                        k, sc = 2 * layer + cols[kind] // 2, cols[kind] % 2
                        o = bank[0 if k == 0 else 1]
                        for m in range(NC):
                            at = ((k % 4) * 2 + sc) * 16 + m * NB
                            for c in range(NC):
                                last = pe.matmul(o[:, at:at + NB], w[:, c, m * P:(m + 1) * P],
                                                 scT[:, layer, c, :], start=c == 0, stop=c == NC - 1)
                        last.then_inc(col_full, 1)
                    if (layer, kind) in rows:
                        i = rows.index((layer, kind))
                        if i >= 2:
                            pe.wait_ge(rowp_done, i - 1)
                        for c in range(NC):
                            last = pe.matmul(bank[6 + i % 2][0:NB, :], scT[:, layer, c, :], w[:, c, :],
                                             start=c == 0, stop=c == NC - 1)
                        last.then_inc(rowp_full, 1)
                pe.wait_ge(const_ready, 1)
                ln_transposes(0, 0)
                ln_transposes(0, 1)

            def tail_a(g, b, n0):
                s = g * NB + b
                pe.wait_ge(o_lo, s * 2 + 2)
                if b == 0:
                    pe.wait_ge(split_done, g * NSA + 4)
                for t in range(NT):
                    o = ring_slot(n0 + t, par_of("A", g, b, t))
                    for c in range(2):
                        last = mm3(o[:, :], lambda h, c=c: ot[:, h, c, t * P:(t + 1) * P],
                                   lambda h, c=c: wo[:, h, c, :], c == 0, c == 1)
                    last.then_inc(ring_full, 1)

            def tails(stage_, g, b):
                tail = tail_of(stage_, g, b)
                if tail is None:
                    return
                n0 = ring_before(stage_, g, b)
                {"A": tail_a, "B": tail_b, "D": tail_d}[tail[0]](tail[1], tail[2], n0)

            def step_a(g, b):
                s = g * NB + b
                first = isinstance(g, int) and g == 0
                if first:
                    need_h(0, b)
                    if b == 0:
                        pe.wait_ge(aconst, 1)
                if b == 0:
                    pe.wait_ge(split_done, g * NSA + 2)

                def accumulate(t):
                    pe.wait_ge(pj_lo, s * 6 + (t + 1))
                    if t == 0 and not (first and b == 0):
                        pe.wait_ge(r_max, s * 2)
                    for pair in range(2):
                        last = mm3(bank[4][:, pair * VW:(pair + 1) * VW],
                                   lambda h: kt[:, t % 2, h, pair * P:(pair + 1) * P],
                                   lambda h: vt[:, t % 2, h, pair, :],
                                   t == 0 and pair == 0, t == NT - 1, skip_group_check=True)
                    last.then_inc(kvmm, 1)

                for t in range(NT):
                    if not (first and b == 0 and t < 2):
                        pe.wait_ge(pj_lo, s * 6 + (t - 1))
                    for c in range(NC):
                        last = mm3(bank[t % 2][:, :], hcol(c, b, t), lambda h, c=c: wkv[:, h, c, :],
                                   c == 0, c == NC - 1)
                    last.then_inc(pj_full, 1)
                    if t > 0:
                        accumulate(t - 1)
                if b == 0:
                    pe.wait_ge(split_done, g * NSA + 3)
                for pair in range(2):
                    pe.wait_ge(pj_lo, s * 6 + (3 + pair))
                    for c in range(NC):
                        last = mm3(bank[pair][:, :], lambda h, c=c: wq[:, h, c, pair * P:(pair + 1) * P],
                                   hrow(c, b), c == 0, c == NC - 1)
                    last.then_inc(pj_full, 1)
                    if pair == 0:
                        accumulate(NT - 1)
                tails("A", g, b)
                pe.wait_ge(pj_lo, s * 6 + 6)
                pe.wait_ge(kvb_lo, s + 1)
                for kind, banks in ((1, (5, 4)), (0, (6, 7))):
                    for pair in range(2):
                        mm3(bank[banks[pair]][:, :], lambda h: kvb[:, h, pair, kind, :],
                            lambda h: qt[:, h, pair, :], True, True).then_inc(nn_full, 1)
                extras("A", g, b)

            def tail_b(e, b, n0):
                s = e * NB + b
                pe.wait_ge(b_lo, s * 2 + 2)
                if b == 0:
                    pe.wait_ge(split_done, e * NSB + (BASE_B + 4))
                for t in range(NT):
                    o = ring_slot(n0 + t, par_of("B", e, b, t))
                    for i in range(2):
                        last = mm3(o[:, :], lambda h, i=i: ab[:, h, i, t * P:(t + 1) * P],
                                   lambda h, i=i: Wd[:, h, i, :], i == 0, i == 1)
                    last.then_inc(ring_full, 1)

            def step_b(e, b):
                s = e * NB + b
                first = isinstance(e, int) and e == 0
                if first:
                    need_h(1, b)
                for i in range(2):
                    if b == 0:
                        pe.wait_ge(split_done, e * NSB + (BASE_B + i + 1))
                    if first and b == 0:
                        pe.wait_ge(pj_lo, 6 * NB * GA)
                        pe.wait_ge(r_max, 2 * NB * GA)
                    else:
                        pe.wait_ge(b_p, s * 2 + (i - 1))
                    for u, o, full in ((0, bank[i], bg_full), (1, bank[4 + i], bu_full)):
                        for c in range(NC):
                            last = mm3(o[:, :], lambda h, c=c: gu[:, i, h, u, c, :], hrow(c, b),
                                       c == 0, c == NC - 1)
                        last.then_inc(full, 1)
                tails("B", e, b)
                extras("B", e, b)
                if first:
                    for n in range(4 * b, 4 * b + 4):
                        half, ic = n // 8, n % 8
                        pe.wait_ge(m_scaled, n + 1)
                        if n == 0:
                            pe.wait_ge(o_lo, 2 * NB * GA)
                        if n == 8:
                            pe.wait_ge(m_lo, 2)
                        for j in range(2):
                            m = 2 * half + j
                            last = pe.matmul(bank[6 + j][:, :], mstage[:, n % 4, m * P:(m + 1) * P],
                                             mstage[:, n % 4, 512:1024], start=ic == 0, stop=ic == 7)
                        last.then_inc(m_used, 1)
            def step_c(b):
                need_h(2, b)
                if b == 0:
                    pe.wait_ge(m_lo, 4)
                    pe.wait_ge(b_p, 2 * NB * GE)
                tails("C", 0, b)
                for t in range(NT):
                    n = NT * b + t
                    if n >= 6:
                        pe.wait_ge(y_read, n - 5)
                    for c in range(NC):
                        last = mm3(bank[YB[n % 6]][:, :], hcol(c, b, t), lambda h, c=c: M[:, h, c, :],
                                   c == 0, c == NC - 1)
                    last.then_inc(y_full, 1)
                extras("C", 0, b)

            def tail_d(g, b, n0):
                s = g * NB + b
                pe.wait_ge(d_lo, s * 4 + 4)
                if b == 0:
                    pe.wait_ge(split_done, g * NSD + (BASE_D + 6))
                for t in range(NT):
                    o = ring_slot(n0 + t, par_of("D", g, b, t))
                    for r in range(4):
                        last = mm3(o[:, :], lambda h, r=r: ad[:, r, h, t * P:(t + 1) * P],
                                   lambda h, r=r: wdd[:, h, r, :], r == 0, r == 3)
                    last.then_inc(ring_full, 1)

            def step_d(g, b):
                s = g * NB + b
                first = isinstance(g, int) and g == 0
                if first:
                    need_h(3, b)
                if first and b == 0:
                    pe.wait_ge(y_read, NT * NB)
                for r in range(4):
                    if b == 0:
                        pe.wait_ge(split_done, g * NSD + (BASE_D + r + 1))
                    if not (first and b == 0 and r < 2):
                        pe.wait_ge(d_h, s * 4 + (r - 1))
                    for u, o, full in ((0, bank[r % 2], dg_full), (1, bank[4 + r % 2], du_full)):
                        for c in range(NC):
                            last = mm3(o[:, :], lambda h, c=c: gud[r // 2][:, r % 2, h, u, c, :], hrow(c, b),
                                       c == 0, c == NC - 1)
                        last.then_inc(full, 1)
                tails("D", g, b)
                extras("D", g, b)

            def epi():
                tail_d(GD - 1, 3, RING[("tail", "D", GD - 1, 3)])

            walk(pe, pro, step_a, step_b, step_c, step_d, epi)

        @block.scalar
        def _(act):
            def load_row(stage_, g, b):
                kind = {"A": R_GA0, "B": R_GB0, "D": R_GB1}[stage_]
                if stage_ == "A" and isinstance(g, int) and g == 0:
                    if b == 0:
                        act.wait_ge(rows_stored, 16)
                    if b >= 2:
                        act.wait_ge(ring_read, RING[("tail", "A", 0, b - 2)] + NT)
                elif isinstance(g, int) and g == 0 and b < 2:
                    prev = {"B": ("A", GA - 1), "D": ("B", GE - 1)}[stage_]
                    act.wait_ge(ring_read, RING[("tail", *prev, b + 2)] + NT)
                elif b >= 2:
                    act.wait_ge(ring_read, ring_at(stage_, g, b - 2) + NT)
                elif isinstance(g, int):
                    act.wait_ge(ring_read, RING[("tail", stage_, g - 1, b + 2)] + NT)
                else:
                    act.wait_ge(ring_read, g * (NB * NT) + (RING[("tail", stage_, 0, b + 2)] - NB * NT + NT))
                act.dma_start(row[:, b % 2, :], rows_d[kind, b, :].partition_broadcast(P)) \
                    .then_inc(row_full[b % 2], 16)

            def wsplit(count, j, dst, size):
                act.wait_ge(stage_full[j % 2], count)
                act.activation(dst, stage[:, j % 2, 0:size], ACT.Copy).then_inc(split_hi, 1)

            def split_a(g, j):
                dst = (W1a[:, 0:1024], W1a[:, 1024:2048], W1b[:, 0:1024], W1b[:, 2048:3072])[j]
                wsplit(g * 32 + 16 * (j // 2 + 1), j, dst, 1024)

            def split_b(e, j):
                dst = (W2[:, 0:1024], W2[:, 2048:3072], Wd[:, HI, 0, :], Wd[:, HI, 1, :])[j]
                wsplit(e * 32 + (8 * BASE_B + 16 * (j // 2 + 1)), j, dst, (1024, 1024, 512, 512)[j])

            def split_d(g, j):
                w = (W1a, W1a, W1b, W1b)[j] if j < 4 else None
                dst = w[:, (j % 2) * 2048:(j % 2) * 2048 + 1024] if j < 4 else \
                    W2[:, (j - 4) * 1024:(j - 3) * 1024]
                wsplit(g * 48 + (8 * BASE_D + 16 * (j // 2 + 1)), j, dst, 1024)

            def ln_out(k, b):
                n0 = RING[("ln", k, b)]
                if k < 2:
                    act.wait_ge(col_done, (2, 8)[k])
                if n0 > 0:
                    act.wait_ge(ring_read, n0)
                for c in range(NC):
                    n = n0 + c
                    act.wait_ge(ring_full, n + 1)
                    if n >= 2:
                        act.wait_ge(ring_done, n - 1)
                    act.activation(tmp[:, n % 2, :], TAIL[n % 2][:, :], ACT.Identity,
                                   scale=modc[:, k, 1, c, b:b + 1], bias=modc[:, k, 0, c, b:b + 1]) \
                        .then_inc(ring_read, 1)
                    act.wait_ge(ring_read, n + 1)
                    act.activation(hT[:, HI, c, b * S:(b + 1) * S], tmp[:, n % 2, :], ACT.Copy) \
                        .then_inc(h_hi, 1)

            def router(b):
                act.wait_ge(rt_sub, b + 1)
                act.activation(pe8[:, :, :], lg[:, :, :], ACT.Exp).then_inc(rt_exp, 1)

            def extras(stage_, g, b):
                ln = layernorms(stage_, g, b)
                if ln:
                    ln_out(*ln)
                rt = routed(stage_, g, b)
                if rt is not None:
                    router(rt)

            def pro():
                for b in range(NB):
                    act.dma_start(x[:, b * NT:(b + 1) * NT, :], x_in[b].rearrange("(t p) n -> p t n", p=P)) \
                        .then_inc(x_in_s[b], 16)
                act.wait_ge(small_loaded, 32)
                act.activation(scT[:, :, :, :], cTs[:, :, :, :], ACT.Silu).then_inc(silu_c, 1)
                for j in range(2):
                    split_a(0, j)
                ln_out(0, 0)
                split_a(0, 2)
                split_a(0, 3)
                ln_out(0, 1)

            def crows(which, b):
                if b > 0 and which < 2:
                    act.wait_ge(pq_sum, NT * b)
                elif b > 0:
                    act.wait_ge(y_read, NT * b)
                act.dma_start(crow[:, which, :], rows_d[R_P1 + which, b, :].partition_broadcast(P)) \
                    .then_inc(crow_full[which], 16)

            def ln_c_rows(stage_, g, b):
                ln = layernorms(stage_, g, b)
                if ln and ln[0] == 2:
                    crows(0, ln[1])
                    crows(1, ln[1])

            def out_hi(s, pair):
                act.wait_ge(o_num, s * 2 + (pair - 1))
                act.activation(ot[:, HI, pair, :], bank[6 + pair][:, :], ACT.Copy).then_inc(o_hi, 1)

            def step_a(g, b):
                s = g * NB + b
                first = isinstance(g, int) and g == 0
                last = isinstance(g, int) and g == GA - 1
                load_row("A", g, b)
                for t in range(NT):
                    act.wait_ge(pj_full, s * 6 + (t + 1))
                    if not (first and b == 0 and t < 2):
                        act.wait_ge(kvmm, s * 4 + (t - 1))
                    act.activation(kt[:, t % 2, HI, :], bank[t % 2][:, 0:256], ACT.Relu)
                    act.activation(vt[:, t % 2, HI, :, 0:P],
                                   bank[t % 2][:, 256:512].rearrange("p (a n) -> p a n", a=2), ACT.Copy) \
                        .then_inc(pj_hi, 1)
                if b == 3 and not last:
                    split_a(g + 1, 0)
                    split_a(g + 1, 1)
                for pair in range(2):
                    if tail_of("A", g, b):
                        out_hi(s, pair)
                    act.wait_ge(pj_full, s * 6 + (5 + pair))
                    if pair == 0 and not (first and b == 0):
                        act.wait_ge(nn_full, s * 4)
                    act.activation(qt[:, HI, pair, :], bank[pair][:, :], ACT.Relu).then_inc(pj_hi, 1)
                act.wait_ge(kvmm, s * 4 + 4)
                if first and b == 0:
                    act.wait_ge(aconst, 1)
                kv = bank[4][:, 0:2 * VW].rearrange("p (a n) -> p a n", a=2)
                for lo in (0, HD):
                    q = slice(lo, lo + HD)
                    act.activation(kvb[q, HI, :, 0, q], kv[q, :, q], ACT.Copy)
                    ins = act.activation(kvb[q, HI, :, 1, q], kv[q, :, P:P + 1].to_broadcast([HD, 2, HD]), ACT.Copy)
                ins.then_inc(kvb_hi, 1)
                if b == 3:
                    if last:
                        split_b(0, 0)
                        split_b(0, 1)
                    else:
                        split_a(g + 1, 2)
                if b == 0 and not first:
                    act.wait_ge(ring_full, ring_before("A", g, b) + NT)
                    split_a(g, 3)
                extras("A", g, b)

            def step_b(e, b):
                s = e * NB + b
                first = isinstance(e, int) and e == 0
                load_row("B", e, b)
                if first and b == 0:
                    for pair in range(2):
                        out_hi(NB * GA, pair)
                    act.wait_ge(kvmm, NT * NB * GA)
                for i in range(2):
                    act.wait_ge(bg_full, s * 2 + (i + 1))
                    if not (first and b == 0):
                        act.wait_ge(b_p, s * 2 + (i - 1))
                    act.activation(sg[:, i, :], bank[i][:, :], ACT.Silu).then_inc(b_silu, 1)
                    if b == 3 and not (isinstance(e, int) and e == GE - 1):
                        act.wait_ge(bu_full, s * 2 + (i + 1))
                        split_b(e + 1, i)
                if tail_of("B", e, b):
                    act.wait_ge(ring_full, ring_before("B", e, b) + NT)
                for i in range(2):
                    act.wait_ge(b_p, s * 2 + (i + 1))
                    act.activation(ab[:, HI, i, :], pr[:, i, :], ACT.Copy).then_inc(b_hi, 1)
                if b == 0:
                    split_b(e, 2)
                    split_b(e, 3)
                ln_c_rows("B", e, b)
                extras("B", e, b)
                if first and b in (1, 3):
                    for j in range(2):
                        m = (b - 1) + j
                        act.wait_ge(m_used, 8 * (m // 2 + 1))
                        act.activation(M[:, HI, m, :], bank[6 + j][:, :], ACT.Copy).then_inc(m_hi, 1)

            def step_c(b):
                ln_c_rows("C", 0, b)
                crows(2, b)
                for t in range(NT):
                    n = NT * b + t
                    act.wait_ge(y_full, n + 1)
                    if t == 0 and b > 0:
                        act.wait_ge(y_read, NT * b)
                    if n > 0:
                        act.wait_ge(y_sq, n)
                    act.activation(sqj[:, :], bank[YB[n % 6]][:, :], ACT.Square,
                                   accum_out=ssum[:, t:t + 1]).then_inc(y_sq, 1)
                if b < 2:
                    if b == 0:
                        act.wait_ge(m_lo, 4)
                    split_d(0, b)
                extras("C", 0, b)

            def step_d(g, b):
                s = g * NB + b
                first = isinstance(g, int) and g == 0
                load_row("D", g, b)
                if first and b == 0:
                    act.wait_ge(y_full, NT * NB)
                    split_d(0, 2)
                    split_d(0, 3)
                for r in range(4):
                    act.wait_ge(dg_full, s * 4 + (r + 1))
                    if first and b == 0 and r == 0:
                        act.wait_ge(ring_done, RING[("tail", "B", GE - 1, 3)] + NT)
                    if not (first and b == 0):
                        act.wait_ge(d_lo, s * 4 + (r - 3))
                    act.activation(hh[:, r, :], bank[r % 2][:, :], ACT.Silu).then_inc(d_silu, 1)
                    if b == 3 and not (isinstance(g, int) and g == GD - 1):
                        act.wait_ge(du_full, s * 4 + (r + 1))
                        split_d(g + 1, r)
                ln = layernorms("D", g, b)
                if ln:
                    ln_out(*ln)
                for r in range(4):
                    if r == 0:
                        act.wait_ge(d_h, s * 4 + 4)
                        if ln:
                            act.wait_ge(ring_full, RING[("ln", *ln)] + NC)
                        if not (first and b == 0):
                            act.wait_ge(d_sp, s * NSP)
                    act.activation(ab4[:, r, :], hh[:, r, :], ACT.Abs).then_inc(d_abs, 1)
                if tail_of("D", g, b):
                    act.wait_ge(ring_full, ring_before("D", g, b) + NT)
                if first and b == 0:
                    act.wait_ge(c_add, NT * NB)
                for r in range(4):
                    act.wait_ge(d_sp, s * NSP + (NSP - 3 + r))
                    act.activation(ad[:, r, HI, :], hh[:, r, :], ACT.Copy).then_inc(d_hi, 1)
                if b == 0:
                    split_d(g, 4)
                    split_d(g, 5)
            walk(act, pro, step_a, step_b, step_c, step_d, lambda: None)

        @block.vector
        def _(dve):
            def link(ins, sem_, count):
                ins.then_inc(sem_, 1)
                dve.wait_ge(sem_, count)

            chain = {"ln": 0, "p": 0, "rt": 0}

            def seq(ins, which):
                chain[which] += 1
                link(ins, {"ln": ln_chain, "p": pchain, "rt": rt_chain}[which], chain[which])

            def take(n, par, after_act=False):
                if after_act:
                    dve.wait_ge(ring_read, n)
                dve.wait_ge(ring_full, n + 1)
                if not (isinstance(n, int) and n < 2):
                    dve.wait_ge(ring_done, n - 1)

            def inv_sqrt():
                seq(dve.tensor_scalar(rstd[:, :].bitcast(I32), ve[:, :].bitcast(I32), -0.5, MAGIC,
                                      ALU.mult, ALU.add), "ln")
                for _ in range(3):
                    seq(dve.tensor_tensor(na[:, :], ve[:, :], rstd[:, :], ALU.mult), "ln")
                    seq(dve.scalar_tensor_tensor(out=na[:, :], in0=na[:, :], scalar=-0.5, in1=rstd[:, :],
                                                 op0=ALU.mult, op1=ALU.mult), "ln")
                    seq(dve.scalar_tensor_tensor(out=rstd[:, :], in0=na[:, :], scalar=1.5, in1=rstd[:, :],
                                                 op0=ALU.add, op1=ALU.mult), "ln")

            def ln_stats(k, b, t):
                if t == 0:
                    if k == 0:
                        dve.wait_ge(x_in_s[b], 16)
                    elif k == 3:
                        dve.wait_ge(c_add, NT * (b + 1))
                    else:
                        prev = {1: ("A", GA - 1), 2: ("B", GE - 1)}[k]
                        dve.wait_ge(ring_done, RING[("tail", *prev, b)] + NT)
                seq(dve.bn_stats(st6[:, t, :], x[:, b * NT + t, :]), "ln")
                seq(dve.bn_aggr(mv[:, t, :], st6[:, t, :]), "ln")

            def ln_apply(k, b):
                seq(dve.tensor_scalar(ve[:, :], mv[:, :, 1], EPS, None, ALU.add), "ln")
                inv_sqrt()
                n = ln_index(k, b)
                if n > 0:
                    dve.wait_ge(ring_full, RING[("ln", (n - 1) // NB, (n - 1) % NB)] + NC)
                if k == 2 and b > 0:
                    dve.wait_ge(pq_add, NT * b)
                if k == 3 and b == 0:
                    dve.wait_ge(pq_add, NT * NB)
                for t in range(NT):
                    last = dve.tensor_scalar(xn[:, t, :], x[:, b * NT + t, :], mv[:, t, 0:1], rstd[:, t:t + 1],
                                             ALU.subtract, ALU.mult)
                last.then_inc(xn_ready, 1)

            def ln_gated(k, b):
                if k == 2:
                    dve.wait_ge(ring_full, RING[("ln", k, b)] + NC)
                    dve.wait_ge(crow_full[0], 16 * (b + 1))
                    dve.wait_ge(crow_full[1], 16 * (b + 1))
                    for t in range(NT):
                        dve.tensor_tensor(xn[:, t, :], xn[:, t, :], crow[:, 0, :], ALU.mult).then_inc(pq_mul, 1)
                    for t in range(NT):
                        dve.wait_ge(pq_mul, NT * b + t + 1)
                        dve.tensor_tensor(xn[:, t, :], xn[:, t, :], crow[:, 1, :], ALU.add).then_inc(pq_sum, 1)

            def router(b):
                n = RING[("rt", b)]
                take(n, n % 2, True)
                dve.tensor_copy(tmp[:, n % 2, 0:NT * 8], TAIL[n % 2][:, 0:NT * 8]).then_inc(ring_read, 1)
                dve.wait_ge(ring_done, n + 1)
                seq(dve.tensor_reduce(m4[:, 0, :], lg[:, :, :], AX_X, ALU.max), "rt")
                dve.tensor_tensor(lg[:, :, :], lg[:, :, :], m4[:, 0, :].unsqueeze(2).to_broadcast([P, NT, 8]),
                                  ALU.subtract).then_inc(rt_sub, 1)
                dve.wait_ge(rt_exp, b + 1)
                seq(dve.tensor_reduce(m4[:, 0, :], pe8[:, :, :], AX_X, ALU.add), "rt")
                seq(dve.reciprocal(m4[:, 1, :], m4[:, 0, :]), "rt")
                seq(dve.tensor_tensor(pe8[:, :, :], pe8[:, :, :], m4[:, 1, :].unsqueeze(2).to_broadcast([P, NT, 8]),
                                      ALU.mult), "rt")
                for t in range(NT):
                    seq(dve.max(v8[:, t, :], pe8[:, t, :]), "rt")
                    seq(dve.max_index(i8[:, t, :], v8[:, t, :], pe8[:, t, :]), "rt")
                    for j in range(2):
                        seq(dve.tensor_scalar(sel[:, j, t, :], iota8[:, :], i8[:, t, j:j + 1], None,
                                              ALU.is_equal), "rt")
                seq(dve.tensor_tensor(m4[:, 0, :], v8[:, :, 0], v8[:, :, 1], ALU.add), "rt")
                seq(dve.reciprocal(m4[:, 1, :], m4[:, 0, :]), "rt")
                seq(dve.tensor_tensor(sel[:, 0, :, :], sel[:, 0, :, :], sel[:, 1, :, :], ALU.add), "rt")
                seq(dve.tensor_tensor(pe8[:, :, :], pe8[:, :, :], m4[:, 1, :].unsqueeze(2).to_broadcast([P, NT, 8]),
                                      ALU.mult), "rt")
                seq(dve.tensor_tensor(rw[:, b * NT:(b + 1) * NT, :], pe8[:, :, :], sel[:, 0, :, :], ALU.mult), "rt")

            def late(stage_, g, b):
                ln = layernorms(stage_, g, b)
                if ln:
                    ln_gated(*ln)
                rt = routed(stage_, g, b)
                if rt is not None:
                    router(rt)

            def pro():
                for e in range(8):
                    dve.memset(iota8[:, e:e + 1], float(e))
                dve.wait_ge(small_loaded, 32)
                for j, other in ((1, 3), (2, 4)):
                    seq(dve.scalar_tensor_tensor(out=cin[:, j, :, :], in0=cin[:, 0, :, :], scalar=0.0,
                                                 in1=cin[:, j, :, :], op0=ALU.mult, op1=ALU.add), "p")
                    seq(dve.tensor_tensor(cin[:, j, :, :], cin[:, j, :, :], cin[:, other, :, :], ALU.mult), "p")
                seq(dve.tensor_tensor(cin[:, 1, :, :], cin[:, 1, :, :], cin[:, 2, :, :], ALU.subtract), "p")
                seq(dve.tensor_reduce(kcoef[:, :], cin[:, 1, :, :], AX_X, ALU.add), "p")
                for t in range(NT):
                    ln_stats(0, 0, t)
                ln_apply(0, 0)

                def columns(n, k, sc):
                    dve.wait_ge(col_full, n)
                    src = bank[0 if k == 0 else 1][:, (k * 2 + sc) * 16:(k * 2 + sc + 1) * 16] \
                        .rearrange("p (c b) -> p c b", c=NC)
                    dve.tensor_scalar(modc[:, k, sc, :, :], src, float(sc), None, ALU.add).then_inc(col_done, 1)

                columns(2, 0, 0)
                columns(2, 0, 1)
                def fetch(i, dst):
                    dve.wait_ge(rowp_full, i + 1)
                    ins = dve.tensor_copy(dst, bank[6 + i % 2][0:NB, :])
                    link(ins, rowp_done, i + 1)

                def gate(v, dst, done=None):
                    seq(dve.tensor_scalar(ptmp[:, 1, :], v, 0.0, 2.0, ALU.is_ge, ALU.mult), "p")
                    seq(dve.scalar_tensor_tensor(out=v, in0=v, scalar=-1.0, in1=v, op0=ALU.mult, op1=ALU.max), "p")
                    seq(dve.tensor_scalar(v, v, 0.25, None, ALU.max), "p")
                    ins = dve.scalar_tensor_tensor(out=dst, in0=ptmp[:, 1, :], scalar=-1.0, in1=v,
                                                   op0=ALU.add, op1=ALU.mult)
                    if done:
                        ins.then_inc(done, 1)
                    else:
                        seq(ins, "p")

                fetch(0, ptmp[:, 0, :])
                gate(ptmp[:, 0, :], prow[:, R_GA0, :])
                fetch(1, ptmp[:, 0, :])
                gate(ptmp[:, 0, :], prow[:, R_GB0, :])
                fetch(2, prow[:, R_Q1, :])
                fetch(3, prow[:, R_P1, :])
                fetch(4, ptmp[:, 0, :])
                gate(ptmp[:, 0, :], prow[:, R_GB1, :])
                g1 = prow[:, R_GB1, :]
                seq(dve.scalar_tensor_tensor(out=prow[:, R_P1, :], in0=prow[:, R_P1, :], scalar=1.0, in1=g1,
                                             op0=ALU.add, op1=ALU.mult), "p")
                seq(dve.tensor_tensor(prow[:, R_Q1, :], prow[:, R_Q1, :], g1, ALU.mult), "p")
                dve.wait_ge(nw_loaded, 16)
                seq(dve.tensor_tensor(prow[:, R_R1, :], prow[:, R_R1, :], g1, ALU.mult), "p")
                fetch(5, ptmp[:, 0, :])
                gate(ptmp[:, 0, :], prow[:, R_GB1, :], rows_ready)
                for n, (k, sc) in enumerate(((1, 0), (1, 1), (2, 0), (2, 1), (3, 0), (3, 1))):
                    columns(8, k, sc)
                dve.wait_ge(col_full, 8)
                dve.memset(kvb[:, :, :, :, :].bitcast(F32), 0.0)
                dve.memset(vt[:, :, HI, :, P:VW].bitcast(F32), 1.0)
                dve.memset(vt[:, :, LO, :, P:VW].bitcast(F32), 0.0).then_inc(aconst, 1)
                for t in range(NT):
                    ln_stats(0, 1, t)
                ln_apply(0, 1)

            def early(stage_, g, b, t):
                ln = layernorms(stage_, g, b)
                if ln:
                    ln_stats(*ln, t)
                    if t == NT - 1:
                        ln_apply(*ln)

            def tail_evac(stage_, g, b, t):
                tail = tail_of(stage_, g, b) if stage_ != "end" else ("D", GD - 1, 3)
                if tail is None:
                    return
                n0 = ring_before(stage_, g, b) if stage_ != "end" else RING[("tail", "D", GD - 1, 3)]
                ts, tg, tb = tail
                key = RING[("tail", ts, tg if isinstance(tg, int) else 1, tb)]
                par = (key + t) % 2
                if t == 0:
                    rn0 = {"A": 0, "B": NB * GA, "D": NB * (GA + GE)}[ts]
                    dve.wait_ge(row_full[tb % 2], tg * 32 + (8 * rn0 + 16 * (tb // 2 + 1)))
                take(n0 + t, par, t == 0)
                if ts == "B":
                    dve.scalar_tensor_tensor(out=tmp[:, par, :], in0=TAIL[par][:, :],
                                             scalar=rwe[:, tb * NT + t:tb * NT + t + 1], in1=row[:, tb % 2, :],
                                             op0=ALU.mult, op1=ALU.mult).then_inc(ring_read, 1)
                elif ts == "A" and isinstance(tg, int) and tg == GA - 1:
                    if t == 0 and tb == 0:
                        dve.wait_ge(bo_loaded, 16)
                    link(dve.tensor_tensor(tmp[:, par, :], TAIL[par][:, :], bor[:, :], ALU.add),
                         bo_add, tb * NT + t + 1)
                    dve.tensor_tensor(tmp[:, par, :], tmp[:, par, :], row[:, tb % 2, :], ALU.mult) \
                        .then_inc(ring_read, 1)
                else:
                    dve.tensor_tensor(tmp[:, par, :], TAIL[par][:, :], row[:, tb % 2, :], ALU.mult) \
                        .then_inc(ring_read, 1)

            def invert(s, pair):
                dve.wait_ge(r_max, s * 2 + (pair - 1))
                dve.reciprocal(rr[:, pair, :], rr[:, pair, :]).then_inc(r_rec, 1)

            def normalise(s, pair):
                dve.wait_ge(nn_full, s * 4 + (pair - 1))
                dve.wait_ge(r_rec, s * 2 + (pair - 1))
                dve.tensor_tensor(bank[6 + pair][:, :], bank[6 + pair][:, :], rr[:, pair, :], ALU.mult) \
                    .then_inc(o_num, 1)

            def out_lo(s, pair):
                dve.wait_ge(o_hi, s * 2 + (pair - 1))
                dve.tensor_tensor(ot[:, LO, pair, :], bank[6 + pair][:, :],
                                  ot[:, HI, pair, :].bitcast(F32), ALU.subtract).then_inc(o_lo, 1)

            def step_a(g, b):
                s = g * NB + b
                for t in range(NT):
                    dve.wait_ge(pj_hi, s * 6 + (t + 1))
                    dve.scalar_tensor_tensor(out=kt[:, t % 2, LO, :], in0=bank[t % 2][:, 0:256], scalar=0.0,
                                             in1=kt[:, t % 2, HI, :].bitcast(F32), op0=ALU.max, op1=ALU.subtract)
                    dve.tensor_tensor(vt[:, t % 2, LO, :, 0:P],
                                      bank[t % 2][:, 256:512].rearrange("p (a n) -> p a n", a=2),
                                      vt[:, t % 2, HI, :, 0:P].bitcast(F32), ALU.subtract).then_inc(pj_lo, 1)
                    if tail_of("A", g, b):
                        (invert if t < 2 else normalise)(s, t % 2)
                    early("A", g, b, t)
                for pair in range(2):
                    dve.wait_ge(pj_hi, s * 6 + (5 + pair))
                    dve.scalar_tensor_tensor(out=qt[:, LO, pair, :], in0=bank[pair][:, :], scalar=0.0,
                                             in1=qt[:, HI, pair, :].bitcast(F32), op0=ALU.max,
                                             op1=ALU.subtract).then_inc(pj_lo, 1)
                    if tail_of("A", g, b):
                        out_lo(s, pair)
                dve.wait_ge(kvb_hi, s + 1)
                kv = bank[4][:, 0:2 * VW].rearrange("p (a n) -> p a n", a=2)
                for lo in (0, HD):
                    q = slice(lo, lo + HD)
                    dve.tensor_tensor(kvb[q, LO, :, 0, q], kv[q, :, q], kvb[q, HI, :, 0, q].bitcast(F32),
                                      ALU.subtract)
                    last = dve.tensor_tensor(kvb[q, LO, :, 1, q], kv[q, :, P:P + 1].to_broadcast([HD, 2, HD]),
                                             kvb[q, HI, :, 1, q].bitcast(F32), ALU.subtract)
                last.then_inc(kvb_lo, 1)
                for t in range(NT):
                    tail_evac("A", g, b, t)
                for pair in range(2):
                    dve.wait_ge(nn_full, s * 4 + (pair + 1))
                    if tail_of("A", g, b):
                        dve.wait_ge(o_num, s * 2)
                    dve.tensor_scalar(rr[:, pair, :], bank[(5, 4)[pair]][:, :], 1e-6, None, ALU.max) \
                        .then_inc(r_max, 1)
                if isinstance(g, int) and g == GA - 1 and b == 3:
                    split_b(0, 0)
                    split_b(0, 1)
                late("A", g, b)

            def split_b(e, i):
                n = e * NSB + (BASE_B + i)
                dve.wait_ge(split_hi, n + 1)
                dve.wait_ge(split_done, n)
                dve.tensor_tensor(W2[:, i * 2048 + 1024:(i + 1) * 2048], stage[:, i, :],
                                  W2[:, i * 2048:i * 2048 + 1024].bitcast(F32), ALU.subtract) \
                    .then_inc(split_done, 1)

            def step_b(e, b):
                s = e * NB + b
                if isinstance(e, int) and e == 0 and b == 0:
                    for part in (invert, normalise, out_lo):
                        for pair in range(2):
                            part(NB * GA, pair)
                for i in range(2):
                    dve.wait_ge(bu_full, s * 2 + (i + 1))
                    dve.wait_ge(b_silu, s * 2 + (i + 1))
                    if not (isinstance(e, int) and e == 0 and b == 0):
                        dve.wait_ge(b_lo, s * 2 + (i - 1))
                    dve.tensor_tensor(pr[:, i, :], sg[:, i, :], bank[4 + i][:, :], ALU.mult).then_inc(b_p, 1)
                    if b == 3 and not (isinstance(e, int) and e == GE - 1):
                        split_b(e + 1, i)
                    early("B", e, b, 2 * i)
                    early("B", e, b, 2 * i + 1)
                for t in range(NT):
                    tail_evac("B", e, b, t)
                if isinstance(e, int) and e == 0:
                    for n in range(4 * b, 4 * b + 4):
                        dve.wait_ge(m_loaded[n % 4], 16 * (n // 4 + 1))
                        dve.tensor_scalar(mstage[:, n % 4, 512:1024], mstage[:, n % 4, 512:1024],
                                          kcoef[:, n % 8:n % 8 + 1], None, ALU.mult).then_inc(m_scaled, 1)
                if b == 0:
                    if not (isinstance(e, int) and e == 0):
                        dve.wait_ge(ring_read, ring_before("B", e, b) + NT)
                        link(dve.tensor_copy(rwe[:, :], rw[:, :, bass.ds(e, 1)].rearrange("p t a -> p (t a)")),
                             rwe_done, e)
                for i in range(2):
                    dve.wait_ge(b_hi, s * 2 + (i + 1))
                    dve.tensor_tensor(ab[:, LO, i, :], pr[:, i, :], ab[:, HI, i, :].bitcast(F32),
                                      ALU.subtract).then_inc(b_lo, 1)
                late("B", e, b)
                if isinstance(e, int) and e == 0:
                    seq(dve.tensor_copy(rwe[:, b * NT:(b + 1) * NT], rw[:, b * NT:(b + 1) * NT, 0]), "rt")
                    if b in (1, 3):
                        for j in range(2):
                            m = (b - 1) + j
                            dve.wait_ge(m_hi, m + 1)
                            dve.tensor_tensor(M[:, LO, m, :], bank[6 + j][:, :], M[:, HI, m, :].bitcast(F32),
                                              ALU.subtract).then_inc(m_lo, 1)

            def step_c(b):
                for t in range(NT):
                    tail_evac("C", 0, b, t)
                ln = layernorms("C", 0, b)
                for t in range(NT):
                    ln_stats(*ln, t)
                ln_apply(*ln)
                dve.wait_ge(y_sq, NT * (b + 1))
                seq(dve.tensor_scalar(ve[:, :], ssum[:, :], 1.0 / H, EPS_RMS, ALU.mult, ALU.add), "ln")
                inv_sqrt()
                dve.wait_ge(crow_full[2], 16 * (b + 1))
                for t in range(NT):
                    n = NT * b + t
                    if n >= 2:
                        dve.wait_ge(c_add, n - 1)
                    dve.scalar_tensor_tensor(out=ct[:, n % 2, :], in0=bank[YB[n % 6]][:, :],
                                             scalar=rstd[:, t:t + 1], in1=crow[:, 2, :], op0=ALU.mult,
                                             op1=ALU.mult).then_inc(y_read, 1)
                ln_gated(*ln)

            def step_d(g, b):
                s = g * NB + b
                for r in range(4):
                    dve.wait_ge(du_full, s * 4 + (r + 1))
                    dve.wait_ge(d_silu, s * 4 + (r + 1))
                    dve.tensor_tensor(hh[:, r, :], hh[:, r, :], bank[4 + r % 2][:, :], ALU.mult).then_inc(d_h, 1)
                    early("D", g, b, r)
                done = [0]

                def op(ins):
                    done[0] += 1
                    ins.then_inc(d_sp, 1)

                def after(k):
                    dve.wait_ge(d_sp, s * NSP + k)

                c01, c23, fa, fb, fs, ft = (fl[:, i, :] for i in range(6))
                a = [ab4[:, r, :] for r in range(4)]
                tt = dve.tensor_tensor
                if layernorms("D", g, b):
                    for t in range(NT):
                        tail_evac("D", g, b, t)
                    late("D", g, b)
                dve.wait_ge(d_abs, s * 4 + 4)
                op(tt(c01, a[0], a[1], ALU.is_ge))
                op(tt(mx[:, :], a[0], a[1], ALU.max))
                op(tt(a[0], a[0], a[1], ALU.min))
                op(tt(c23, a[2], a[3], ALU.is_ge))
                if not layernorms("D", g, b):
                    tail_evac("D", g, b, 0)
                after(4)
                op(tt(a[1], a[2], a[3], ALU.max))
                op(tt(a[2], a[2], a[3], ALU.min))
                after(5)
                op(tt(fb, a[0], a[1], ALU.is_ge))
                after(6)
                op(tt(fa, mx[:, :], a[2], ALU.is_ge))
                if not layernorms("D", g, b):
                    tail_evac("D", g, b, 1)
                after(8)
                op(tt(fs, fa, fb, ALU.add))
                after(9)
                op(tt(ft, fs, c01, ALU.add))
                op(tt(fa, fs, c01, ALU.subtract))
                op(tt(fb, fs, c23, ALU.subtract))
                op(tt(fs, fs, c23, ALU.add))
                if not layernorms("D", g, b):
                    tail_evac("D", g, b, 2)
                for r, (flag, bound, cmp) in enumerate(((ft, 2.0, ALU.is_ge), (fa, 1.0, ALU.is_ge),
                                                        (fb, 0.0, ALU.is_le), (fs, 1.0, ALU.is_le))):
                    after(10 + r)
                    op(dve.scalar_tensor_tensor(out=hh[:, r, :], in0=flag, scalar=bound, in1=hh[:, r, :],
                                                op0=cmp, op1=ALU.mult))
                if not layernorms("D", g, b):
                    tail_evac("D", g, b, 3)
                assert done[0] == NSP

            def epi():
                for t in range(NT):
                    tail_evac("end", GD - 1, 3, t)

            walk(dve, pro, step_a, step_b, step_c, step_d, epi)

        @block.gpsimd
        def _(pool):
            def lo_part(dst, src, hi):
                return pool.tensor_tensor(dst, src, hi.bitcast(F32), ALU.subtract)

            def wsplit(n, j, lo, hi, size):
                pool.wait_ge(split_hi, n + 1)
                if not (isinstance(n, int) and n == 0):
                    pool.wait_ge(split_done, n)
                lo_part(lo, stage[:, j % 2, 0:size], hi).then_inc(split_done, 1)

            def split_a(g, j):
                w, at = ((W1a, 0), (W1a, 1024), (W1b, 0), (W1b, 2048))[j]
                off = (2048, 2048, 1024, 1024)[j]
                wsplit(g * NSA + j, j, w[:, at + off:at + off + 1024], w[:, at:at + 1024], 1024)

            def split_b(e, j):
                n = e * NSB + (BASE_B + j)
                wsplit(n, j, Wd[:, LO, j - 2, :], Wd[:, HI, j - 2, :], 512)

            def split_d(g, j):
                n = g * NSD + (BASE_D + j)
                if j < 4:
                    w, at = (W1a, W1a, W1b, W1b)[j], (j % 2) * 2048
                    wsplit(n, j, w[:, at + 1024:at + 2048], w[:, at:at + 1024], 1024)
                else:
                    at = (j - 4) * 1024
                    wsplit(n, j, W2[:, 2048 + at:2048 + at + 1024], W2[:, at:at + 1024], 1024)

            def ln_out(k, b):
                n0 = RING[("ln", k, b)]
                for c in range(NC):
                    pool.wait_ge(h_hi, ln_index(k, b) * NC + c + 1)
                    hs = slice(b * S, (b + 1) * S)
                    lo_part(hT[:, LO, c, hs], tmp[:, (n0 + c) % 2, :], hT[:, HI, c, hs]).then_inc(ring_done, 1)
                if k == 2:
                    for t in range(NT):
                        pool.wait_ge(pq_sum, NT * b + t + 1)
                        xt = x[:, b * NT + t, :]
                        pool.tensor_tensor(xt, xt, xn[:, t, :], ALU.add).then_inc(pq_add, 1)

            def extras(stage_, g, b):
                ln = layernorms(stage_, g, b)
                if ln:
                    ln_out(*ln)
                rt = routed(stage_, g, b)
                if rt is not None:
                    n = RING[("rt", rt)]
                    pool.wait_ge(ring_read, n + 1)
                    pool.tensor_copy(lg[:, :, :], tmp[:, n % 2, 0:NT * 8].rearrange("p (t e) -> p t e", t=NT)) \
                        .then_inc(ring_done, 1)

            def add_tail(tail, n0):
                ts, tg, tb = tail
                key = RING[("tail", ts, tg if isinstance(tg, int) else 1, tb)]
                for t in range(NT):
                    pool.wait_ge(ring_read, n0 + t + 1)
                    xt = x[:, tb * NT + t, :]
                    pool.tensor_tensor(xt, xt, tmp[:, (key + t) % 2, :], ALU.add).then_inc(ring_done, 1)

            def tails(stage_, g, b):
                tail = tail_of(stage_, g, b)
                if tail:
                    add_tail(tail, ring_before(stage_, g, b))

            def pro():
                pool.memset(ident[:, :], 0.0).then_inc(zeroed, 1)
                pool.wait_ge(zeroed, 1)
                pool.affine_select(out=ident[:, :], in_=ident[:, :], compare_op=ALU.not_equal, fill=1.0, base=0,
                                   pattern=[[-1, P]], channel_multiplier=1).then_inc(const_ready, 1)
                pool.dma_start(prow[:, R_R1, :], norm_w.partition_broadcast(NB)).then_inc(nw_loaded, 16)
                pool.dma_start(gwr[:, :, :], gwT).then_inc(gw_loaded, 16)
                pool.wait_ge(gw_loaded, 16)
                pool.tensor_copy(gw[:, HI, :, :], gwr[:, :, :]).then_inc(gw_hi_s, 1)
                pool.wait_ge(gw_hi_s, 1)
                lo_part(gw[:, LO, :, :], gwr[:, :, :], gw[:, HI, :, :]).then_inc(gw_ready, 1)
                split_a(0, 0)
                split_a(0, 1)
                ln_out(0, 0)
                split_a(0, 2)
                split_a(0, 3)
                ln_out(0, 1)

            def step_a(g, b):
                if b == 3 and not (isinstance(g, int) and g == GA - 1):
                    for j in range(3):
                        split_a(g + 1, j)
                tails("A", g, b)
                if b == 0 and not (isinstance(g, int) and g == 0):
                    split_a(g, 3)
                extras("A", g, b)

            def step_b(e, b):
                tails("B", e, b)
                if b == 0:
                    split_b(e, 2)
                    split_b(e, 3)
                extras("B", e, b)

            def step_c(b):
                tails("C", 0, b)
                if b < 2:
                    split_d(0, b)
                for t in range(NT):
                    n = NT * b + t
                    pool.wait_ge(y_read, n + 1)
                    xt = x[:, NT * b + t, :]
                    pool.tensor_tensor(xt, xt, ct[:, n % 2, :], ALU.add).then_inc(c_add, 1)
                extras("C", 0, b)

            def step_d(g, b):
                s = g * NB + b
                if isinstance(g, int) and g == 0 and b == 0:
                    split_d(0, 2)
                    split_d(0, 3)
                if b == 3 and not (isinstance(g, int) and g == GD - 1):
                    for j in range(4):
                        split_d(g + 1, j)
                ln = layernorms("D", g, b)
                tails("D", g, b)
                if ln:
                    ln_out(*ln)
                for r in range(4):
                    pool.wait_ge(d_hi, s * 4 + (r + 1))
                    lo_part(ad[:, r, LO, :], hh[:, r, :], ad[:, r, HI, :]).then_inc(d_lo, 1)
                if b == 0:
                    split_d(g, 4)
                    split_d(g, 5)

            def epi():
                add_tail(("D", GD - 1, 3), RING[("tail", "D", GD - 1, 3)])

            walk(pool, pro, step_a, step_b, step_c, step_d, epi)


def kernel(**inputs):
    import numpy as np
    import concourse.bacc as bacc
    from concourse.bass_utils import run_bass_kernel_spmd as run

    a = {k: np.asarray(v) for k, v in inputs.items()}

    def chunks(w):
        return w.reshape(-1, P, w.shape[-1]).transpose(1, 0, 2)

    gw_ = 256
    wk, wv, wq = (chunks(a[f"L0_attn_W{n}"]).reshape(P, NC, GA, gw_) for n in "kvq")
    kv = np.concatenate([wk, wv], axis=3).transpose(2, 0, 1, 3).reshape(GA, P, 2, 1024)
    wa = np.concatenate([kv, wq.transpose(2, 0, 1, 3).reshape(GA, P, 1, 1024),
                         a["L0_attn_Wo"].reshape(GA, 2, P, H).transpose(0, 2, 1, 3).reshape(GA, P, 1, 1024)], axis=2)
    def up(w):
        return w.reshape(GE, 2, P, NC, P).transpose(0, 4, 1, 3, 2)
    gu_ = np.stack([up(a["L0_ffn_gate_proj_w"]), up(a["L0_ffn_up_proj_w"])], axis=3).reshape(GE, P, 2048)
    dn_ = a["L0_ffn_down_proj_w"].reshape(GE, H, 2, P).transpose(0, 3, 2, 1).reshape(GE, P, 1024)
    wbe = np.concatenate([gu_, dn_], axis=2)
    def cols(w):
        return w.reshape(NC, P, GD, P, 4).transpose(2, 1, 4, 0, 3)
    gud_ = np.stack([cols(a["L1_ffn_w_gate"]), cols(a["L1_ffn_w_up"])], axis=3).reshape(GD, P, 4, 1024)
    dnd_ = a["L1_ffn_w_down"].reshape(GD, P, 4, H).reshape(GD, P, 2, 1024)
    wdn = np.concatenate([gud_, dnd_], axis=2)
    winout = np.concatenate([a["L1_attn_W_in"].reshape(8, P, H),
                             a["L1_attn_W_out"].T.reshape(8, P, H)], axis=2)
    coef = np.stack([a[f"L1_attn_{n}"].reshape(8, P, DS).transpose(1, 0, 2)
                     for n in ("A_theta", "B_real", "B_imag", "C_real", "C_imag")], axis=1)
    cT = np.stack([a[f"L{i}_c"].T.reshape(NC, P, NB).transpose(1, 0, 2) for i in range(2)], axis=1)
    wmods = [a[f"L{i}_wmod"].reshape(NC, P, 6, H).transpose(2, 1, 0, 3).reshape(6, P, NC * H) for i in range(2)]
    arrays = {
        "x_in": a["L0_attn_hidden_states"], "wa": wa, "wbe": wbe, "wdn": wdn, "winout": winout, "coef": coef,
        "cT": cT, "wmod0": wmods[0], "wmod1": wmods[1],
        "gwT": chunks(a["L0_ffn_gate_w"].T), "bo": a["L0_attn_bo"], "norm_w": a["L1_attn_norm_w"],
    }
    arrays = {k: np.ascontiguousarray(v) for k, v in arrays.items()}

    nc = bacc.Bacc("TRN2", target_bir_lowering=False, num_devices=1)
    args = [nc.dram_tensor(k, v.shape, F32, kind="ExternalInput").ap() for k, v in arrays.items()]
    out = nc.dram_tensor("out", (NB, S, H), F32, kind="ExternalOutput").ap()
    rows_d = nc.dram_tensor("rows_d", (6, NB, H), F32, kind="Internal").ap()
    build(nc, *args, out, rows_d)
    r = run(nc, [arrays], core_ids=[0])
    return r.results[0]["out"]
```

```python
from contextlib import ExitStack

import concourse.bass as bass
from concourse import mybir

F32 = mybir.dt.float32
F32R = mybir.dt.float32r
BF16 = mybir.dt.bfloat16
I32 = mybir.dt.int32
U32 = mybir.dt.uint32
ALU = mybir.AluOpType
ACT = mybir.ActivationFunctionType
AX_X = mybir.AxisListType.X

P = 128
NB = 4
S = 512
H = 512
NT = S // P
NC = H // P
GA = 8
GE = 8
GD = 4
HD = 64
VW = 2 * HD + 2
DS = 16
EPS = 1e-5
EPS_RMS = float(2.0 ** -23)
MAGIC = 1597463007.0
HI, LO = 0, 1
R_GA0, R_GB0, R_P1, R_Q1, R_R1, R_GB1 = range(6)
SA, CA, GAT, SB, CB, GBT = range(6)
COL_KIND = {SA: 0, CA: 1, SB: 2, CB: 3}
ROW_PART = [(0, GAT), (0, GBT), (1, SA), (1, CA), (1, GAT), (1, GBT)]
NSA, NSB, NSD = 4, 4, 6
BASE_B = NSA * GA
BASE_D = BASE_B + NSB * GE


def layernorms(stage, g, b):
    nxt = {"A": 1, "B": 2}.get(stage)
    if stage == "C":
        return (2, b + 2) if b < 2 else (3, b - 2)
    if isinstance(g, int) and g == 0 and b < 2:
        return {"A": 0, "B": 1, "D": 3}[stage], b + 2
    if nxt and isinstance(g, int) and g == 7 and b >= 2:
        return nxt, b - 2
    return None


def ln_index(k, b):
    return k * NB + b


def routed(stage, g, b):
    return b if stage == "B" and isinstance(g, int) and g == 0 else None


def gated_in(stage, g, b):
    if stage == "B" and isinstance(g, int) and g == GE - 1 and b >= 2:
        return b - 2
    return {1: 2, 3: 3}.get(b) if stage == "C" else None


def tail_of(stage, g, b):
    if b > 0:
        return (stage, g, b - 1) if stage != "C" else None
    if isinstance(g, int) and g == 0:
        return {"A": None, "B": ("A", GA - 1, 3), "C": ("B", GE - 1, 3), "D": None}[stage]
    return stage, g - 1, 3


def plan_ring():
    at, n = {("ln", 0, 0, 0): 0, ("ln", 0, 0, 1): 2, ("ln", 0, 1, 0): 4, ("ln", 0, 1, 1): 6}, 8
    for stage, groups in (("A", GA), ("B", GE), ("C", 1), ("D", GD)):
        for g in range(groups):
            for b in range(NB):
                tail, ln = tail_of(stage, g, b), layernorms(stage, g, b)
                parts = [("tail", *tail)] if tail else []
                if ln:
                    halves = [("ln", *ln, 0), ("ln", *ln, 1)]
                    parts = {"A": halves[:1] + parts + halves[1:], "B": halves[:1] + parts + halves[1:],
                             "C": parts + halves, "D": halves + parts}[stage]
                for part in parts:
                    at[part] = n
                    n += NT if part[0] == "tail" else NC // 2
                rt = routed(stage, g, b)
                if rt is not None:
                    at[("rt", rt)] = n
                    n += 1
    at[("tail", "D", GD - 1, 3)] = n
    return at


RING = plan_ring()


def ln_end(k, b):
    return RING[("ln", k, b, 1)] + NC // 2


def ring_at(stage, g, b):
    if isinstance(g, int):
        return RING[("tail", stage, g, b)]
    return g * (NB * NT) + (RING[("tail", stage, 1, b)] - NB * NT)


def ring_before(stage, g, b):
    tail = tail_of(stage, g, b)
    if tail is None:
        return None
    if isinstance(g, int):
        return RING[("tail", *tail)]
    if b > 0:
        return ring_at(stage, g, b - 1)
    return g * (NB * NT) + (RING[("tail", stage, 0, 3)] - NB * NT)


def walk(eng, pro, step_a, step_b, step_c, step_d, epi):
    pro()
    for step, groups in ((step_a, GA), (step_b, GE), (step_c, 0), (step_d, GD)):
        if groups == 0:
            for b in range(NB):
                step(b)
            continue
        for b in range(NB):
            step(0, b)
        with eng.Fori(1, groups - 1) as g:
            for b in range(NB):
                step(g, b)
        for b in range(NB):
            step(groups - 1, b)
    epi()


def build(nc, x_in, wa, wbe, wdn, winout, coef, cT, wmod0, wmod1, gwT, bo, norm_w, out, rows_d):
    with ExitStack() as ctx:
        def sb(name, shape, dt=F32):
            return ctx.enter_context(nc.sbuf_tensor(name, shape, dt))

        def sem(name):
            return ctx.enter_context(nc.semaphore(name))

        x = sb("x", [P, NB * NT, H])
        hT = sb("hT", [P, 2, NC, NB * S], F32R)
        stage = sb("stage", [P, 2, 1024])
        tmp = sb("tmp", [P, 2, S])
        row = sb("row", [P, 2, H])
        xn = sb("xn", [P, NT, H])
        ident = sb("ident", [P, P])
        modc = sb("modc", [P, 4, 2, NC, NB])
        scT = sb("scT", [P, 2, NC, NB])
        cTs = sb("cTs", [P, 2, NC, NB])
        kcoef = sb("kcoef", [P, 8])
        st6 = sb("st6", [P, NT, 6])
        mv = sb("mv", [P, NT, 2])
        ve = sb("ve", [P, NT])
        na = sb("na", [P, NT])
        rstd = sb("rstd", [P, NT])
        ssum = sb("ssum", [P, NT])
        gw = sb("gw", [P, 2, NC, 8], F32R)
        rw = sb("rw", [P, NB * NT, 8])
        rwe = sb("rwe", [P, NB * NT])
        iota8 = sb("iota8", [P, 8])
        gwr = sb("gwr", [P, NC, 8])
        lg = sb("lg", [P, NT, 8])
        pe8 = sb("pe8", [P, NT, 8])
        m4 = sb("m4", [P, 2, NT])
        v8 = sb("v8", [P, NT, 8])
        i8 = sb("i8", [P, NT, 8], U32)
        sel = sb("sel", [P, 2, NT, 8])

        def shared(makers):
            outs = []
            for maker in makers:
                with ExitStack() as part:
                    outs.append(maker(lambda name, shape, dt=F32: part.enter_context(
                        nc.sbuf_tensor(name, shape, dt))))
            return outs

        (W1a, mstage) = shared([lambda a: a("W1a", [P, 4096], F32R), lambda a: a("mstage", [P, 4, 1024])])
        hold1 = sb("hold1", [P, 4096])
        W1b = sb("W1b", [P, 4096], F32R)
        (W2, xw, (prow, ptmp)) = shared([lambda a: a("W2", [P, 4096], F32R),
                                     lambda a: a("xw", [P, 2, NT, H]),
                                     lambda a: (a("prow", [NB, 6, H]), a("ptmp", [NB, 2, H]))])
        hold2 = sb("hold2", [P, 4096])

        def over_pro(a):
            return a("wm", [P, 4, NC * H]), a("cin", [P, 5, 8, DS])

        def over_a(a):
            return (a("kt", [P, 2, 2, 256], F32R), a("vt", [P, 2, 2, 2, VW], F32R), a("qt", [P, 2, 2, S], F32R),
                    a("ot", [P, 2, 2, S], F32R), a("kvb", [P, 2, 2, 2, P], F32R), a("rr", [P, 2, S]),
                    a("bor", [P, H]))

        def over_b(a):
            return (a("sg", [P, 2, S]), a("pr", [P, 2, S]), a("ab", [P, 2, 2, S], F32R),
                    a("Wd", [P, 2, 2, 512], F32R), a("crow", [P, 3, H]), a("sqj", [P, S], BF16),
                    a("ct", [P, 2, S]))

        def over_d(a):
            return (a("hh", [P, 4, S]), a("mx", [P, S]), a("fl", [P, 6, S], BF16), a("ad", [P, 4, 2, S], F32R))

        ((wm, cin), (kt, vt, qt, ot, kvb, rr, bor), (sg, pr, ab, Wd, crow, sqj, ct),
         (hh, mx, fl, ad)) = shared([over_pro, over_a, over_b, over_d])
        hold3 = sb("hold3", [P, 9000])

        wkv = W1a[:, :].rearrange("p (s c n) -> p s c n", s=2, c=NC)
        wq = W1b[:, 0:2048].rearrange("p (s c n) -> p s c n", s=2, c=NC)
        wo = W1b[:, 2048:4096].rearrange("p (s c n) -> p s c n", s=2, c=2)
        gu = W2[:, :].rearrange("p (i s u c n) -> p i s u c n", i=2, s=2, u=2, c=NC)
        M = W1b[:, :].rearrange("p (s c n) -> p s c n", s=2, c=NC)
        gud = [w[:, :].rearrange("p (r s u c n) -> p r s u c n", r=2, s=2, u=2, c=NC) for w in (W1a, W1b)]
        wdd = W2[:, :].rearrange("p (s r n) -> p s r n", s=2, r=4)
        yn = [ct[:, 0, :], ct[:, 1, :], sg[:, 0, :], sg[:, 1, :]]

        def xn_of(k, b):
            if k == 2 and b >= 2:
                return xw[:, b - 2, :, :]
            return xn

        ab4 = xn

        bank = [ctx.enter_context(nc.psum_tensor(f"bank{i}", [P, 512], F32)) for i in range(8)]
        TAIL = bank[2:4]
        YB = [0, 1, 4, 5, 6, 7]

        x_in_s = [sem(f"x_loaded{b}") for b in range(NB)]
        small_loaded = sem("small_loaded")
        bo_loaded = sem("bo_loaded")
        wm_loaded = [sem(f"wmod_loaded{i}") for i in range(4)]
        nw_loaded = sem("norm_w_loaded")
        gw_loaded = sem("router_weights_loaded")
        zeroed = sem("identity_zeroed")
        silu_c = sem("silu_c_done")
        col_full = sem("mod_columns_full")
        col_done = sem("mod_columns_done")
        rowp_full = sem("mod_row_full")
        rowp_done = sem("mod_row_done")
        rows_ready = sem("rows_ready")
        rows_stored = sem("rows_stored")
        const_ready = sem("constants_ready")
        gw_hi_s = sem("router_weights_hi")
        gw_ready = sem("router_weights_ready")
        aconst = sem("stage_a_constants")
        pchain = sem("prologue_chain")
        stage_full = [sem(f"stage_full{i}") for i in range(2)]
        split_hi = sem("split_hi")
        split_done = sem("split_done")
        row_full = [sem(f"row_full{i}") for i in range(2)]
        crow_full = [sem(f"crow_full{i}") for i in range(3)]
        ring_full = sem("ring_full")
        ring_read = sem("ring_read")
        ring_done = sem("ring_done")
        ln_chain = sem("ln_chain")
        xn_ready = sem("xn_ready")
        h_hi = sem("h_hi")
        pq_mul = sem("pq_mul")
        pq_sum = sem("pq_sum")
        pq_add = sem("pq_added")
        pj_full = sem("a_proj_full")
        pj_hi = sem("a_proj_hi")
        pj_lo = sem("a_proj_lo")
        kvmm = sem("a_kv_accumulated")
        kvb_hi = sem("a_kvb_hi")
        kvb_lo = sem("a_kvb_lo")
        nn_full = sem("a_norm_num_full")
        r_max = sem("a_norm_clipped")
        r_rec = sem("a_norm_inverted")
        o_num = sem("a_out_normalised")
        o_hi = sem("a_out_hi")
        o_lo = sem("a_out_lo")
        bo_add = sem("a_bias_added")
        bg_full = sem("b_gate_full")
        bu_full = sem("b_up_full")
        b_silu = sem("b_silu_done")
        b_p = sem("b_product_done")
        b_hi = sem("b_act_hi")
        b_lo = sem("b_act_lo")
        rwe_done = sem("b_rwe_done")
        m_loaded = [sem(f"m_loaded{i}") for i in range(4)]
        m_scaled = sem("m_scaled")
        m_used = sem("m_used")
        m_hi = sem("m_hi")
        m_lo = sem("m_lo")
        rt_chain = sem("router_chain")
        rt_sub = sem("router_shifted")
        rt_exp = sem("router_exp")
        y_full = sem("c_y_full")
        y_sq = sem("c_y_squared")
        y_read = sem("c_y_read")
        c_add = sem("c_x_added")
        dg_full = sem("d_gate_full")
        du_full = sem("d_up_full")
        d_silu = sem("d_silu_done")
        d_h = sem("d_h_done")
        d_abs = sem("d_abs_done")
        d_sp = sem("d_sparsify_chain")
        d_hi = sem("d_act_hi")
        d_lo = sem("d_act_lo")
        out_stored = sem("out_stored")

        block = ctx.enter_context(nc.Block())
        NSP = 17

        @block.sync
        def _(sp):
            sp.dma_start(cTs[:, :, :, :], cT).then_inc(small_loaded, 16)
            sp.dma_start(cin[:, :, :, :], coef).then_inc(small_loaded, 16)

            def wmod_part(n):
                src = (wmod0, wmod1)[n // 6][n % 6]
                if n >= 4:
                    sp.wait_ge(col_full, sum(m % 6 in COL_KIND for m in range(n - 3)))
                    if any((m // 6, m % 6) in ROW_PART for m in range(n - 3)):
                        sp.wait_ge(rowp_full, sum((m // 6, m % 6) in ROW_PART for m in range(n - 3)))
                sp.dma_start(wm[:, n % 4, :], src).then_inc(wm_loaded[n % 4], 16)

            def raw(n, j, src, size):
                if not (isinstance(n, int) and n < 2):
                    sp.wait_ge(split_done, n - 1)
                sp.dma_start(stage[:, j % 2, 0:size], src).then_inc(stage_full[j % 2], 16)

            def wa_slice(g, j):
                raw(g * NSA + j, j, wa[bass.ds(g, 1), :, j, :].rearrange("a p n -> p (a n)"), 1024)

            def wb_slice(e, j):
                n = e * NSB + (BASE_B + j)
                off, size = ((0, 1024), (1024, 1024), (2048, 512), (2560, 512))[j]
                raw(n, j, wbe[bass.ds(e, 1), :, off:off + size].rearrange("a p n -> p (a n)"), size)

            def wd_slice(g, j):
                raw(g * NSD + (BASE_D + j), j, wdn[bass.ds(g, 1), :, j, :].rearrange("a p n -> p (a n)"), 1024)

            def pro():
                wmod_part(0)
                wmod_part(1)
                wa_slice(0, 0)
                wa_slice(0, 1)
                wmod_part(2)
                wmod_part(3)
                wa_slice(0, 2)
                wa_slice(0, 3)
                for n in range(4, 12):
                    wmod_part(n)
                sp.wait_ge(rows_ready, 1)
                sp.dma_start(rows_d.rearrange("k b n -> b k n"), prow[:, :, :]).then_inc(rows_stored, 16)

            def step_a(g, b):
                if isinstance(g, int) and g == 0 and b == 0:
                    sp.wait_ge(aconst, 1)
                    sp.dma_start(bor[:, :], bo.partition_broadcast(P)).then_inc(bo_loaded, 16)
                if b == 2 and not (isinstance(g, int) and g == GA - 1):
                    for j in range(3):
                        wa_slice(g + 1, j)
                if b == 0 and not (isinstance(g, int) and g == 0):
                    wa_slice(g, 3)
                if b == 2 and isinstance(g, int) and g == GA - 1:
                    wb_slice(0, 0)
                    wb_slice(0, 1)

            def m_load(n):
                if n >= 4:
                    sp.wait_ge(m_used, n - 3)
                else:
                    sp.wait_ge(pj_full, 6 * NB * GA)
                sp.dma_start(mstage[:, n % 4, :], winout[n % 8]).then_inc(m_loaded[n % 4], 16)

            def step_b(e, b):
                if b == 0:
                    wb_slice(e, 2)
                    wb_slice(e, 3)
                if isinstance(e, int) and e == 0:
                    for n in range(4 * b, 4 * b + 4):
                        m_load(n)
                if b == 2 and not (isinstance(e, int) and e == GE - 1):
                    wb_slice(e + 1, 0)
                    wb_slice(e + 1, 1)
                if b == 3 and isinstance(e, int) and e == GE - 1:
                    wd_slice(0, 0)
                    wd_slice(0, 1)

            def step_c(b):
                if b == 3:
                    wd_slice(0, 2)
                    wd_slice(0, 3)

            def step_d(g, b):
                if b == 0:
                    wd_slice(g, 4)
                    wd_slice(g, 5)
                if b == 2 and not (isinstance(g, int) and g == GD - 1):
                    for j in range(4):
                        wd_slice(g + 1, j)
                if isinstance(g, int) and g == GD - 1 and b >= 1:
                    store(b - 1)

            def store(b):
                sp.wait_ge(ring_done, RING[("tail", "D", GD - 1, b)] + NT)
                sp.dma_start(out[b].rearrange("(t p) n -> p t n", p=P),
                             x[:, b * NT:(b + 1) * NT, :]).then_inc(out_stored, 16)

            def epi():
                store(3)
                sp.wait_ge(out_stored, 16 * NB)
                sp.wait_ge(rows_stored, 16)

            walk(sp, pro, step_a, step_b, step_c, step_d, epi)

        @block.tensor
        def _(pe):
            def mm3(o, lhs, rhs, start, stop, **kw):
                pe.matmul(o, lhs(HI), rhs(HI), start=start, stop=False, **kw)
                pe.matmul(o, lhs(HI), rhs(LO), start=False, stop=False, **kw)
                return pe.matmul(o, lhs(LO), rhs(HI), start=False, stop=stop, **kw)

            def hcol(c, b, t):
                return lambda s: hT[:, s, c, b * S + t * P:b * S + (t + 1) * P]

            def hrow(c, b):
                return lambda s: hT[:, s, c, b * S:(b + 1) * S]

            def ring_slot(n, par):
                if not (isinstance(n, int) and n < 2):
                    pe.wait_ge(ring_read, n - 1)
                return TAIL[par]

            def par_of(stage, g, b, t):
                base = RING[("tail", stage, g if isinstance(g, int) else 1, b)]
                return (base + t) % 2

            def ln_transposes(ln, half):
                if ln is None:
                    return
                k, b = ln
                if half == 0:
                    pe.wait_ge(xn_ready, ln_index(k, b) + 1)
                for i in range(2):
                    n, c = RING[("ln", k, b, half)] + i, 2 * half + i
                    o = ring_slot(n, n % 2)
                    for t in range(NT):
                        last = pe.transpose(o[:, t * P:(t + 1) * P], xn_of(k, b)[:, t, c * P:(c + 1) * P], ident[:, :])
                    last.then_inc(ring_full, 1)

            def need_h(k, b):
                pe.wait_ge(ring_done, ln_end(k, b))

            def router(b):
                n = RING[("rt", b)]
                need_h(1, b)
                pe.wait_ge(gw_ready, 1)
                o = ring_slot(n, n % 2)
                for t in range(NT):
                    for c in range(NC):
                        last = mm3(o[:, t * 8:(t + 1) * 8], hcol(c, b, t), lambda s, c=c: gw[:, s, c, :],
                                   c == 0, c == NC - 1)
                last.then_inc(ring_full, 1)

            def extras(stage_, g, b):
                rt = routed(stage_, g, b)
                if rt is not None:
                    router(rt)

            def pro():
                pe.wait_ge(silu_c, 1)
                cols, rows = COL_KIND, ROW_PART
                for n in range(12):
                    layer, kind = n // 6, n % 6
                    w = wm[:, n % 4, :].rearrange("p (c n) -> p c n", c=NC)
                    pe.wait_ge(wm_loaded[n % 4], 16 * (n // 4 + 1))
                    if kind in cols:
                        k, sc = 2 * layer + cols[kind] // 2, cols[kind] % 2
                        o = bank[0 if k == 0 else 1]
                        for m in range(NC):
                            at = ((k % 4) * 2 + sc) * 16 + m * NB
                            for c in range(NC):
                                last = pe.matmul(o[:, at:at + NB], w[:, c, m * P:(m + 1) * P],
                                                 scT[:, layer, c, :], start=c == 0, stop=c == NC - 1)
                        last.then_inc(col_full, 1)
                    if (layer, kind) in rows:
                        i = rows.index((layer, kind))
                        if i >= 2:
                            pe.wait_ge(rowp_done, i - 1)
                        for c in range(NC):
                            last = pe.matmul(bank[6 + i % 2][0:NB, :], scT[:, layer, c, :], w[:, c, :],
                                             start=c == 0, stop=c == NC - 1)
                        last.then_inc(rowp_full, 1)
                pe.wait_ge(const_ready, 1)
                for b in range(2):
                    ln_transposes((0, b), 0)
                    ln_transposes((0, b), 1)

            def tail_a(g, b, n0):
                s = g * NB + b
                pe.wait_ge(o_lo, s * 2 + 2)
                if b == 0:
                    pe.wait_ge(split_done, g * NSA + 4)
                for t in range(NT):
                    o = ring_slot(n0 + t, par_of("A", g, b, t))
                    for c in range(2):
                        last = mm3(o[:, :], lambda h, c=c: ot[:, h, c, t * P:(t + 1) * P],
                                   lambda h, c=c: wo[:, h, c, :], c == 0, c == 1)
                    last.then_inc(ring_full, 1)

            def tails(stage_, g, b):
                tail = tail_of(stage_, g, b)
                if tail is None:
                    return
                n0 = ring_before(stage_, g, b)
                {"A": tail_a, "B": tail_b, "D": tail_d}[tail[0]](tail[1], tail[2], n0)

            def step_a(g, b):
                s = g * NB + b
                first = isinstance(g, int) and g == 0
                if first:
                    need_h(0, b)
                    if b == 0:
                        pe.wait_ge(aconst, 1)
                if b == 0:
                    pe.wait_ge(split_done, g * NSA + 2)

                def accumulate(t):
                    pe.wait_ge(pj_lo, s * 6 + (t + 1))
                    if t == 0 and not (first and b == 0):
                        pe.wait_ge(r_max, s * 2)
                    for pair in range(2):
                        last = mm3(bank[4][:, pair * VW:(pair + 1) * VW],
                                   lambda h: kt[:, t % 2, h, pair * P:(pair + 1) * P],
                                   lambda h: vt[:, t % 2, h, pair, :],
                                   t == 0 and pair == 0, t == NT - 1, skip_group_check=True)
                    last.then_inc(kvmm, 1)

                for t in range(NT):
                    if not (first and b == 0 and t < 2):
                        pe.wait_ge(pj_lo, s * 6 + (t - 1))
                    for c in range(NC):
                        last = mm3(bank[t % 2][:, :], hcol(c, b, t), lambda h, c=c: wkv[:, h, c, :],
                                   c == 0, c == NC - 1)
                    last.then_inc(pj_full, 1)
                    if t > 0:
                        accumulate(t - 1)
                if b == 0:
                    pe.wait_ge(split_done, g * NSA + 3)
                for pair in range(2):
                    pe.wait_ge(pj_lo, s * 6 + (3 + pair))
                    for c in range(NC):
                        last = mm3(bank[pair][:, :], lambda h, c=c: wq[:, h, c, pair * P:(pair + 1) * P],
                                   hrow(c, b), c == 0, c == NC - 1)
                    last.then_inc(pj_full, 1)
                    if pair == 0:
                        accumulate(NT - 1)
                ln = layernorms("A", g, b)
                ln_transposes(ln, 0)
                tails("A", g, b)
                ln_transposes(ln, 1)
                pe.wait_ge(pj_lo, s * 6 + 6)
                pe.wait_ge(kvb_lo, s + 1)
                for kind, banks in ((1, (5, 4)), (0, (6, 7))):
                    for pair in range(2):
                        mm3(bank[banks[pair]][:, :], lambda h: kvb[:, h, pair, kind, :],
                            lambda h: qt[:, h, pair, :], True, True).then_inc(nn_full, 1)
                extras("A", g, b)

            def tail_b(e, b, n0):
                s = e * NB + b
                pe.wait_ge(b_lo, s * 2 + 2)
                if b == 0:
                    pe.wait_ge(split_done, e * NSB + (BASE_B + 4))
                for t in range(NT):
                    o = ring_slot(n0 + t, par_of("B", e, b, t))
                    for i in range(2):
                        last = mm3(o[:, :], lambda h, i=i: ab[:, h, i, t * P:(t + 1) * P],
                                   lambda h, i=i: Wd[:, h, i, :], i == 0, i == 1)
                    last.then_inc(ring_full, 1)

            def step_b(e, b):
                s = e * NB + b
                first = isinstance(e, int) and e == 0
                if first:
                    need_h(1, b)
                for i in range(2):
                    if b == 0:
                        pe.wait_ge(split_done, e * NSB + (BASE_B + i + 1))
                    if first and b == 0:
                        pe.wait_ge(pj_lo, 6 * NB * GA)
                        pe.wait_ge(r_max, 2 * NB * GA)
                    else:
                        pe.wait_ge(b_p, s * 2 + (i - 1))
                    for u, o, full in ((0, bank[i], bg_full), (1, bank[4 + i], bu_full)):
                        for c in range(NC):
                            last = mm3(o[:, :], lambda h, c=c: gu[:, i, h, u, c, :], hrow(c, b),
                                       c == 0, c == NC - 1)
                        last.then_inc(full, 1)
                ln = layernorms("B", e, b)
                ln_transposes(ln, 0)
                tails("B", e, b)
                ln_transposes(ln, 1)
                extras("B", e, b)
                if first:
                    for n in range(4 * b, 4 * b + 4):
                        half, ic = n // 8, n % 8
                        pe.wait_ge(m_scaled, n + 1)
                        if n == 0:
                            pe.wait_ge(o_lo, 2 * NB * GA)
                        if n == 8:
                            pe.wait_ge(m_lo, 2)
                        for j in range(2):
                            m = 2 * half + j
                            last = pe.matmul(bank[6 + j][:, :], mstage[:, n % 4, m * P:(m + 1) * P],
                                             mstage[:, n % 4, 512:1024], start=ic == 0, stop=ic == 7)
                        last.then_inc(m_used, 1)
            def step_c(b):
                need_h(2, b)
                if b == 0:
                    pe.wait_ge(m_lo, 4)
                    pe.wait_ge(b_p, 2 * NB * GE)
                tails("C", 0, b)
                for t in range(NT):
                    n = NT * b + t
                    if n >= 6:
                        pe.wait_ge(y_read, n - 5)
                    for c in range(NC):
                        last = mm3(bank[YB[n % 6]][:, :], hcol(c, b, t), lambda h, c=c: M[:, h, c, :],
                                   c == 0, c == NC - 1)
                    last.then_inc(y_full, 1)
                for half in range(2):
                    ln_transposes(layernorms("C", 0, b), half)

            def tail_d(g, b, n0):
                s = g * NB + b
                pe.wait_ge(d_lo, s * 4 + 4)
                if b == 0:
                    pe.wait_ge(split_done, g * NSD + (BASE_D + 6))
                for t in range(NT):
                    o = ring_slot(n0 + t, par_of("D", g, b, t))
                    for r in range(4):
                        last = mm3(o[:, :], lambda h, r=r: ad[:, r, h, t * P:(t + 1) * P],
                                   lambda h, r=r: wdd[:, h, r, :], r == 0, r == 3)
                    last.then_inc(ring_full, 1)

            def step_d(g, b):
                s = g * NB + b
                first = isinstance(g, int) and g == 0
                if first:
                    need_h(3, b)
                if first and b == 0:
                    pe.wait_ge(y_read, NT * NB)
                for r in range(4):
                    if b == 0:
                        pe.wait_ge(split_done, g * NSD + (BASE_D + r + 1))
                    if not (first and b == 0 and r < 2):
                        pe.wait_ge(d_h, s * 4 + (r - 1))
                    for u, o, full in ((0, bank[r % 2], dg_full), (1, bank[4 + r % 2], du_full)):
                        for c in range(NC):
                            last = mm3(o[:, :], lambda h, c=c: gud[r // 2][:, r % 2, h, u, c, :], hrow(c, b),
                                       c == 0, c == NC - 1)
                        last.then_inc(full, 1)
                    if b == 0 and r in (1, 2):
                        ln_transposes(layernorms("D", g, b), r - 1)
                if b > 0:
                    ln_transposes(layernorms("D", g, b), 0)
                    ln_transposes(layernorms("D", g, b), 1)
                tails("D", g, b)

            def epi():
                tail_d(GD - 1, 3, RING[("tail", "D", GD - 1, 3)])

            walk(pe, pro, step_a, step_b, step_c, step_d, epi)

        @block.scalar
        def _(act):
            def load_row(stage_, g, b):
                kind = {"A": R_GA0, "B": R_GB0, "D": R_GB1}[stage_]
                if stage_ == "A" and isinstance(g, int) and g == 0:
                    if b == 0:
                        act.wait_ge(rows_stored, 16)
                    if b >= 2:
                        act.wait_ge(ring_read, RING[("tail", "A", 0, b - 2)] + NT)
                elif isinstance(g, int) and g == 0 and b < 2:
                    prev = {"B": ("A", GA - 1), "D": ("B", GE - 1)}[stage_]
                    act.wait_ge(ring_read, RING[("tail", *prev, b + 2)] + NT)
                elif b >= 2:
                    act.wait_ge(ring_read, ring_at(stage_, g, b - 2) + NT)
                elif isinstance(g, int):
                    act.wait_ge(ring_read, RING[("tail", stage_, g - 1, b + 2)] + NT)
                else:
                    act.wait_ge(ring_read, g * (NB * NT) + (RING[("tail", stage_, 1, b + 2)] - 2 * NB * NT + NT))
                act.dma_start(row[:, b % 2, :], rows_d[kind, b, :].partition_broadcast(P)) \
                    .then_inc(row_full[b % 2], 16)

            def wsplit(count, j, dst, size):
                act.wait_ge(stage_full[j % 2], count)
                act.activation(dst, stage[:, j % 2, 0:size], ACT.Copy).then_inc(split_hi, 1)

            def split_a(g, j):
                dst = (W1a[:, 0:1024], W1a[:, 1024:2048], W1b[:, 0:1024], W1b[:, 2048:3072])[j]
                wsplit(g * 32 + 16 * (j // 2 + 1), j, dst, 1024)

            def split_b(e, j):
                dst = (W2[:, 0:1024], W2[:, 2048:3072], Wd[:, HI, 0, :], Wd[:, HI, 1, :])[j]
                wsplit(e * 32 + (8 * BASE_B + 16 * (j // 2 + 1)), j, dst, (1024, 1024, 512, 512)[j])

            def split_d(g, j):
                w = (W1a, W1a, W1b, W1b)[j] if j < 4 else None
                dst = w[:, (j % 2) * 2048:(j % 2) * 2048 + 1024] if j < 4 else \
                    W2[:, (j - 4) * 1024:(j - 3) * 1024]
                wsplit(g * 48 + (8 * BASE_D + 16 * (j // 2 + 1)), j, dst, 1024)

            def ln_out(ln, half):
                if ln is None:
                    return
                k, b = ln
                n0 = RING[("ln", k, b, half)]
                if k < 2:
                    act.wait_ge(col_done, (2, 8)[k])
                if n0 > 0:
                    act.wait_ge(ring_read, n0)
                for i in range(2):
                    n, c = n0 + i, 2 * half + i
                    act.wait_ge(ring_full, n + 1)
                    if n >= 2:
                        act.wait_ge(ring_done, n - 1)
                    act.activation(tmp[:, n % 2, :], TAIL[n % 2][:, :], ACT.Identity,
                                   scale=modc[:, k, 1, c, b:b + 1], bias=modc[:, k, 0, c, b:b + 1]) \
                        .then_inc(ring_read, 1)
                    act.wait_ge(ring_read, n + 1)
                    act.activation(hT[:, HI, c, b * S:(b + 1) * S], tmp[:, n % 2, :], ACT.Copy) \
                        .then_inc(h_hi, 1)

            def router(b):
                act.wait_ge(rt_sub, b + 1)
                act.activation(pe8[:, :, :], lg[:, :, :], ACT.Exp).then_inc(rt_exp, 1)

            def extras(stage_, g, b):
                rt = routed(stage_, g, b)
                if rt is not None:
                    router(rt)

            def pro():
                for b in range(NB):
                    act.dma_start(x[:, b * NT:(b + 1) * NT, :], x_in[b].rearrange("(t p) n -> p t n", p=P)) \
                        .then_inc(x_in_s[b], 16)
                act.wait_ge(small_loaded, 32)
                act.activation(scT[:, :, :, :], cTs[:, :, :, :], ACT.Silu).then_inc(silu_c, 1)
                for j in range(2):
                    split_a(0, j)
                ln_out((0, 0), 0)
                ln_out((0, 0), 1)
                split_a(0, 2)
                split_a(0, 3)
                ln_out((0, 1), 0)
                ln_out((0, 1), 1)

            def crows(which, b):
                if b > 0 and which < 2:
                    act.wait_ge(pq_sum, NT * b)
                elif b > 0:
                    act.wait_ge(y_read, NT * b)
                act.dma_start(crow[:, which, :], rows_d[R_P1 + which, b, :].partition_broadcast(P)) \
                    .then_inc(crow_full[which], 16)

            def gated_rows(stage_, g, b):
                if stage_ == "B" and gated_in("B", g, b) is not None:
                    crows(0, gated_in("B", g, b))
                    crows(1, gated_in("B", g, b))
                if stage_ == "C" and b in (0, 3):
                    crows(0, 2 + b // 3)
                    crows(1, 2 + b // 3)

            def out_hi(s, pair):
                act.wait_ge(o_num, s * 2 + (pair - 1))
                act.activation(ot[:, HI, pair, :], bank[6 + pair][:, :], ACT.Copy).then_inc(o_hi, 1)

            def step_a(g, b):
                s = g * NB + b
                first = isinstance(g, int) and g == 0
                last = isinstance(g, int) and g == GA - 1
                load_row("A", g, b)
                for t in range(NT):
                    act.wait_ge(pj_full, s * 6 + (t + 1))
                    if not (first and b == 0 and t < 2):
                        act.wait_ge(kvmm, s * 4 + (t - 1))
                    act.activation(kt[:, t % 2, HI, :], bank[t % 2][:, 0:256], ACT.Relu)
                    act.activation(vt[:, t % 2, HI, :, 0:P],
                                   bank[t % 2][:, 256:512].rearrange("p (a n) -> p a n", a=2), ACT.Copy) \
                        .then_inc(pj_hi, 1)
                if b == 3 and not last:
                    split_a(g + 1, 0)
                    split_a(g + 1, 1)
                if b == 3 and last:
                    split_b(0, 0)
                    split_b(0, 1)
                if tail_of("A", g, b):
                    out_hi(s, 0)
                    out_hi(s, 1)
                for pair in range(2):
                    act.wait_ge(pj_full, s * 6 + (5 + pair))
                    if pair == 0 and not (first and b == 0):
                        act.wait_ge(nn_full, s * 4)
                    act.activation(qt[:, HI, pair, :], bank[pair][:, :], ACT.Relu).then_inc(pj_hi, 1)
                ln = layernorms("A", g, b)
                ln_out(ln, 0)
                act.wait_ge(kvmm, s * 4 + 4)
                if first and b == 0:
                    act.wait_ge(aconst, 1)
                kv = bank[4][:, 0:2 * VW].rearrange("p (a n) -> p a n", a=2)
                for lo in (0, HD):
                    q = slice(lo, lo + HD)
                    act.activation(kvb[q, HI, :, 0, q], kv[q, :, q], ACT.Copy)
                    ins = act.activation(kvb[q, HI, :, 1, q], kv[q, :, P:P + 1].to_broadcast([HD, 2, HD]), ACT.Copy)
                ins.then_inc(kvb_hi, 1)
                ln_out(ln, 1)
                if b == 3 and not last:
                    split_a(g + 1, 2)
                if b == 0 and not first:
                    act.wait_ge(ring_full, ring_before("A", g, b) + NT)
                    split_a(g, 3)
                extras("A", g, b)

            def step_b(e, b):
                s = e * NB + b
                first = isinstance(e, int) and e == 0
                load_row("B", e, b)
                if first and b == 0:
                    for pair in range(2):
                        out_hi(NB * GA, pair)
                    act.wait_ge(kvmm, NT * NB * GA)
                for i in range(2):
                    act.wait_ge(bg_full, s * 2 + (i + 1))
                    if not (first and b == 0):
                        act.wait_ge(b_p, s * 2 + (i - 1))
                    act.activation(sg[:, i, :], bank[i][:, :], ACT.Silu).then_inc(b_silu, 1)
                    if b == 3 and not (isinstance(e, int) and e == GE - 1):
                        act.wait_ge(bu_full, s * 2 + (i + 1))
                        split_b(e + 1, i)
                gated_rows("B", e, b)
                if first:
                    for n in range(4 * b, 4 * b + 4):
                        act.wait_ge(m_loaded[n % 4], 16 * (n // 4 + 1))
                        act.activation(mstage[:, n % 4, 512:1024], mstage[:, n % 4, 512:1024], ACT.Copy,
                                       scale=kcoef[:, n % 8:n % 8 + 1]).then_inc(m_scaled, 1)
                ln = layernorms("B", e, b)
                ln_out(ln, 0)
                if tail_of("B", e, b):
                    act.wait_ge(ring_full, ring_before("B", e, b) + NT)
                for i in range(2):
                    act.wait_ge(b_p, s * 2 + (i + 1))
                    act.activation(ab[:, HI, i, :], pr[:, i, :], ACT.Copy).then_inc(b_hi, 1)
                if b == 0:
                    split_b(e, 2)
                    split_b(e, 3)
                ln_out(ln, 1)
                extras("B", e, b)
                if first and b in (1, 3):
                    for j in range(2):
                        m = (b - 1) + j
                        act.wait_ge(m_used, 8 * (m // 2 + 1))
                        act.activation(M[:, HI, m, :], bank[6 + j][:, :], ACT.Copy).then_inc(m_hi, 1)

            def step_c(b):
                gated_rows("C", 0, b)
                crows(2, b)
                for t in range(NT):
                    n = NT * b + t
                    act.wait_ge(y_full, n + 1)
                    if t == 0 and b > 0:
                        act.wait_ge(y_read, NT * b)
                    if n > 0:
                        act.wait_ge(y_sq, n)
                    act.activation(sqj[:, :], bank[YB[n % 6]][:, :], ACT.Square,
                                   accum_out=ssum[:, t:t + 1]).then_inc(y_sq, 1)
                ln_out(layernorms("C", 0, b), 0)
                ln_out(layernorms("C", 0, b), 1)
                if b < 2:
                    if b == 0:
                        act.wait_ge(m_lo, 4)
                    split_d(0, b)

            def step_d(g, b):
                s = g * NB + b
                first = isinstance(g, int) and g == 0
                ln = layernorms("D", g, b)
                load_row("D", g, b)

                def absolute(r):
                    act.wait_ge(d_h, s * 4 + (r + 1))
                    if r == 0:
                        if ln:
                            act.wait_ge(ring_full, ln_end(*ln))
                        if not (first and b == 0):
                            act.wait_ge(d_sp, s * NSP)
                    act.activation(ab4[:, r, :], hh[:, r, :], ACT.Abs).then_inc(d_abs, 1)

                if first and b == 0:
                    act.wait_ge(y_full, NT * NB)
                    split_d(0, 2)
                    split_d(0, 3)
                for r in range(4):
                    act.wait_ge(dg_full, s * 4 + (r + 1))
                    if first and b == 0 and r == 0:
                        act.wait_ge(ring_done, RING[("tail", "B", GE - 1, 3)] + NT)
                    if not (first and b == 0):
                        act.wait_ge(d_lo, s * 4 + (r - 3))
                    act.activation(hh[:, r, :], bank[r % 2][:, :], ACT.Silu).then_inc(d_silu, 1)
                    if b == 3 and not (isinstance(g, int) and g == GD - 1):
                        act.wait_ge(du_full, s * 4 + (r + 1))
                        split_d(g + 1, r)
                    if b == 0 and r in (1, 2):
                        ln_out(ln, r - 1)
                    if not ln and r > 0:
                        absolute(r - 1)
                if ln and b > 0:
                    ln_out(ln, 0)
                    ln_out(ln, 1)
                for r in range(4) if ln else (3,):
                    absolute(r)
                if tail_of("D", g, b):
                    act.wait_ge(ring_full, ring_before("D", g, b) + NT)
                if first and b == 0:
                    act.wait_ge(c_add, NT * NB)
                for r in range(4):
                    act.wait_ge(d_sp, s * NSP + (NSP - 3 + r))
                    act.activation(ad[:, r, HI, :], hh[:, r, :], ACT.Copy).then_inc(d_hi, 1)
                if b == 0:
                    if first:
                        act.wait_ge(pq_add, NT * NB)
                    split_d(g, 4)
                    split_d(g, 5)

            walk(act, pro, step_a, step_b, step_c, step_d, lambda: None)

        @block.vector
        def _(dve):
            def link(ins, sem_, count):
                ins.then_inc(sem_, 1)
                dve.wait_ge(sem_, count)

            chain = {"ln": 0, "p": 0, "rt": 0}

            def seq(ins, which):
                chain[which] += 1
                link(ins, {"ln": ln_chain, "p": pchain, "rt": rt_chain}[which], chain[which])

            def take(n, par, after_act=False):
                if after_act:
                    dve.wait_ge(ring_read, n)
                dve.wait_ge(ring_full, n + 1)
                if not (isinstance(n, int) and n < 2):
                    dve.wait_ge(ring_done, n - 1)

            def inv_sqrt():
                seq(dve.tensor_scalar(rstd[:, :].bitcast(I32), ve[:, :].bitcast(I32), -0.5, MAGIC,
                                      ALU.mult, ALU.add), "ln")
                for _ in range(3):
                    seq(dve.tensor_tensor(na[:, :], ve[:, :], rstd[:, :], ALU.mult), "ln")
                    seq(dve.scalar_tensor_tensor(out=na[:, :], in0=na[:, :], scalar=-0.5, in1=rstd[:, :],
                                                 op0=ALU.mult, op1=ALU.mult), "ln")
                    seq(dve.scalar_tensor_tensor(out=rstd[:, :], in0=na[:, :], scalar=1.5, in1=rstd[:, :],
                                                 op0=ALU.add, op1=ALU.mult), "ln")

            def ln_stats(k, b, tiles):
                if 0 in tiles:
                    if k == 0:
                        dve.wait_ge(x_in_s[b], 16)
                    elif k == 3:
                        dve.wait_ge(c_add, NT * (b + 1))
                        dve.wait_ge(pq_add, NT * (b + 1))
                    else:
                        prev = {1: ("A", GA - 1), 2: ("B", GE - 1)}[k]
                        dve.wait_ge(ring_done, RING[("tail", *prev, b)] + NT)
                for t in tiles:
                    last = dve.bn_stats(st6[:, t, :], x[:, b * NT + t, :])
                seq(last, "ln")
                for t in tiles:
                    last = dve.bn_aggr(mv[:, t, :], st6[:, t, :])
                seq(last, "ln")

            def ln_rstd():
                seq(dve.tensor_scalar(ve[:, :], mv[:, :, 1], EPS, None, ALU.add), "ln")
                inv_sqrt()

            def ln_apply(k, b):
                n = ln_index(k, b)
                if n > 0:
                    dve.wait_ge(ring_full, ln_end((n - 1) // NB, (n - 1) % NB))
                if (k, b) in ((2, 1), (3, 0)):
                    dve.wait_ge(pq_add, NT * (b if b else 2))
                for t in range(NT):
                    last = dve.tensor_scalar(xn_of(k, b)[:, t, :], x[:, b * NT + t, :], mv[:, t, 0:1], rstd[:, t:t + 1],
                                             ALU.subtract, ALU.mult)
                last.then_inc(xn_ready, 1)

            def gated(b):
                xg = xn_of(2, b)
                dve.wait_ge(ring_full, ln_end(2, b))
                dve.wait_ge(crow_full[0], 16 * (b + 1))
                dve.wait_ge(crow_full[1], 16 * (b + 1))
                for t in range(NT):
                    dve.tensor_tensor(xg[:, t, :], xg[:, t, :], crow[:, 0, :], ALU.mult).then_inc(pq_mul, 1)
                for t in range(NT):
                    dve.wait_ge(pq_mul, NT * b + t + 1)
                    dve.tensor_tensor(xg[:, t, :], xg[:, t, :], crow[:, 1, :], ALU.add).then_inc(pq_sum, 1)

            def router(b):
                n = RING[("rt", b)]
                take(n, n % 2, True)
                dve.tensor_copy(tmp[:, n % 2, 0:NT * 8], TAIL[n % 2][:, 0:NT * 8]).then_inc(ring_read, 1)
                dve.wait_ge(ring_done, n + 1)
                seq(dve.tensor_reduce(m4[:, 0, :], lg[:, :, :], AX_X, ALU.max), "rt")
                dve.tensor_tensor(lg[:, :, :], lg[:, :, :], m4[:, 0, :].unsqueeze(2).to_broadcast([P, NT, 8]),
                                  ALU.subtract).then_inc(rt_sub, 1)
                dve.wait_ge(rt_exp, b + 1)
                seq(dve.tensor_reduce(m4[:, 0, :], pe8[:, :, :], AX_X, ALU.add), "rt")
                seq(dve.reciprocal(m4[:, 1, :], m4[:, 0, :]), "rt")
                seq(dve.tensor_tensor(pe8[:, :, :], pe8[:, :, :], m4[:, 1, :].unsqueeze(2).to_broadcast([P, NT, 8]),
                                      ALU.mult), "rt")
                for t in range(NT):
                    seq(dve.max(v8[:, t, :], pe8[:, t, :]), "rt")
                    seq(dve.max_index(i8[:, t, :], v8[:, t, :], pe8[:, t, :]), "rt")
                    for j in range(2):
                        seq(dve.tensor_scalar(sel[:, j, t, :], iota8[:, :], i8[:, t, j:j + 1], None,
                                              ALU.is_equal), "rt")
                seq(dve.tensor_tensor(m4[:, 0, :], v8[:, :, 0], v8[:, :, 1], ALU.add), "rt")
                seq(dve.reciprocal(m4[:, 1, :], m4[:, 0, :]), "rt")
                seq(dve.tensor_tensor(sel[:, 0, :, :], sel[:, 0, :, :], sel[:, 1, :, :], ALU.add), "rt")
                seq(dve.tensor_tensor(pe8[:, :, :], pe8[:, :, :], m4[:, 1, :].unsqueeze(2).to_broadcast([P, NT, 8]),
                                      ALU.mult), "rt")
                seq(dve.tensor_tensor(rw[:, b * NT:(b + 1) * NT, :], pe8[:, :, :], sel[:, 0, :, :], ALU.mult), "rt")

            def late(stage_, g, b):
                if gated_in(stage_, g, b) is not None:
                    gated(gated_in(stage_, g, b))
                rt = routed(stage_, g, b)
                if rt is not None:
                    router(rt)

            def pro():
                for e in range(8):
                    dve.memset(iota8[:, e:e + 1], float(e))
                dve.wait_ge(small_loaded, 32)
                for j, other in ((1, 3), (2, 4)):
                    seq(dve.scalar_tensor_tensor(out=cin[:, j, :, :], in0=cin[:, 0, :, :], scalar=0.0,
                                                 in1=cin[:, j, :, :], op0=ALU.mult, op1=ALU.add), "p")
                    seq(dve.tensor_tensor(cin[:, j, :, :], cin[:, j, :, :], cin[:, other, :, :], ALU.mult), "p")
                seq(dve.tensor_tensor(cin[:, 1, :, :], cin[:, 1, :, :], cin[:, 2, :, :], ALU.subtract), "p")
                seq(dve.tensor_reduce(kcoef[:, :], cin[:, 1, :, :], AX_X, ALU.add), "p")
                ln_stats(0, 0, range(NT))
                ln_rstd()
                ln_apply(0, 0)

                def columns(n, k, sc):
                    dve.wait_ge(col_full, n)
                    src = bank[0 if k == 0 else 1][:, (k * 2 + sc) * 16:(k * 2 + sc + 1) * 16] \
                        .rearrange("p (c b) -> p c b", c=NC)
                    dve.tensor_scalar(modc[:, k, sc, :, :], src, float(sc), None, ALU.add).then_inc(col_done, 1)

                columns(2, 0, 0)
                columns(2, 0, 1)
                def fetch(i, dst):
                    dve.wait_ge(rowp_full, i + 1)
                    ins = dve.tensor_copy(dst, bank[6 + i % 2][0:NB, :])
                    link(ins, rowp_done, i + 1)

                def gate(v, dst, done=None):
                    seq(dve.tensor_scalar(ptmp[:, 1, :], v, 0.0, 2.0, ALU.is_ge, ALU.mult), "p")
                    seq(dve.scalar_tensor_tensor(out=v, in0=v, scalar=-1.0, in1=v, op0=ALU.mult, op1=ALU.max), "p")
                    seq(dve.tensor_scalar(v, v, 0.25, None, ALU.max), "p")
                    ins = dve.scalar_tensor_tensor(out=dst, in0=ptmp[:, 1, :], scalar=-1.0, in1=v,
                                                   op0=ALU.add, op1=ALU.mult)
                    if done:
                        ins.then_inc(done, 1)
                    else:
                        seq(ins, "p")

                fetch(0, ptmp[:, 0, :])
                gate(ptmp[:, 0, :], prow[:, R_GA0, :])
                fetch(1, ptmp[:, 0, :])
                gate(ptmp[:, 0, :], prow[:, R_GB0, :])
                fetch(2, prow[:, R_Q1, :])
                fetch(3, prow[:, R_P1, :])
                fetch(4, ptmp[:, 0, :])
                gate(ptmp[:, 0, :], prow[:, R_GB1, :])
                g1 = prow[:, R_GB1, :]
                seq(dve.scalar_tensor_tensor(out=prow[:, R_P1, :], in0=prow[:, R_P1, :], scalar=1.0, in1=g1,
                                             op0=ALU.add, op1=ALU.mult), "p")
                seq(dve.tensor_tensor(prow[:, R_Q1, :], prow[:, R_Q1, :], g1, ALU.mult), "p")
                dve.wait_ge(nw_loaded, 16)
                seq(dve.tensor_tensor(prow[:, R_R1, :], prow[:, R_R1, :], g1, ALU.mult), "p")
                fetch(5, ptmp[:, 0, :])
                gate(ptmp[:, 0, :], prow[:, R_GB1, :], rows_ready)
                for n, (k, sc) in enumerate(((1, 0), (1, 1), (2, 0), (2, 1), (3, 0), (3, 1))):
                    columns(8, k, sc)
                dve.wait_ge(col_full, 8)
                dve.memset(kvb[:, :, :, :, :].bitcast(F32), 0.0)
                dve.memset(vt[:, :, HI, :, P:VW].bitcast(F32), 1.0)
                dve.memset(vt[:, :, LO, :, P:VW].bitcast(F32), 0.0).then_inc(aconst, 1)
                ln_stats(0, 1, range(NT))
                ln_rstd()
                ln_apply(0, 1)

            def stats(ln, tiles):
                if ln:
                    ln_stats(*ln, tiles)
                    if NT - 1 in tiles:
                        ln_rstd()

            def tail_evac(stage_, g, b, t):
                tail = tail_of(stage_, g, b) if stage_ != "end" else ("D", GD - 1, 3)
                if tail is None:
                    return
                n0 = ring_before(stage_, g, b) if stage_ != "end" else RING[("tail", "D", GD - 1, 3)]
                ts, tg, tb = tail
                key = RING[("tail", ts, tg if isinstance(tg, int) else 1, tb)]
                par = (key + t) % 2
                if t == 0:
                    rn0 = {"A": 0, "B": NB * GA, "D": NB * (GA + GE)}[ts]
                    dve.wait_ge(row_full[tb % 2], tg * 32 + (8 * rn0 + 16 * (tb // 2 + 1)))
                take(n0 + t, par, t == 0)
                if ts == "B":
                    dve.scalar_tensor_tensor(out=tmp[:, par, :], in0=TAIL[par][:, :],
                                             scalar=rwe[:, tb * NT + t:tb * NT + t + 1], in1=row[:, tb % 2, :],
                                             op0=ALU.mult, op1=ALU.mult).then_inc(ring_read, 1)
                elif ts == "A" and isinstance(tg, int) and tg == GA - 1:
                    if t == 0 and tb == 0:
                        dve.wait_ge(bo_loaded, 16)
                    link(dve.tensor_tensor(tmp[:, par, :], TAIL[par][:, :], bor[:, :], ALU.add),
                         bo_add, tb * NT + t + 1)
                    dve.tensor_tensor(tmp[:, par, :], tmp[:, par, :], row[:, tb % 2, :], ALU.mult) \
                        .then_inc(ring_read, 1)
                else:
                    dve.tensor_tensor(tmp[:, par, :], TAIL[par][:, :], row[:, tb % 2, :], ALU.mult) \
                        .then_inc(ring_read, 1)

            def invert(s, pair):
                dve.wait_ge(r_max, s * 2 + (pair - 1))
                dve.reciprocal(rr[:, pair, :], rr[:, pair, :]).then_inc(r_rec, 1)

            def normalise(s, pair):
                dve.wait_ge(nn_full, s * 4 + (pair - 1))
                dve.wait_ge(r_rec, s * 2 + (pair - 1))
                dve.tensor_tensor(bank[6 + pair][:, :], bank[6 + pair][:, :], rr[:, pair, :], ALU.mult) \
                    .then_inc(o_num, 1)

            def out_lo(s, pair):
                dve.wait_ge(o_hi, s * 2 + (pair - 1))
                dve.tensor_tensor(ot[:, LO, pair, :], bank[6 + pair][:, :],
                                  ot[:, HI, pair, :].bitcast(F32), ALU.subtract).then_inc(o_lo, 1)

            def step_a(g, b):
                s = g * NB + b
                ln = layernorms("A", g, b)
                for t in range(NT):
                    dve.wait_ge(pj_hi, s * 6 + (t + 1))
                    dve.scalar_tensor_tensor(out=kt[:, t % 2, LO, :], in0=bank[t % 2][:, 0:256], scalar=0.0,
                                             in1=kt[:, t % 2, HI, :].bitcast(F32), op0=ALU.max, op1=ALU.subtract)
                    dve.tensor_tensor(vt[:, t % 2, LO, :, 0:P],
                                      bank[t % 2][:, 256:512].rearrange("p (a n) -> p a n", a=2),
                                      vt[:, t % 2, HI, :, 0:P].bitcast(F32), ALU.subtract).then_inc(pj_lo, 1)
                    if tail_of("A", g, b):
                        if t == 0:
                            invert(s, 1)
                        if t >= 2:
                            normalise(s, t % 2)
                    if t in (1, 2):
                        stats(ln, (2 * t - 2, 2 * t - 1))
                if tail_of("A", g, b):
                    out_lo(s, 0)
                    out_lo(s, 1)
                if ln:
                    ln_apply(*ln)
                for pair in range(2):
                    dve.wait_ge(pj_hi, s * 6 + (5 + pair))
                    dve.scalar_tensor_tensor(out=qt[:, LO, pair, :], in0=bank[pair][:, :], scalar=0.0,
                                             in1=qt[:, HI, pair, :].bitcast(F32), op0=ALU.max,
                                             op1=ALU.subtract).then_inc(pj_lo, 1)
                tail_evac("A", g, b, 0)
                dve.wait_ge(kvb_hi, s + 1)
                kv = bank[4][:, 0:2 * VW].rearrange("p (a n) -> p a n", a=2)
                for lo in (0, HD):
                    q = slice(lo, lo + HD)
                    dve.tensor_tensor(kvb[q, LO, :, 0, q], kv[q, :, q], kvb[q, HI, :, 0, q].bitcast(F32),
                                      ALU.subtract)
                    last = dve.tensor_tensor(kvb[q, LO, :, 1, q], kv[q, :, P:P + 1].to_broadcast([HD, 2, HD]),
                                             kvb[q, HI, :, 1, q].bitcast(F32), ALU.subtract)
                last.then_inc(kvb_lo, 1)
                for t in range(1, NT):
                    tail_evac("A", g, b, t)
                for pair in range(2):
                    dve.wait_ge(nn_full, s * 4 + (pair + 1))
                    if tail_of("A", g, b):
                        dve.wait_ge(o_num, s * 2)
                    dve.tensor_scalar(rr[:, pair, :], bank[(5, 4)[pair]][:, :], 1e-6, None, ALU.max) \
                        .then_inc(r_max, 1)
                invert(s + 1, 0)

            def split_b(e, i):
                n = e * NSB + (BASE_B + i)
                dve.wait_ge(split_hi, n + 1)
                dve.wait_ge(split_done, n)
                dve.tensor_tensor(W2[:, i * 2048 + 1024:(i + 1) * 2048], stage[:, i, :],
                                  W2[:, i * 2048:i * 2048 + 1024].bitcast(F32), ALU.subtract) \
                    .then_inc(split_done, 1)

            def step_b(e, b):
                s = e * NB + b
                if isinstance(e, int) and e == 0 and b == 0:
                    invert(NB * GA, 1)
                    for part in (normalise, out_lo):
                        for pair in range(2):
                            part(NB * GA, pair)
                ln = layernorms("B", e, b)
                stats(ln, range(NT))
                for i in range(2):
                    dve.wait_ge(bu_full, s * 2 + (i + 1))
                    dve.wait_ge(b_silu, s * 2 + (i + 1))
                    if not (isinstance(e, int) and e == 0 and b == 0):
                        dve.wait_ge(b_lo, s * 2 + (i - 1))
                    dve.tensor_tensor(pr[:, i, :], sg[:, i, :], bank[4 + i][:, :], ALU.mult).then_inc(b_p, 1)
                    if b == 3 and not (isinstance(e, int) and e == GE - 1):
                        split_b(e + 1, i)
                    if ln and i == 0:
                        ln_apply(*ln)
                for t in range(NT):
                    tail_evac("B", e, b, t)
                if b == 0:
                    if not (isinstance(e, int) and e == 0):
                        dve.wait_ge(ring_read, ring_before("B", e, b) + NT)
                        link(dve.tensor_copy(rwe[:, :], rw[:, :, bass.ds(e, 1)].rearrange("p t a -> p (t a)")),
                             rwe_done, e)
                for i in range(2):
                    dve.wait_ge(b_hi, s * 2 + (i + 1))
                    dve.tensor_tensor(ab[:, LO, i, :], pr[:, i, :], ab[:, HI, i, :].bitcast(F32),
                                      ALU.subtract).then_inc(b_lo, 1)
                late("B", e, b)
                if isinstance(e, int) and e == 0:
                    seq(dve.tensor_copy(rwe[:, b * NT:(b + 1) * NT], rw[:, b * NT:(b + 1) * NT, 0]), "rt")
                    if b in (1, 3):
                        for j in range(2):
                            m = (b - 1) + j
                            dve.wait_ge(m_hi, m + 1)
                            dve.tensor_tensor(M[:, LO, m, :], bank[6 + j][:, :], M[:, HI, m, :].bitcast(F32),
                                              ALU.subtract).then_inc(m_lo, 1)

            def step_c(b):
                for t in range(NT):
                    tail_evac("C", 0, b, t)
                ln = layernorms("C", 0, b)
                stats(ln, range(NT))
                ln_apply(*ln)
                dve.wait_ge(y_sq, NT * (b + 1))
                seq(dve.tensor_scalar(ve[:, :], ssum[:, :], 1.0 / H, EPS_RMS, ALU.mult, ALU.add), "ln")
                inv_sqrt()
                dve.wait_ge(crow_full[2], 16 * (b + 1))
                for t in range(NT):
                    n = NT * b + t
                    if n >= 4:
                        dve.wait_ge(c_add, n - 3)
                    dve.scalar_tensor_tensor(out=yn[n % 4], in0=bank[YB[n % 6]][:, :],
                                             scalar=rstd[:, t:t + 1], in1=crow[:, 2, :], op0=ALU.mult,
                                             op1=ALU.mult).then_inc(y_read, 1)
                if gated_in("C", 0, b) is not None:
                    gated(gated_in("C", 0, b))

            def step_d(g, b):
                s = g * NB + b
                ln = layernorms("D", g, b)
                if ln and b == 0:
                    stats(ln, range(NT))
                    ln_apply(*ln)
                for r in range(4):
                    dve.wait_ge(du_full, s * 4 + (r + 1))
                    dve.wait_ge(d_silu, s * 4 + (r + 1))
                    dve.tensor_tensor(hh[:, r, :], hh[:, r, :], bank[4 + r % 2][:, :], ALU.mult).then_inc(d_h, 1)
                    if ln and b > 0 and r == 1:
                        stats(ln, range(NT))
                    if ln and b > 0 and r == 2:
                        ln_apply(*ln)
                done = [0]

                def op(ins):
                    done[0] += 1
                    ins.then_inc(d_sp, 1)

                def after(k):
                    dve.wait_ge(d_sp, s * NSP + k)

                c01, c23, fa, fb, fs, ft = (fl[:, i, :] for i in range(6))
                a = [ab4[:, r, :] for r in range(4)]
                tt = dve.tensor_tensor
                dve.wait_ge(d_abs, s * 4 + 2)
                op(tt(c01, a[0], a[1], ALU.is_ge))
                op(tt(mx[:, :], a[0], a[1], ALU.max))
                tail_evac("D", g, b, 0)
                op(tt(a[0], a[0], a[1], ALU.min))
                dve.wait_ge(d_abs, s * 4 + 4)
                op(tt(c23, a[2], a[3], ALU.is_ge))
                after(4)
                op(tt(a[1], a[2], a[3], ALU.max))
                tail_evac("D", g, b, 1)
                op(tt(a[2], a[2], a[3], ALU.min))
                after(5)
                op(tt(fb, a[0], a[1], ALU.is_ge))
                after(6)
                op(tt(fa, mx[:, :], a[2], ALU.is_ge))
                tail_evac("D", g, b, 2)
                after(8)
                op(tt(fs, fa, fb, ALU.add))
                after(9)
                op(tt(ft, fs, c01, ALU.add))
                op(tt(fa, fs, c01, ALU.subtract))
                op(tt(fb, fs, c23, ALU.subtract))
                op(tt(fs, fs, c23, ALU.add))
                tail_evac("D", g, b, 3)
                for r, (flag, bound, cmp) in enumerate(((ft, 2.0, ALU.is_ge), (fa, 1.0, ALU.is_ge),
                                                        (fb, 0.0, ALU.is_le), (fs, 1.0, ALU.is_le))):
                    after(10 + r)
                    op(dve.scalar_tensor_tensor(out=hh[:, r, :], in0=flag, scalar=bound, in1=hh[:, r, :],
                                                op0=cmp, op1=ALU.mult))
                assert done[0] == NSP

            def epi():
                for t in range(NT):
                    tail_evac("end", GD - 1, 3, t)

            walk(dve, pro, step_a, step_b, step_c, step_d, epi)

        @block.gpsimd
        def _(pool):
            def lo_part(dst, src, hi):
                return pool.tensor_tensor(dst, src, hi.bitcast(F32), ALU.subtract)

            def wsplit(n, j, lo, hi, size):
                pool.wait_ge(split_hi, n + 1)
                if not (isinstance(n, int) and n == 0):
                    pool.wait_ge(split_done, n)
                lo_part(lo, stage[:, j % 2, 0:size], hi).then_inc(split_done, 1)

            def split_a(g, j):
                w, at = ((W1a, 0), (W1a, 1024), (W1b, 0), (W1b, 2048))[j]
                off = (2048, 2048, 1024, 1024)[j]
                wsplit(g * NSA + j, j, w[:, at + off:at + off + 1024], w[:, at:at + 1024], 1024)

            def split_b(e, j):
                n = e * NSB + (BASE_B + j)
                if j < 2:
                    wsplit(n, j, W2[:, j * 2048 + 1024:(j + 1) * 2048], W2[:, j * 2048:j * 2048 + 1024], 1024)
                else:
                    wsplit(n, j, Wd[:, LO, j - 2, :], Wd[:, HI, j - 2, :], 512)

            def split_d(g, j):
                n = g * NSD + (BASE_D + j)
                if j < 4:
                    w, at = (W1a, W1a, W1b, W1b)[j], (j % 2) * 2048
                    wsplit(n, j, w[:, at + 1024:at + 2048], w[:, at:at + 1024], 1024)
                else:
                    at = (j - 4) * 1024
                    wsplit(n, j, W2[:, 2048 + at:2048 + at + 1024], W2[:, at:at + 1024], 1024)

            def ln_out(ln, half):
                if ln is None:
                    return
                k, b = ln
                for i in range(2):
                    n, c = RING[("ln", k, b, half)] + i, 2 * half + i
                    pool.wait_ge(h_hi, ln_index(k, b) * NC + c + 1)
                    hs = slice(b * S, (b + 1) * S)
                    lo_part(hT[:, LO, c, hs], tmp[:, n % 2, :], hT[:, HI, c, hs]).then_inc(ring_done, 1)

            def gated_add(b):
                if b is not None:
                    if b == 3:
                        pool.wait_ge(c_add, NT * NB)
                    for t in range(NT):
                        pool.wait_ge(pq_sum, NT * b + t + 1)
                        xt = x[:, b * NT + t, :]
                        pool.tensor_tensor(xt, xt, xn_of(2, b)[:, t, :], ALU.add).then_inc(pq_add, 1)

            def extras(stage_, g, b):
                rt = routed(stage_, g, b)
                if rt is not None:
                    n = RING[("rt", rt)]
                    pool.wait_ge(ring_read, n + 1)
                    pool.tensor_copy(lg[:, :, :], tmp[:, n % 2, 0:NT * 8].rearrange("p (t e) -> p t e", t=NT)) \
                        .then_inc(ring_done, 1)

            def add_tail(tail, n0):
                ts, tg, tb = tail
                key = RING[("tail", ts, tg if isinstance(tg, int) else 1, tb)]
                for t in range(NT):
                    pool.wait_ge(ring_read, n0 + t + 1)
                    xt = x[:, tb * NT + t, :]
                    pool.tensor_tensor(xt, xt, tmp[:, (key + t) % 2, :], ALU.add).then_inc(ring_done, 1)

            def tails(stage_, g, b):
                tail = tail_of(stage_, g, b)
                if tail:
                    add_tail(tail, ring_before(stage_, g, b))

            def pro():
                pool.memset(ident[:, :], 0.0).then_inc(zeroed, 1)
                pool.wait_ge(zeroed, 1)
                pool.affine_select(out=ident[:, :], in_=ident[:, :], compare_op=ALU.not_equal, fill=1.0, base=0,
                                   pattern=[[-1, P]], channel_multiplier=1).then_inc(const_ready, 1)
                pool.dma_start(prow[:, R_R1, :], norm_w.partition_broadcast(NB)).then_inc(nw_loaded, 16)
                pool.dma_start(gwr[:, :, :], gwT).then_inc(gw_loaded, 16)
                pool.wait_ge(gw_loaded, 16)
                pool.tensor_copy(gw[:, HI, :, :], gwr[:, :, :]).then_inc(gw_hi_s, 1)
                pool.wait_ge(gw_hi_s, 1)
                lo_part(gw[:, LO, :, :], gwr[:, :, :], gw[:, HI, :, :]).then_inc(gw_ready, 1)
                split_a(0, 0)
                split_a(0, 1)
                ln_out((0, 0), 0)
                ln_out((0, 0), 1)
                split_a(0, 2)
                split_a(0, 3)
                ln_out((0, 1), 0)
                ln_out((0, 1), 1)

            def step_a(g, b):
                if b == 3 and not (isinstance(g, int) and g == GA - 1):
                    for j in range(3):
                        split_a(g + 1, j)
                if b == 3 and isinstance(g, int) and g == GA - 1:
                    split_b(0, 0)
                    split_b(0, 1)
                ln = layernorms("A", g, b)
                ln_out(ln, 0)
                tails("A", g, b)
                if b == 0 and not (isinstance(g, int) and g == 0):
                    split_a(g, 3)
                ln_out(ln, 1)
                extras("A", g, b)

            def step_b(e, b):
                ln = layernorms("B", e, b)
                ln_out(ln, 0)
                tails("B", e, b)
                if b == 0:
                    split_b(e, 2)
                    split_b(e, 3)
                ln_out(ln, 1)
                gated_add(gated_in("B", e, b))
                extras("B", e, b)

            def step_c(b):
                tails("C", 0, b)
                ln = layernorms("C", 0, b)
                if b == 2:
                    pool.wait_ge(pq_add, NT * 3)
                for t in range(NT):
                    n = NT * b + t
                    pool.wait_ge(y_read, n + 1)
                    xt = x[:, NT * b + t, :]
                    pool.tensor_tensor(xt, xt, yn[n % 4], ALU.add).then_inc(c_add, 1)
                ln_out(ln, 0)
                ln_out(ln, 1)
                if b < 2:
                    split_d(0, b)
                gated_add(gated_in("C", 0, b))

            def step_d(g, b):
                s = g * NB + b
                if isinstance(g, int) and g == 0 and b == 0:
                    split_d(0, 2)
                    split_d(0, 3)
                if b == 3 and not (isinstance(g, int) and g == GD - 1):
                    for j in range(4):
                        split_d(g + 1, j)
                ln = layernorms("D", g, b)
                ln_out(ln, 0)
                ln_out(ln, 1)
                tails("D", g, b)
                for r in range(4):
                    pool.wait_ge(d_hi, s * 4 + (r + 1))
                    lo_part(ad[:, r, LO, :], hh[:, r, :], ad[:, r, HI, :]).then_inc(d_lo, 1)
                if b == 0:
                    split_d(g, 4)
                    split_d(g, 5)

            def epi():
                add_tail(("D", GD - 1, 3), RING[("tail", "D", GD - 1, 3)])

            walk(pool, pro, step_a, step_b, step_c, step_d, epi)


def kernel(**inputs):
    import numpy as np
    import concourse.bacc as bacc
    from concourse.bass_utils import run_bass_kernel_spmd as run

    a = {k: np.asarray(v) for k, v in inputs.items()}

    def chunks(w):
        return w.reshape(-1, P, w.shape[-1]).transpose(1, 0, 2)

    gw_ = 256
    wk, wv, wq = (chunks(a[f"L0_attn_W{n}"]).reshape(P, NC, GA, gw_) for n in "kvq")
    kv = np.concatenate([wk, wv], axis=3).transpose(2, 0, 1, 3).reshape(GA, P, 2, 1024)
    wa = np.concatenate([kv, wq.transpose(2, 0, 1, 3).reshape(GA, P, 1, 1024),
                         a["L0_attn_Wo"].reshape(GA, 2, P, H).transpose(0, 2, 1, 3).reshape(GA, P, 1, 1024)], axis=2)
    def up(w):
        return w.reshape(GE, 2, P, NC, P).transpose(0, 4, 1, 3, 2)
    gu_ = np.stack([up(a["L0_ffn_gate_proj_w"]), up(a["L0_ffn_up_proj_w"])], axis=3).reshape(GE, P, 2048)
    dn_ = a["L0_ffn_down_proj_w"].reshape(GE, H, 2, P).transpose(0, 3, 2, 1).reshape(GE, P, 1024)
    wbe = np.concatenate([gu_, dn_], axis=2)
    def cols(w):
        return w.reshape(NC, P, GD, P, 4).transpose(2, 1, 4, 0, 3)
    gud_ = np.stack([cols(a["L1_ffn_w_gate"]), cols(a["L1_ffn_w_up"])], axis=3).reshape(GD, P, 4, 1024)
    dnd_ = a["L1_ffn_w_down"].reshape(GD, P, 4, H).reshape(GD, P, 2, 1024)
    wdn = np.concatenate([gud_, dnd_], axis=2)
    winout = np.concatenate([a["L1_attn_W_in"].reshape(8, P, H),
                             a["L1_attn_W_out"].T.reshape(8, P, H)], axis=2)
    coef = np.stack([a[f"L1_attn_{n}"].reshape(8, P, DS).transpose(1, 0, 2)
                     for n in ("A_theta", "B_real", "B_imag", "C_real", "C_imag")], axis=1)
    cT = np.stack([a[f"L{i}_c"].T.reshape(NC, P, NB).transpose(1, 0, 2) for i in range(2)], axis=1)
    wmods = [a[f"L{i}_wmod"].reshape(NC, P, 6, H).transpose(2, 1, 0, 3).reshape(6, P, NC * H) for i in range(2)]
    arrays = {
        "x_in": a["L0_attn_hidden_states"], "wa": wa, "wbe": wbe, "wdn": wdn, "winout": winout, "coef": coef,
        "cT": cT, "wmod0": wmods[0], "wmod1": wmods[1],
        "gwT": chunks(a["L0_ffn_gate_w"].T), "bo": a["L0_attn_bo"], "norm_w": a["L1_attn_norm_w"],
    }
    arrays = {k: np.ascontiguousarray(v) for k, v in arrays.items()}

    nc = bacc.Bacc("TRN2", target_bir_lowering=False, num_devices=1)
    args = [nc.dram_tensor(k, v.shape, F32, kind="ExternalInput").ap() for k, v in arrays.items()]
    out = nc.dram_tensor("out", (NB, S, H), F32, kind="ExternalOutput").ap()
    rows_d = nc.dram_tensor("rows_d", (6, NB, H), F32, kind="Internal").ap()
    build(nc, *args, out, rows_d)
    r = run(nc, [arrays], core_ids=[0])
    return r.results[0]["out"]
```

```python
from contextlib import ExitStack

import concourse.bass as bass
from concourse import mybir

F32 = mybir.dt.float32
F32R = mybir.dt.float32r
BF16 = mybir.dt.bfloat16
I32 = mybir.dt.int32
U32 = mybir.dt.uint32
ALU = mybir.AluOpType
ACT = mybir.ActivationFunctionType
AX_X = mybir.AxisListType.X

P = 128
NB = 4
S = 512
H = 512
NT = S // P
NC = H // P
GA = 8
GE = 8
GD = 4
HD = 64
VW = 2 * HD + 2
DS = 16
EPS = 1e-5
EPS_RMS = float(2.0 ** -23)
MAGIC = 1597463007.0
HI, LO = 0, 1
R_GA0, R_GB0, R_P1, R_Q1, R_R1, R_GB1 = range(6)
SA, CA, GAT, SB, CB, GBT = range(6)
COL_KIND = {SA: 0, CA: 1, SB: 2, CB: 3}
ROW_KIND = {(0, GAT): R_GA0, (0, GBT): R_GB0, (1, SA): R_Q1, (1, CA): R_P1, (1, GAT): R_R1, (1, GBT): R_GB1}
MOD_PARTS = [(0, GAT), (0, SB), (0, CB), (0, GBT), (1, GAT), (1, SA), (1, CA), (1, SB), (1, CB), (1, GBT)]
MOD_FINISH = [(0,), (3,), (4, 5), (6, 9)]
MOD_PLACE = [(0, 0), (0, 1), (0, 2), (1, 0), (1, 2), (2, 0), (2, 1), (2, 2), (3, 0), (3, 2)]
NSA, NSB, NSD = 4, 4, 6
BASE_B = NSA * GA
BASE_D = BASE_B + NSB * GE


def layernorms(stage, g, b):
    nxt = {"A": 1, "B": 2}.get(stage)
    if stage == "C":
        return (2, b + 2) if b < 2 else (3, b - 2)
    if stage == "A" and isinstance(g, int) and g == 0:
        return (0, b + 1) if b < 3 else None
    if isinstance(g, int) and g == 0 and b < 2:
        return {"B": 1, "D": 3}[stage], b + 2
    if nxt and isinstance(g, int) and g == 7 and b >= 2:
        return nxt, b - 2
    return None


def ln_index(k, b):
    return k * NB + b


def routed(stage, g, b):
    return b if stage == "B" and isinstance(g, int) and g == 0 else None


def mod_uses(g, b, place):
    if not (isinstance(g, int) and g == 0 and (b, place) in MOD_PLACE):
        return []
    i = MOD_PLACE.index((b, place))
    return ([(i - 1, "col")] if i > 0 and MOD_PARTS[i - 1][1] in COL_KIND else []) + [(i, "row")]


def gated_in(stage, g, b):
    if stage == "B" and isinstance(g, int) and g == GE - 1 and b >= 2:
        return b - 2
    return {1: 2, 3: 3}.get(b) if stage == "C" else None


def tail_of(stage, g, b):
    if b > 0:
        return (stage, g, b - 1) if stage != "C" else None
    if isinstance(g, int) and g == 0:
        return {"A": None, "B": ("A", GA - 1, 3), "C": ("B", GE - 1, 3), "D": None}[stage]
    return stage, g - 1, 3


def plan_ring():
    at, n = {("ln", 0, 0, 0): 0, ("ln", 0, 0, 1): 2}, 4
    for stage, groups in (("A", GA), ("B", GE), ("C", 1), ("D", GD)):
        for g in range(groups):
            for b in range(NB):
                tail, ln = tail_of(stage, g, b), layernorms(stage, g, b)
                parts = [("tail", *tail)] if tail else []
                if ln:
                    halves = [("ln", *ln, 0), ("ln", *ln, 1)]
                    parts = {"A": halves[:1] + parts + halves[1:], "B": halves[:1] + parts + halves[1:],
                             "C": parts + halves, "D": halves + parts}[stage]
                if stage == "A" and g == 0:
                    mods = [[("mod", *use) for use in mod_uses(0, b, k)] for k in range(3)]
                    parts = mods[0] + mods[1] + (halves if ln else []) + mods[2] + ([("tail", *tail)] if tail else [])
                for part in parts:
                    at[part] = n
                    n += {"tail": NT, "ln": NC // 2, "mod": 1}[part[0]]
                rt = routed(stage, g, b)
                if rt is not None:
                    at[("rt", rt)] = n
                    n += 1
    at[("tail", "D", GD - 1, 3)] = n
    return at


RING = plan_ring()


def ln_end(k, b):
    return RING[("ln", k, b, 1)] + NC // 2


def ring_at(stage, g, b):
    if isinstance(g, int):
        return RING[("tail", stage, g, b)]
    return g * (NB * NT) + (RING[("tail", stage, 1, b)] - NB * NT)


def ring_before(stage, g, b):
    tail = tail_of(stage, g, b)
    if tail is None:
        return None
    if isinstance(g, int):
        return RING[("tail", *tail)]
    if b > 0:
        return ring_at(stage, g, b - 1)
    return g * (NB * NT) + (RING[("tail", stage, 0, 3)] - NB * NT)


def walk(eng, pro, step_a, step_b, step_c, step_d, epi):
    pro()
    for step, groups in ((step_a, GA), (step_b, GE), (step_c, 0), (step_d, GD)):
        if groups == 0:
            for b in range(NB):
                step(b)
            continue
        for b in range(NB):
            step(0, b)
        with eng.Fori(1, groups - 1) as g:
            for b in range(NB):
                step(g, b)
        for b in range(NB):
            step(groups - 1, b)
    epi()


def build(nc, x_in, wa, wbe, wdn, winout, coef, cT, wmod0, wmod1, gwT, bo, norm_w, out, rows_d):
    with ExitStack() as ctx:
        def sb(name, shape, dt=F32):
            return ctx.enter_context(nc.sbuf_tensor(name, shape, dt))

        def sem(name):
            return ctx.enter_context(nc.semaphore(name))

        x = sb("x", [P, NB * NT, H])
        hT = sb("hT", [P, 2, NC, NB * S], F32R)
        stage = sb("stage", [P, 2, 1024])
        tmp = sb("tmp", [P, 2, S])
        row = sb("row", [P, 2, H])
        xn = sb("xn", [P, NT, H])
        ident = sb("ident", [P, P])
        modc = sb("modc", [P, 4, 2, NC, NB])
        scT = sb("scT", [P, 2, NC, NB])
        cTs = sb("cTs", [P, 2, NC, NB])
        kcoef = sb("kcoef", [P, 8])
        st6 = sb("st6", [P, NT, 6])
        mv = sb("mv", [P, NT, 2])
        ve = sb("ve", [P, NT])
        na = sb("na", [P, NT])
        rstd = sb("rstd", [P, NT])
        ssum = sb("ssum", [P, NT])
        gw = sb("gw", [P, 2, NC, 8], F32R)
        rw = sb("rw", [P, NB * NT, 8])
        rwe = sb("rwe", [P, NB * NT])
        iota8 = sb("iota8", [P, 8])
        gwr = sb("gwr", [P, NC, 8])
        lg = sb("lg", [P, NT, 8])
        pe8 = sb("pe8", [P, NT, 8])
        m4 = sb("m4", [P, 2, NT])
        v8 = sb("v8", [P, NT, 8])
        i8 = sb("i8", [P, NT, 8], U32)
        mark = sb("mark", [1, len(MOD_PARTS)])
        sel = sb("sel", [P, 2, NT, 8])

        def shared(makers):
            outs = []
            for maker in makers:
                with ExitStack() as part:
                    outs.append(maker(lambda name, shape, dt=F32: part.enter_context(
                        nc.sbuf_tensor(name, shape, dt))))
            return outs

        (W1a, mstage) = shared([lambda a: a("W1a", [P, 4096], F32R), lambda a: a("mstage", [P, 4, 1024])])
        hold1 = sb("hold1", [P, 4096])
        W1b = sb("W1b", [P, 4096], F32R)
        (W2, xw, (mw, prow)) = shared([lambda a: a("W2", [P, 4096], F32R),
                                     lambda a: a("xw", [P, 2, NT, H]),
                                     lambda a: (a("mw", [P, NC * H]), a("prow", [NB, 4, H]))])
        hold2 = sb("hold2", [P, 4096])

        def over_pro(a):
            return a("before_wm", [P, 2064]), a("wm", [P, 2, NC * H])

        def over_a(a):
            return (a("kt", [P, 2, 2, 256], F32R), a("vt", [P, 2, 2, 2, VW], F32R), a("qt", [P, 2, 2, S], F32R),
                    a("ot", [P, 2, 2, S], F32R), a("kvb", [P, 2, 2, 2, P], F32R), a("rr", [P, 2, S]),
                    a("bor", [P, H]), a("colrow", [NB, H]))

        def over_b(a):
            return (a("sg", [P, 2, S]), a("pr", [P, 2, S]), a("ab", [P, 2, 2, S], F32R),
                    a("Wd", [P, 2, 2, 512], F32R), a("crow", [P, 3, H]), a("sqj", [P, S], BF16),
                    a("ct", [P, 2, S]))

        def over_d(a):
            return (a("hh", [P, 4, S]), a("mx", [P, S]), a("fl", [P, 6, S], BF16), a("ad", [P, 4, 2, S], F32R))

        ((_, wm), (kt, vt, qt, ot, kvb, rr, bor, colrow), (sg, pr, ab, Wd, crow, sqj, ct),
         (hh, mx, fl, ad)) = shared([over_pro, over_a, over_b, over_d])
        hold3 = sb("hold3", [P, 9232])

        wkv = W1a[:, :].rearrange("p (s c n) -> p s c n", s=2, c=NC)
        wq = W1b[:, 0:2048].rearrange("p (s c n) -> p s c n", s=2, c=NC)
        wo = W1b[:, 2048:4096].rearrange("p (s c n) -> p s c n", s=2, c=2)
        gu = W2[:, :].rearrange("p (i s u c n) -> p i s u c n", i=2, s=2, u=2, c=NC)
        M = W1b[:, :].rearrange("p (s c n) -> p s c n", s=2, c=NC)
        gud = [w[:, :].rearrange("p (r s u c n) -> p r s u c n", r=2, s=2, u=2, c=NC) for w in (W1a, W1b)]
        wdd = W2[:, :].rearrange("p (s r n) -> p s r n", s=2, r=4)
        yn = [ct[:, 0, :], ct[:, 1, :], sg[:, 0, :], sg[:, 1, :]]

        def xn_of(k, b):
            if k == 2 and b >= 2:
                return xw[:, b - 2, :, :]
            return xn

        SIGN, ROW_A, GATE1, ROW_B = range(4)
        ROW_OF = [ROW_A, None, None, ROW_B, GATE1, ROW_A, ROW_B, None, None, ROW_A]
        FREED_BY = {R_Q1: R_GA0, R_P1: R_GB0, R_GB1: R_Q1}
        mod_row = [colrow[:, :] if r is None else prow[:, r, :] for r in ROW_OF]
        cin = xn[:, 0:2, :].rearrange("p t n -> p (t n)")[:, 0:5 * 8 * DS] \
            .rearrange("p (k i s) -> p k i s", k=5, i=8)
        ab4 = xn

        bank = [ctx.enter_context(nc.psum_tensor(f"bank{i}", [P, 512], F32)) for i in range(8)]
        TAIL = bank[2:4]
        YB = [0, 1, 4, 5, 6, 7]

        x_in_s = [sem(f"x_loaded{b}") for b in range(NB)]
        c_loaded = sem("c_loaded")
        coef_loaded = sem("coef_loaded")
        bo_loaded = sem("bo_loaded")
        wm_loaded = [sem(f"wmod_loaded{i}") for i in range(2)]
        mw_loaded = sem("wmod_part_loaded")
        nw_loaded = sem("norm_w_loaded")
        gw_loaded = sem("router_weights_loaded")
        zeroed = sem("identity_zeroed")
        silu_c = sem("silu_c_done")
        mrow_full = sem("first_mod_rows_full")
        mrow_copied = sem("first_mod_rows_copied")
        col_full = sem("mod_columns_full")
        col_done = sem("mod_columns_done")
        mod_chain = sem("mod_row_chain")
        row_stored = [sem(f"mod_row_stored{i}") for i in range(6)]
        const_ready = sem("constants_ready")
        gw_hi_s = sem("router_weights_hi")
        gw_ready = sem("router_weights_ready")
        aconst = sem("stage_a_constants")
        pchain = sem("prologue_chain")
        stage_full = [sem(f"stage_full{i}") for i in range(2)]
        split_hi = sem("split_hi")
        split_done = sem("split_done")
        row_full = [sem(f"row_full{i}") for i in range(2)]
        crow_full = [sem(f"crow_full{i}") for i in range(3)]
        ring_full = sem("ring_full")
        ring_read = sem("ring_read")
        ring_done = sem("ring_done")
        ln_chain = sem("ln_chain")
        xn_ready = sem("xn_ready")
        h_hi = sem("h_hi")
        pq_mul = sem("pq_mul")
        pq_sum = sem("pq_sum")
        pq_add = sem("pq_added")
        pj_full = sem("a_proj_full")
        pj_hi = sem("a_proj_hi")
        pj_lo = sem("a_proj_lo")
        kvmm = sem("a_kv_accumulated")
        kvb_hi = sem("a_kvb_hi")
        kvb_lo = sem("a_kvb_lo")
        nn_full = sem("a_norm_num_full")
        r_max = sem("a_norm_clipped")
        r_rec = sem("a_norm_inverted")
        o_num = sem("a_out_normalised")
        o_hi = sem("a_out_hi")
        o_lo = sem("a_out_lo")
        bo_add = sem("a_bias_added")
        bg_full = sem("b_gate_full")
        bu_full = sem("b_up_full")
        b_silu = sem("b_silu_done")
        b_p = sem("b_product_done")
        b_hi = sem("b_act_hi")
        b_lo = sem("b_act_lo")
        rwe_done = sem("b_rwe_done")
        m_loaded = [sem(f"m_loaded{i}") for i in range(4)]
        m_scaled = sem("m_scaled")
        m_used = sem("m_used")
        m_hi = sem("m_hi")
        m_lo = sem("m_lo")
        rt_chain = sem("router_chain")
        rt_sub = sem("router_shifted")
        rt_exp = sem("router_exp")
        y_full = sem("c_y_full")
        y_sq = sem("c_y_squared")
        y_read = sem("c_y_read")
        c_add = sem("c_x_added")
        dg_full = sem("d_gate_full")
        du_full = sem("d_up_full")
        d_silu = sem("d_silu_done")
        d_h = sem("d_h_done")
        d_abs = sem("d_abs_done")
        d_sp = sem("d_sparsify_chain")
        d_hi = sem("d_act_hi")
        d_lo = sem("d_act_lo")
        out_stored = sem("out_stored")

        block = ctx.enter_context(nc.Block())
        NSP = 17

        @block.sync
        def _(sp):
            sp.dma_start(cTs[:, :, :, :], cT).then_inc(c_loaded, 16)

            def mod_load(i):
                if i > 0:
                    sp.wait_ge(ring_full, RING[("mod", i - 1, "row")] + 1)
                layer, part = MOD_PARTS[i]
                sp.dma_start(mw[:, :], (wmod0, wmod1)[layer][part]).then_inc(mw_loaded, 16)

            def raw(n, j, src, size):
                if not (isinstance(n, int) and n < 2):
                    sp.wait_ge(split_done, n - 1)
                sp.dma_start(stage[:, j % 2, 0:size], src).then_inc(stage_full[j % 2], 16)

            def wa_slice(g, j):
                raw(g * NSA + j, j, wa[bass.ds(g, 1), :, j, :].rearrange("a p n -> p (a n)"), 1024)

            def wb_slice(e, j):
                n = e * NSB + (BASE_B + j)
                off, size = ((0, 1024), (1024, 1024), (2048, 512), (2560, 512))[j]
                raw(n, j, wbe[bass.ds(e, 1), :, off:off + size].rearrange("a p n -> p (a n)"), size)

            def wd_slice(g, j):
                raw(g * NSD + (BASE_D + j), j, wdn[bass.ds(g, 1), :, j, :].rearrange("a p n -> p (a n)"), 1024)

            def pro():
                for part in (SA, CA):
                    sp.dma_start(wm[:, part, :], wmod0[part]).then_inc(wm_loaded[part], 16)
                wa_slice(0, 0)
                wa_slice(0, 1)
                mod_load(0)
                wa_slice(0, 2)
                wa_slice(0, 3)
                sp.dma_start(bor[:, :], bo.partition_broadcast(P)).then_inc(bo_loaded, 16)

            def step_a(g, b):
                first = isinstance(g, int) and g == 0
                if b == 2 and not (isinstance(g, int) and g == GA - 1):
                    wa_slice(g + 1, 0)
                    wa_slice(g + 1, 1)
                if first:
                    for i in ((1, 2, 3), (4, 5), (6, 7, 8), (9,))[b]:
                        mod_load(i)
                    if b == 3:
                        sp.wait_ge(ring_full, ln_end(0, 3))
                        sp.dma_start(cin, coef).then_inc(coef_loaded, 16)
                if (b == 3 if first else b == 2) and not (isinstance(g, int) and g == GA - 1):
                    wa_slice(g + 1, 2)
                if b == 0 and not first:
                    wa_slice(g, 3)
                if b == 2 and isinstance(g, int) and g == GA - 1:
                    wb_slice(0, 0)
                    wb_slice(0, 1)

            def m_load(n):
                if n >= 4:
                    sp.wait_ge(m_used, n - 3)
                else:
                    sp.wait_ge(pj_full, 6 * NB * GA)
                sp.dma_start(mstage[:, n % 4, :], winout[n % 8]).then_inc(m_loaded[n % 4], 16)

            def step_b(e, b):
                if b == 0:
                    wb_slice(e, 2)
                    wb_slice(e, 3)
                if isinstance(e, int) and e == 0:
                    for n in range(4 * b, 4 * b + 4):
                        m_load(n)
                if b == 2 and not (isinstance(e, int) and e == GE - 1):
                    wb_slice(e + 1, 0)
                    wb_slice(e + 1, 1)
                if b == 3 and isinstance(e, int) and e == GE - 1:
                    wd_slice(0, 0)
                    wd_slice(0, 1)

            def step_c(b):
                if b == 3:
                    wd_slice(0, 2)
                    wd_slice(0, 3)

            def step_d(g, b):
                if b == 0:
                    wd_slice(g, 4)
                    wd_slice(g, 5)
                if b == 2 and not (isinstance(g, int) and g == GD - 1):
                    for j in range(4):
                        wd_slice(g + 1, j)
                if isinstance(g, int) and g == GD - 1 and b >= 1:
                    store(b - 1)

            def store(b):
                sp.wait_ge(ring_done, RING[("tail", "D", GD - 1, b)] + NT)
                sp.dma_start(out[b].rearrange("(t p) n -> p t n", p=P),
                             x[:, b * NT:(b + 1) * NT, :]).then_inc(out_stored, 16)

            def epi():
                store(3)
                sp.wait_ge(out_stored, 16 * NB)
                for stored in row_stored:
                    sp.wait_ge(stored, 16)

            walk(sp, pro, step_a, step_b, step_c, step_d, epi)

        @block.tensor
        def _(pe):
            def mm3(o, lhs, rhs, start, stop, **kw):
                pe.matmul(o, lhs(HI), rhs(HI), start=start, stop=False, **kw)
                pe.matmul(o, lhs(HI), rhs(LO), start=False, stop=False, **kw)
                return pe.matmul(o, lhs(LO), rhs(HI), start=False, stop=stop, **kw)

            def hcol(c, b, t):
                return lambda s: hT[:, s, c, b * S + t * P:b * S + (t + 1) * P]

            def hrow(c, b):
                return lambda s: hT[:, s, c, b * S:(b + 1) * S]

            def ring_slot(n, par):
                if not (isinstance(n, int) and n < 2):
                    pe.wait_ge(ring_read, n - 1)
                return TAIL[par]

            def par_of(stage, g, b, t):
                base = RING[("tail", stage, g if isinstance(g, int) else 1, b)]
                return (base + t) % 2

            def ln_transposes(ln, half):
                if ln is None:
                    return
                k, b = ln
                if half == 0:
                    pe.wait_ge(xn_ready, ln_index(k, b) + 1)
                for i in range(2):
                    n, c = RING[("ln", k, b, half)] + i, 2 * half + i
                    o = ring_slot(n, n % 2)
                    for t in range(NT):
                        last = pe.transpose(o[:, t * P:(t + 1) * P], xn_of(k, b)[:, t, c * P:(c + 1) * P], ident[:, :])
                    last.then_inc(ring_full, 1)

            def need_h(k, b):
                pe.wait_ge(ring_done, ln_end(k, b))

            def router(b):
                n = RING[("rt", b)]
                need_h(1, b)
                pe.wait_ge(gw_ready, 1)
                o = ring_slot(n, n % 2)
                for t in range(NT):
                    for c in range(NC):
                        last = mm3(o[:, t * 8:(t + 1) * 8], hcol(c, b, t), lambda s, c=c: gw[:, s, c, :],
                                   c == 0, c == NC - 1)
                last.then_inc(ring_full, 1)

            def extras(stage_, g, b):
                rt = routed(stage_, g, b)
                if rt is not None:
                    router(rt)

            def mod_product(o, w, layer):
                for c in range(NC):
                    last = pe.matmul(o[0:NB, :], scT[:, layer, c, :], w[:, c * H:(c + 1) * H],
                                     start=c == 0, stop=c == NC - 1)
                return last

            def mod_columns(o, r):
                for m in range(NC):
                    last = pe.transpose(o[:, m * NB:(m + 1) * NB], r[:, m * P:(m + 1) * P], ident[0:NB, 0:NB])
                return last

            def mod_products(g, b, place):
                for i, use in mod_uses(g, b, place):
                    n = RING[("mod", i, use)]
                    if use == "row":
                        pe.wait_ge(mw_loaded, 16 * (i + 1))
                    else:
                        pe.wait_ge(ring_read, RING[("mod", i, "row")] + 1)
                    o = ring_slot(n, n % 2)
                    last = mod_columns(o, mod_row[i]) if use == "col" else mod_product(o, mw, MOD_PARTS[i][0])
                    last.then_inc(ring_full, 1)

            def warm_up(count):
                for _ in range(count):
                    pe.transpose(bank[4][:, 0:P], ident[:, :], ident[:, :])

            def pro():
                pe.wait_ge(const_ready, 1)
                warm_up(36)
                pe.wait_ge(silu_c, 1)
                for part in (SA, CA):
                    pe.wait_ge(wm_loaded[part], 16)
                    mod_product(bank[part], wm[:, part, :], 0).then_inc(mrow_full, 1)
                for part in (SA, CA):
                    pe.wait_ge(mrow_copied, part + 1)
                    mod_columns(bank[6 + part], prow[:, part, :]).then_inc(col_full, 1)
                ln_transposes((0, 0), 0)
                ln_transposes((0, 0), 1)

            def tail_a(g, b, n0):
                s = g * NB + b
                pe.wait_ge(o_lo, s * 2 + 2)
                if b == 0:
                    pe.wait_ge(split_done, g * NSA + 4)
                for t in range(NT):
                    o = ring_slot(n0 + t, par_of("A", g, b, t))
                    for c in range(2):
                        last = mm3(o[:, :], lambda h, c=c: ot[:, h, c, t * P:(t + 1) * P],
                                   lambda h, c=c: wo[:, h, c, :], c == 0, c == 1)
                    last.then_inc(ring_full, 1)

            def tails(stage_, g, b):
                tail = tail_of(stage_, g, b)
                if tail is None:
                    return
                n0 = ring_before(stage_, g, b)
                {"A": tail_a, "B": tail_b, "D": tail_d}[tail[0]](tail[1], tail[2], n0)

            def step_a(g, b):
                s = g * NB + b
                first = isinstance(g, int) and g == 0
                ln = layernorms("A", g, b)
                if first:
                    need_h(0, b)
                    if b == 0:
                        pe.wait_ge(aconst, 1)
                if b == 0:
                    pe.wait_ge(split_done, g * NSA + 2)

                def accumulate(t):
                    pe.wait_ge(pj_lo, s * 6 + (t + 1))
                    if t == 0 and not (first and b == 0):
                        pe.wait_ge(r_max, s * 2)
                    for pair in range(2):
                        last = mm3(bank[4][:, pair * VW:(pair + 1) * VW],
                                   lambda h: kt[:, t % 2, h, pair * P:(pair + 1) * P],
                                   lambda h: vt[:, t % 2, h, pair, :],
                                   t == 0 and pair == 0, t == NT - 1, skip_group_check=True)
                    last.then_inc(kvmm, 1)

                for t in range(NT):
                    if not (first and b == 0 and t < 2):
                        pe.wait_ge(pj_lo, s * 6 + (t - 1))
                    for c in range(NC):
                        last = mm3(bank[t % 2][:, :], hcol(c, b, t), lambda h, c=c: wkv[:, h, c, :],
                                   c == 0, c == NC - 1)
                    last.then_inc(pj_full, 1)
                    if t > 0:
                        accumulate(t - 1)
                    if t in (0, 2):
                        mod_products(g, b, t // 2)
                if b == 0:
                    pe.wait_ge(split_done, g * NSA + 3)
                for pair in range(2):
                    pe.wait_ge(pj_lo, s * 6 + (3 + pair))
                    for c in range(NC):
                        last = mm3(bank[pair][:, :], lambda h, c=c: wq[:, h, c, pair * P:(pair + 1) * P],
                                   hrow(c, b), c == 0, c == NC - 1)
                    last.then_inc(pj_full, 1)
                    if pair == 0:
                        accumulate(NT - 1)
                    if first:
                        ln_transposes(ln, pair)
                if not first:
                    ln_transposes(ln, 0)
                mod_products(g, b, 2)
                tails("A", g, b)
                if not first:
                    ln_transposes(ln, 1)
                pe.wait_ge(pj_lo, s * 6 + 6)
                pe.wait_ge(kvb_lo, s + 1)
                for kind, banks in ((1, (5, 4)), (0, (6, 7))):
                    for pair in range(2):
                        mm3(bank[banks[pair]][:, :], lambda h: kvb[:, h, pair, kind, :],
                            lambda h: qt[:, h, pair, :], True, True).then_inc(nn_full, 1)
                extras("A", g, b)

            def tail_b(e, b, n0):
                s = e * NB + b
                pe.wait_ge(b_lo, s * 2 + 2)
                if b == 0:
                    pe.wait_ge(split_done, e * NSB + (BASE_B + 4))
                for t in range(NT):
                    o = ring_slot(n0 + t, par_of("B", e, b, t))
                    for i in range(2):
                        last = mm3(o[:, :], lambda h, i=i: ab[:, h, i, t * P:(t + 1) * P],
                                   lambda h, i=i: Wd[:, h, i, :], i == 0, i == 1)
                    last.then_inc(ring_full, 1)

            def step_b(e, b):
                s = e * NB + b
                first = isinstance(e, int) and e == 0
                if first:
                    need_h(1, b)
                for i in range(2):
                    if b == 0:
                        pe.wait_ge(split_done, e * NSB + (BASE_B + i + 1))
                    if first and b == 0:
                        pe.wait_ge(pj_lo, 6 * NB * GA)
                        pe.wait_ge(r_max, 2 * NB * GA)
                    else:
                        pe.wait_ge(b_p, s * 2 + (i - 1))
                    for u, o, full in ((0, bank[i], bg_full), (1, bank[4 + i], bu_full)):
                        for c in range(NC):
                            last = mm3(o[:, :], lambda h, c=c: gu[:, i, h, u, c, :], hrow(c, b),
                                       c == 0, c == NC - 1)
                        last.then_inc(full, 1)
                ln = layernorms("B", e, b)
                ln_transposes(ln, 0)
                tails("B", e, b)
                ln_transposes(ln, 1)
                extras("B", e, b)
                if first:
                    for n in range(4 * b, 4 * b + 4):
                        half, ic = n // 8, n % 8
                        pe.wait_ge(m_scaled, n + 1)
                        if n == 0:
                            pe.wait_ge(o_lo, 2 * NB * GA)
                        if n == 8:
                            pe.wait_ge(m_lo, 2)
                        for j in range(2):
                            m = 2 * half + j
                            last = pe.matmul(bank[6 + j][:, :], mstage[:, n % 4, m * P:(m + 1) * P],
                                             mstage[:, n % 4, 512:1024], start=ic == 0, stop=ic == 7)
                        last.then_inc(m_used, 1)
            def step_c(b):
                need_h(2, b)
                if b == 0:
                    pe.wait_ge(m_lo, 4)
                    pe.wait_ge(b_p, 2 * NB * GE)
                tails("C", 0, b)
                for t in range(NT):
                    n = NT * b + t
                    if n >= 6:
                        pe.wait_ge(y_read, n - 5)
                    for c in range(NC):
                        last = mm3(bank[YB[n % 6]][:, :], hcol(c, b, t), lambda h, c=c: M[:, h, c, :],
                                   c == 0, c == NC - 1)
                    last.then_inc(y_full, 1)
                for half in range(2):
                    ln_transposes(layernorms("C", 0, b), half)

            def tail_d(g, b, n0):
                s = g * NB + b
                pe.wait_ge(d_lo, s * 4 + 4)
                if b == 0:
                    pe.wait_ge(split_done, g * NSD + (BASE_D + 6))
                for t in range(NT):
                    o = ring_slot(n0 + t, par_of("D", g, b, t))
                    for r in range(4):
                        last = mm3(o[:, :], lambda h, r=r: ad[:, r, h, t * P:(t + 1) * P],
                                   lambda h, r=r: wdd[:, h, r, :], r == 0, r == 3)
                    last.then_inc(ring_full, 1)

            def step_d(g, b):
                s = g * NB + b
                first = isinstance(g, int) and g == 0
                if first:
                    need_h(3, b)
                if first and b == 0:
                    pe.wait_ge(y_read, NT * NB)
                for r in range(4):
                    if b == 0:
                        pe.wait_ge(split_done, g * NSD + (BASE_D + r + 1))
                    if not (first and b == 0 and r < 2):
                        pe.wait_ge(d_h, s * 4 + (r - 1))
                    for u, o, full in ((0, bank[r % 2], dg_full), (1, bank[4 + r % 2], du_full)):
                        for c in range(NC):
                            last = mm3(o[:, :], lambda h, c=c: gud[r // 2][:, r % 2, h, u, c, :], hrow(c, b),
                                       c == 0, c == NC - 1)
                        last.then_inc(full, 1)
                    if b == 0 and r in (1, 2):
                        ln_transposes(layernorms("D", g, b), r - 1)
                if b > 0:
                    ln_transposes(layernorms("D", g, b), 0)
                    ln_transposes(layernorms("D", g, b), 1)
                tails("D", g, b)

            def epi():
                tail_d(GD - 1, 3, RING[("tail", "D", GD - 1, 3)])

            walk(pe, pro, step_a, step_b, step_c, step_d, epi)

        @block.scalar
        def _(act):
            def load_row(stage_, g, b):
                kind = {"A": R_GA0, "B": R_GB0, "D": R_GB1}[stage_]
                if isinstance(g, int) and g == 0 and b == 0:
                    act.wait_ge(row_stored[kind], 16)
                if stage_ == "A" and isinstance(g, int) and g == 0:
                    if b >= 2:
                        act.wait_ge(ring_read, RING[("tail", "A", 0, b - 2)] + NT)
                elif isinstance(g, int) and g == 0 and b < 2:
                    prev = {"B": ("A", GA - 1), "D": ("B", GE - 1)}[stage_]
                    act.wait_ge(ring_read, RING[("tail", *prev, b + 2)] + NT)
                elif b >= 2:
                    act.wait_ge(ring_read, ring_at(stage_, g, b - 2) + NT)
                elif isinstance(g, int):
                    act.wait_ge(ring_read, RING[("tail", stage_, g - 1, b + 2)] + NT)
                else:
                    act.wait_ge(ring_read, g * (NB * NT) + (RING[("tail", stage_, 1, b + 2)] - 2 * NB * NT + NT))
                act.dma_start(row[:, b % 2, :], rows_d[kind, b, :].partition_broadcast(P)) \
                    .then_inc(row_full[b % 2], 16)

            def wsplit(count, j, dst, size):
                act.wait_ge(stage_full[j % 2], count)
                act.activation(dst, stage[:, j % 2, 0:size], ACT.Copy).then_inc(split_hi, 1)

            def split_a(g, j):
                dst = (W1a[:, 0:1024], W1a[:, 1024:2048], W1b[:, 0:1024], W1b[:, 2048:3072])[j]
                wsplit(g * 32 + 16 * (j // 2 + 1), j, dst, 1024)

            def split_b(e, j):
                dst = (W2[:, 0:1024], W2[:, 2048:3072], Wd[:, HI, 0, :], Wd[:, HI, 1, :])[j]
                wsplit(e * 32 + (8 * BASE_B + 16 * (j // 2 + 1)), j, dst, (1024, 1024, 512, 512)[j])

            def split_d(g, j):
                w = (W1a, W1a, W1b, W1b)[j] if j < 4 else None
                dst = w[:, (j % 2) * 2048:(j % 2) * 2048 + 1024] if j < 4 else \
                    W2[:, (j - 4) * 1024:(j - 3) * 1024]
                wsplit(g * 48 + (8 * BASE_D + 16 * (j // 2 + 1)), j, dst, 1024)

            def ln_out(ln, half):
                if ln is None:
                    return
                k, b = ln
                n0 = RING[("ln", k, b, half)]
                if k == 0:
                    act.wait_ge(col_done, 2)
                elif k == 1:
                    act.wait_ge(ring_done, RING[("mod", 8, "col")] + 1)
                if n0 > 0:
                    act.wait_ge(ring_read, n0)
                for i in range(2):
                    n, c = n0 + i, 2 * half + i
                    act.wait_ge(ring_full, n + 1)
                    if n >= 2:
                        act.wait_ge(ring_done, n - 1)
                    act.activation(tmp[:, n % 2, :], TAIL[n % 2][:, :], ACT.Identity,
                                   scale=modc[:, k, 1, c, b:b + 1], bias=modc[:, k, 0, c, b:b + 1]) \
                        .then_inc(ring_read, 1)
                    act.wait_ge(ring_read, n + 1)
                    act.activation(hT[:, HI, c, b * S:(b + 1) * S], tmp[:, n % 2, :], ACT.Copy) \
                        .then_inc(h_hi, 1)

            def router(b):
                act.wait_ge(rt_sub, b + 1)
                act.activation(pe8[:, :, :], lg[:, :, :], ACT.Exp).then_inc(rt_exp, 1)

            def extras(stage_, g, b):
                rt = routed(stage_, g, b)
                if rt is not None:
                    router(rt)

            def load_x(b):
                act.dma_start(x[:, b * NT:(b + 1) * NT, :], x_in[b].rearrange("(t p) n -> p t n", p=P)) \
                    .then_inc(x_in_s[b], 16)

            def pro():
                load_x(0)
                act.wait_ge(c_loaded, 16)
                act.activation(scT[:, :, :, :], cTs[:, :, :, :], ACT.Silu).then_inc(silu_c, 1)
                split_a(0, 0)
                split_a(0, 1)
                ln_out((0, 0), 0)
                ln_out((0, 0), 1)
                load_x(1)
                for j in range(2, NSA):
                    split_a(0, j)
                load_x(2)
                load_x(3)

            def crows(which, b):
                if b == 0:
                    act.wait_ge(row_stored[R_P1 + which], 16)
                elif which < 2:
                    act.wait_ge(pq_sum, NT * b)
                else:
                    act.wait_ge(y_read, NT * b)
                act.dma_start(crow[:, which, :], rows_d[R_P1 + which, b, :].partition_broadcast(P)) \
                    .then_inc(crow_full[which], 16)

            def gated_rows(stage_, g, b):
                if stage_ == "B" and gated_in("B", g, b) is not None:
                    crows(0, gated_in("B", g, b))
                    crows(1, gated_in("B", g, b))
                if stage_ == "C" and b in (0, 3):
                    crows(0, 2 + b // 3)
                    crows(1, 2 + b // 3)

            def out_hi(s, pair):
                act.wait_ge(o_num, s * 2 + (pair - 1))
                act.activation(ot[:, HI, pair, :], bank[6 + pair][:, :], ACT.Copy).then_inc(o_hi, 1)

            def step_a(g, b):
                s = g * NB + b
                first = isinstance(g, int) and g == 0
                last = isinstance(g, int) and g == GA - 1
                ln = layernorms("A", g, b)
                if not (first and b < 2):
                    load_row("A", g, b)
                for t in range(NT):
                    act.wait_ge(pj_full, s * 6 + (t + 1))
                    if not (first and b == 0 and t < 2):
                        act.wait_ge(kvmm, s * 4 + (t - 1))
                    act.activation(kt[:, t % 2, HI, :], bank[t % 2][:, 0:256], ACT.Relu)
                    act.activation(vt[:, t % 2, HI, :, 0:P],
                                   bank[t % 2][:, 256:512].rearrange("p (a n) -> p a n", a=2), ACT.Copy) \
                        .then_inc(pj_hi, 1)
                if b == 3 and not last:
                    split_a(g + 1, 0)
                    split_a(g + 1, 1)
                if b == 3 and last:
                    for stored in row_stored:
                        act.wait_ge(stored, 16)
                    split_b(0, 0)
                    split_b(0, 1)
                if first and b == 1:
                    load_row("A", g, 0)
                    load_row("A", g, 1)
                if tail_of("A", g, b):
                    out_hi(s, 0)
                    out_hi(s, 1)
                for pair in range(2):
                    act.wait_ge(pj_full, s * 6 + (5 + pair))
                    if pair == 0 and not (first and b == 0):
                        act.wait_ge(nn_full, s * 4)
                    act.activation(qt[:, HI, pair, :], bank[pair][:, :], ACT.Relu).then_inc(pj_hi, 1)
                    if first:
                        ln_out(ln, pair)
                if not first:
                    ln_out(ln, 0)
                act.wait_ge(kvmm, s * 4 + 4)
                if first and b == 0:
                    act.wait_ge(aconst, 1)
                kv = bank[4][:, 0:2 * VW].rearrange("p (a n) -> p a n", a=2)
                for lo in (0, HD):
                    q = slice(lo, lo + HD)
                    act.activation(kvb[q, HI, :, 0, q], kv[q, :, q], ACT.Copy)
                    ins = act.activation(kvb[q, HI, :, 1, q], kv[q, :, P:P + 1].to_broadcast([HD, 2, HD]), ACT.Copy)
                ins.then_inc(kvb_hi, 1)
                if not first:
                    ln_out(ln, 1)
                if b == 3 and not last:
                    split_a(g + 1, 2)
                if b == 0 and not first:
                    act.wait_ge(ring_full, ring_before("A", g, b) + NT)
                    split_a(g, 3)

            def step_b(e, b):
                s = e * NB + b
                first = isinstance(e, int) and e == 0
                load_row("B", e, b)
                if first and b == 0:
                    for pair in range(2):
                        out_hi(NB * GA, pair)
                    act.wait_ge(kvmm, NT * NB * GA)
                for i in range(2):
                    act.wait_ge(bg_full, s * 2 + (i + 1))
                    if not (first and b == 0):
                        act.wait_ge(b_p, s * 2 + (i - 1))
                    act.activation(sg[:, i, :], bank[i][:, :], ACT.Silu).then_inc(b_silu, 1)
                    if b == 3 and not (isinstance(e, int) and e == GE - 1):
                        act.wait_ge(bu_full, s * 2 + (i + 1))
                        split_b(e + 1, i)
                gated_rows("B", e, b)
                if first:
                    for n in range(4 * b, 4 * b + 4):
                        act.wait_ge(m_loaded[n % 4], 16 * (n // 4 + 1))
                        act.activation(mstage[:, n % 4, 512:1024], mstage[:, n % 4, 512:1024], ACT.Copy,
                                       scale=kcoef[:, n % 8:n % 8 + 1]).then_inc(m_scaled, 1)
                ln = layernorms("B", e, b)
                ln_out(ln, 0)
                if tail_of("B", e, b):
                    act.wait_ge(ring_full, ring_before("B", e, b) + NT)
                for i in range(2):
                    act.wait_ge(b_p, s * 2 + (i + 1))
                    act.activation(ab[:, HI, i, :], pr[:, i, :], ACT.Copy).then_inc(b_hi, 1)
                if b == 0:
                    split_b(e, 2)
                    split_b(e, 3)
                ln_out(ln, 1)
                extras("B", e, b)
                if first and b in (1, 3):
                    for j in range(2):
                        m = (b - 1) + j
                        act.wait_ge(m_used, 8 * (m // 2 + 1))
                        act.activation(M[:, HI, m, :], bank[6 + j][:, :], ACT.Copy).then_inc(m_hi, 1)

            def step_c(b):
                gated_rows("C", 0, b)
                crows(2, b)
                for t in range(NT):
                    n = NT * b + t
                    act.wait_ge(y_full, n + 1)
                    if t == 0 and b > 0:
                        act.wait_ge(y_read, NT * b)
                    if n > 0:
                        act.wait_ge(y_sq, n)
                    act.activation(sqj[:, :], bank[YB[n % 6]][:, :], ACT.Square,
                                   accum_out=ssum[:, t:t + 1]).then_inc(y_sq, 1)
                ln_out(layernorms("C", 0, b), 0)
                ln_out(layernorms("C", 0, b), 1)
                if b < 2:
                    if b == 0:
                        act.wait_ge(m_lo, 4)
                    split_d(0, b)

            def step_d(g, b):
                s = g * NB + b
                first = isinstance(g, int) and g == 0
                ln = layernorms("D", g, b)
                load_row("D", g, b)

                def absolute(r):
                    act.wait_ge(d_h, s * 4 + (r + 1))
                    if r == 0:
                        if ln:
                            act.wait_ge(ring_full, ln_end(*ln))
                        if not (first and b == 0):
                            act.wait_ge(d_sp, s * NSP)
                    act.activation(ab4[:, r, :], hh[:, r, :], ACT.Abs).then_inc(d_abs, 1)

                if first and b == 0:
                    act.wait_ge(y_full, NT * NB)
                    split_d(0, 2)
                    split_d(0, 3)
                for r in range(4):
                    act.wait_ge(dg_full, s * 4 + (r + 1))
                    if first and b == 0 and r == 0:
                        act.wait_ge(ring_done, RING[("tail", "B", GE - 1, 3)] + NT)
                    if not (first and b == 0):
                        act.wait_ge(d_lo, s * 4 + (r - 3))
                    act.activation(hh[:, r, :], bank[r % 2][:, :], ACT.Silu).then_inc(d_silu, 1)
                    if b == 3 and not (isinstance(g, int) and g == GD - 1):
                        act.wait_ge(du_full, s * 4 + (r + 1))
                        split_d(g + 1, r)
                    if b == 0 and r in (1, 2):
                        ln_out(ln, r - 1)
                    if not ln and r > 0:
                        absolute(r - 1)
                if ln and b > 0:
                    ln_out(ln, 0)
                    ln_out(ln, 1)
                for r in range(4) if ln else (3,):
                    absolute(r)
                if tail_of("D", g, b):
                    act.wait_ge(ring_full, ring_before("D", g, b) + NT)
                if first and b == 0:
                    act.wait_ge(c_add, NT * NB)
                for r in range(4):
                    act.wait_ge(d_sp, s * NSP + (NSP - 3 + r))
                    act.activation(ad[:, r, HI, :], hh[:, r, :], ACT.Copy).then_inc(d_hi, 1)
                if b == 0:
                    if first:
                        act.wait_ge(pq_add, NT * NB)
                    split_d(g, 4)
                    split_d(g, 5)

            walk(act, pro, step_a, step_b, step_c, step_d, lambda: None)

        @block.vector
        def _(dve):
            def link(ins, sem_, count):
                ins.then_inc(sem_, 1)
                dve.wait_ge(sem_, count)

            chain = {"ln": 0, "p": 0, "rt": 0}

            def seq(ins, which):
                chain[which] += 1
                link(ins, {"ln": ln_chain, "p": pchain, "rt": rt_chain}[which], chain[which])

            def take(n, par, after_act=False):
                if after_act:
                    dve.wait_ge(ring_read, n)
                dve.wait_ge(ring_full, n + 1)
                if not (isinstance(n, int) and n < 2):
                    dve.wait_ge(ring_done, n - 1)

            def inv_sqrt():
                seq(dve.tensor_scalar(rstd[:, :].bitcast(I32), ve[:, :].bitcast(I32), -0.5, MAGIC,
                                      ALU.mult, ALU.add), "ln")
                for _ in range(3):
                    seq(dve.tensor_tensor(na[:, :], ve[:, :], rstd[:, :], ALU.mult), "ln")
                    seq(dve.scalar_tensor_tensor(out=na[:, :], in0=na[:, :], scalar=-0.5, in1=rstd[:, :],
                                                 op0=ALU.mult, op1=ALU.mult), "ln")
                    seq(dve.scalar_tensor_tensor(out=rstd[:, :], in0=na[:, :], scalar=1.5, in1=rstd[:, :],
                                                 op0=ALU.add, op1=ALU.mult), "ln")

            def ln_stats(k, b, tiles):
                if 0 in tiles:
                    if k == 0:
                        dve.wait_ge(x_in_s[b], 16)
                    elif k == 3:
                        dve.wait_ge(c_add, NT * (b + 1))
                        dve.wait_ge(pq_add, NT * (b + 1))
                    else:
                        prev = {1: ("A", GA - 1), 2: ("B", GE - 1)}[k]
                        dve.wait_ge(ring_done, RING[("tail", *prev, b)] + NT)
                for t in tiles:
                    last = dve.bn_stats(st6[:, t, :], x[:, b * NT + t, :])
                seq(last, "ln")
                for t in tiles:
                    last = dve.bn_aggr(mv[:, t, :], st6[:, t, :])
                seq(last, "ln")

            def ln_rstd():
                seq(dve.tensor_scalar(ve[:, :], mv[:, :, 1], EPS, None, ALU.add), "ln")
                inv_sqrt()

            def ln_apply(k, b):
                n = ln_index(k, b)
                if n > 0:
                    dve.wait_ge(ring_full, ln_end((n - 1) // NB, (n - 1) % NB))
                if (k, b) in ((2, 1), (3, 0)):
                    dve.wait_ge(pq_add, NT * (b if b else 2))
                for t in range(NT):
                    last = dve.tensor_scalar(xn_of(k, b)[:, t, :], x[:, b * NT + t, :], mv[:, t, 0:1], rstd[:, t:t + 1],
                                             ALU.subtract, ALU.mult)
                last.then_inc(xn_ready, 1)

            def gated(b):
                xg = xn_of(2, b)
                dve.wait_ge(ring_full, ln_end(2, b))
                dve.wait_ge(crow_full[0], 16 * (b + 1))
                dve.wait_ge(crow_full[1], 16 * (b + 1))
                for t in range(NT):
                    dve.tensor_tensor(xg[:, t, :], xg[:, t, :], crow[:, 0, :], ALU.mult).then_inc(pq_mul, 1)
                for t in range(NT):
                    dve.wait_ge(pq_mul, NT * b + t + 1)
                    dve.tensor_tensor(xg[:, t, :], xg[:, t, :], crow[:, 1, :], ALU.add).then_inc(pq_sum, 1)

            def router(b):
                n = RING[("rt", b)]
                take(n, n % 2, True)
                dve.tensor_copy(tmp[:, n % 2, 0:NT * 8], TAIL[n % 2][:, 0:NT * 8]).then_inc(ring_read, 1)
                dve.wait_ge(ring_done, n + 1)
                seq(dve.tensor_reduce(m4[:, 0, :], lg[:, :, :], AX_X, ALU.max), "rt")
                dve.tensor_tensor(lg[:, :, :], lg[:, :, :], m4[:, 0, :].unsqueeze(2).to_broadcast([P, NT, 8]),
                                  ALU.subtract).then_inc(rt_sub, 1)
                dve.wait_ge(rt_exp, b + 1)
                seq(dve.tensor_reduce(m4[:, 0, :], pe8[:, :, :], AX_X, ALU.add), "rt")
                seq(dve.reciprocal(m4[:, 1, :], m4[:, 0, :]), "rt")
                seq(dve.tensor_tensor(pe8[:, :, :], pe8[:, :, :], m4[:, 1, :].unsqueeze(2).to_broadcast([P, NT, 8]),
                                      ALU.mult), "rt")
                for t in range(NT):
                    seq(dve.max(v8[:, t, :], pe8[:, t, :]), "rt")
                    seq(dve.max_index(i8[:, t, :], v8[:, t, :], pe8[:, t, :]), "rt")
                    for j in range(2):
                        seq(dve.tensor_scalar(sel[:, j, t, :], iota8[:, :], i8[:, t, j:j + 1], None,
                                              ALU.is_equal), "rt")
                seq(dve.tensor_tensor(m4[:, 0, :], v8[:, :, 0], v8[:, :, 1], ALU.add), "rt")
                seq(dve.reciprocal(m4[:, 1, :], m4[:, 0, :]), "rt")
                seq(dve.tensor_tensor(sel[:, 0, :, :], sel[:, 0, :, :], sel[:, 1, :, :], ALU.add), "rt")
                seq(dve.tensor_tensor(pe8[:, :, :], pe8[:, :, :], m4[:, 1, :].unsqueeze(2).to_broadcast([P, NT, 8]),
                                      ALU.mult), "rt")
                seq(dve.tensor_tensor(rw[:, b * NT:(b + 1) * NT, :], pe8[:, :, :], sel[:, 0, :, :], ALU.mult), "rt")

            def late(stage_, g, b):
                if gated_in(stage_, g, b) is not None:
                    gated(gated_in(stage_, g, b))
                rt = routed(stage_, g, b)
                if rt is not None:
                    router(rt)

            def pro():
                for e in range(8):
                    dve.memset(iota8[:, e:e + 1], float(e))
                dve.memset(kvb[:, :, :, :, :].bitcast(F32), 0.0)
                dve.memset(vt[:, :, HI, :, P:VW].bitcast(F32), 1.0)
                dve.memset(vt[:, :, LO, :, P:VW].bitcast(F32), 0.0).then_inc(aconst, 1)
                ln_stats(0, 0, range(NT))
                ln_rstd()
                ln_apply(0, 0)
                for part in (SA, CA):
                    dve.wait_ge(mrow_full, part + 1)
                    dve.tensor_copy(prow[:, part, :], bank[part][0:NB, :]).then_inc(mrow_copied, 1)
                for part in (SA, CA):
                    dve.wait_ge(col_full, part + 1)
                    dve.tensor_scalar(modc[:, 0, part, :, :],
                                      bank[6 + part][:, 0:16].rearrange("p (c b) -> p c b", c=NC),
                                      float(part), None, ALU.add).then_inc(col_done, 1)
                first_split(0)
                first_split(1)
                for c in range(NC):
                    dve.wait_ge(h_hi, c + 1)
                    dve.tensor_tensor(hT[:, LO, c, 0:S], tmp[:, c % 2, :], hT[:, HI, c, 0:S].bitcast(F32),
                                      ALU.subtract).then_inc(ring_done, 1)

            def first_split(j):
                dve.wait_ge(split_hi, j + 1)
                if j > 0:
                    dve.wait_ge(split_done, j)
                dve.tensor_tensor(W1a[:, 2048 + j * 1024:3072 + j * 1024], stage[:, j, :],
                                  W1a[:, j * 1024:(j + 1) * 1024].bitcast(F32), ALU.subtract) \
                    .then_inc(split_done, 1)

            def tuple_coefficients():
                dve.wait_ge(coef_loaded, 16)
                for j, other in ((1, 3), (2, 4)):
                    seq(dve.scalar_tensor_tensor(out=cin[:, j, :, :], in0=cin[:, 0, :, :], scalar=0.0,
                                                 in1=cin[:, j, :, :], op0=ALU.mult, op1=ALU.add), "p")
                    seq(dve.tensor_tensor(cin[:, j, :, :], cin[:, j, :, :], cin[:, other, :, :], ALU.mult), "p")
                seq(dve.tensor_tensor(cin[:, 1, :, :], cin[:, 1, :, :], cin[:, 2, :, :], ALU.subtract), "p")
                seq(dve.tensor_reduce(kcoef[:, :], cin[:, 1, :, :], AX_X, ALU.add), "p")

            def mod_evac(g, b, place):
                for i, use in mod_uses(g, b, place):
                    n = RING[("mod", i, use)]
                    if use == "col":
                        take(n, n % 2, True)
                        dve.tensor_copy(tmp[:, n % 2, 0:16], TAIL[n % 2][:, 0:16]).then_inc(ring_read, 1)
                        continue
                    before = FREED_BY.get(ROW_KIND.get(MOD_PARTS[i]))
                    if before is not None:
                        dve.wait_ge(row_stored[before], 16)
                    dve.wait_ge(ring_read, n)
                    dve.wait_ge(ring_full, n + 1)
                    dve.tensor_copy(mod_row[i], TAIL[n % 2][0:NB, :]).then_inc(ring_read, 1)

            def stats(ln, tiles):
                if ln:
                    ln_stats(*ln, tiles)
                    if NT - 1 in tiles:
                        ln_rstd()

            def tail_evac(stage_, g, b, t):
                tail = tail_of(stage_, g, b) if stage_ != "end" else ("D", GD - 1, 3)
                if tail is None:
                    return
                n0 = ring_before(stage_, g, b) if stage_ != "end" else RING[("tail", "D", GD - 1, 3)]
                ts, tg, tb = tail
                key = RING[("tail", ts, tg if isinstance(tg, int) else 1, tb)]
                par = (key + t) % 2
                if t == 0:
                    rn0 = {"A": 0, "B": NB * GA, "D": NB * (GA + GE)}[ts]
                    dve.wait_ge(row_full[tb % 2], tg * 32 + (8 * rn0 + 16 * (tb // 2 + 1)))
                take(n0 + t, par, t == 0)
                if ts == "B":
                    dve.scalar_tensor_tensor(out=tmp[:, par, :], in0=TAIL[par][:, :],
                                             scalar=rwe[:, tb * NT + t:tb * NT + t + 1], in1=row[:, tb % 2, :],
                                             op0=ALU.mult, op1=ALU.mult).then_inc(ring_read, 1)
                elif ts == "A" and isinstance(tg, int) and tg == GA - 1:
                    if t == 0 and tb == 0:
                        dve.wait_ge(bo_loaded, 16)
                    link(dve.tensor_tensor(tmp[:, par, :], TAIL[par][:, :], bor[:, :], ALU.add),
                         bo_add, tb * NT + t + 1)
                    dve.tensor_tensor(tmp[:, par, :], tmp[:, par, :], row[:, tb % 2, :], ALU.mult) \
                        .then_inc(ring_read, 1)
                else:
                    dve.tensor_tensor(tmp[:, par, :], TAIL[par][:, :], row[:, tb % 2, :], ALU.mult) \
                        .then_inc(ring_read, 1)

            def invert(s, pair):
                dve.wait_ge(r_max, s * 2 + (pair - 1))
                dve.reciprocal(rr[:, pair, :], rr[:, pair, :]).then_inc(r_rec, 1)

            def normalise(s, pair):
                dve.wait_ge(nn_full, s * 4 + (pair - 1))
                dve.wait_ge(r_rec, s * 2 + (pair - 1))
                dve.tensor_tensor(bank[6 + pair][:, :], bank[6 + pair][:, :], rr[:, pair, :], ALU.mult) \
                    .then_inc(o_num, 1)

            def out_lo(s, pair):
                dve.wait_ge(o_hi, s * 2 + (pair - 1))
                dve.tensor_tensor(ot[:, LO, pair, :], bank[6 + pair][:, :],
                                  ot[:, HI, pair, :].bitcast(F32), ALU.subtract).then_inc(o_lo, 1)

            def step_a(g, b):
                s = g * NB + b
                first = isinstance(g, int) and g == 0
                ln = layernorms("A", g, b)
                for t in range(NT):
                    dve.wait_ge(pj_hi, s * 6 + (t + 1))
                    dve.scalar_tensor_tensor(out=kt[:, t % 2, LO, :], in0=bank[t % 2][:, 0:256], scalar=0.0,
                                             in1=kt[:, t % 2, HI, :].bitcast(F32), op0=ALU.max, op1=ALU.subtract)
                    dve.tensor_tensor(vt[:, t % 2, LO, :, 0:P],
                                      bank[t % 2][:, 256:512].rearrange("p (a n) -> p a n", a=2),
                                      vt[:, t % 2, HI, :, 0:P].bitcast(F32), ALU.subtract).then_inc(pj_lo, 1)
                    if tail_of("A", g, b):
                        if t == 0:
                            invert(s, 1)
                        if t >= 2:
                            normalise(s, t % 2)
                    if first and t < 2:
                        stats(ln, (2 * t, 2 * t + 1))
                    elif first and t == 2 and ln:
                        ln_apply(*ln)
                    elif not first and t in (1, 2):
                        stats(ln, (2 * t - 2, 2 * t - 1))
                    if t in (1, 3):
                        mod_evac(g, b, t // 2)
                if tail_of("A", g, b):
                    out_lo(s, 0)
                    out_lo(s, 1)
                if ln and not first:
                    ln_apply(*ln)
                for pair in range(2):
                    dve.wait_ge(pj_hi, s * 6 + (5 + pair))
                    dve.scalar_tensor_tensor(out=qt[:, LO, pair, :], in0=bank[pair][:, :], scalar=0.0,
                                             in1=qt[:, HI, pair, :].bitcast(F32), op0=ALU.max,
                                             op1=ALU.subtract).then_inc(pj_lo, 1)
                if not first:
                    tail_evac("A", g, b, 0)
                dve.wait_ge(kvb_hi, s + 1)
                kv = bank[4][:, 0:2 * VW].rearrange("p (a n) -> p a n", a=2)
                for lo in (0, HD):
                    q = slice(lo, lo + HD)
                    dve.tensor_tensor(kvb[q, LO, :, 0, q], kv[q, :, q], kvb[q, HI, :, 0, q].bitcast(F32),
                                      ALU.subtract)
                    last = dve.tensor_tensor(kvb[q, LO, :, 1, q], kv[q, :, P:P + 1].to_broadcast([HD, 2, HD]),
                                             kvb[q, HI, :, 1, q].bitcast(F32), ALU.subtract)
                last.then_inc(kvb_lo, 1)
                mod_evac(g, b, 2)
                for t in range(0 if first else 1, NT):
                    tail_evac("A", g, b, t)
                for pair in range(2):
                    dve.wait_ge(nn_full, s * 4 + (pair + 1))
                    if tail_of("A", g, b):
                        dve.wait_ge(o_num, s * 2)
                    dve.tensor_scalar(rr[:, pair, :], bank[(5, 4)[pair]][:, :], 1e-6, None, ALU.max) \
                        .then_inc(r_max, 1)
                invert(s + 1, 0)
                if first and b == 3:
                    tuple_coefficients()

            def split_b(e, i):
                n = e * NSB + (BASE_B + i)
                dve.wait_ge(split_hi, n + 1)
                dve.wait_ge(split_done, n)
                dve.tensor_tensor(W2[:, i * 2048 + 1024:(i + 1) * 2048], stage[:, i, :],
                                  W2[:, i * 2048:i * 2048 + 1024].bitcast(F32), ALU.subtract) \
                    .then_inc(split_done, 1)

            def step_b(e, b):
                s = e * NB + b
                if isinstance(e, int) and e == 0 and b == 0:
                    invert(NB * GA, 1)
                    for part in (normalise, out_lo):
                        for pair in range(2):
                            part(NB * GA, pair)
                ln = layernorms("B", e, b)
                stats(ln, range(NT))
                for i in range(2):
                    dve.wait_ge(bu_full, s * 2 + (i + 1))
                    dve.wait_ge(b_silu, s * 2 + (i + 1))
                    if not (isinstance(e, int) and e == 0 and b == 0):
                        dve.wait_ge(b_lo, s * 2 + (i - 1))
                    dve.tensor_tensor(pr[:, i, :], sg[:, i, :], bank[4 + i][:, :], ALU.mult).then_inc(b_p, 1)
                    if b == 3 and not (isinstance(e, int) and e == GE - 1):
                        split_b(e + 1, i)
                    if ln and i == 0:
                        ln_apply(*ln)
                for t in range(NT):
                    tail_evac("B", e, b, t)
                if b == 0:
                    if not (isinstance(e, int) and e == 0):
                        dve.wait_ge(ring_read, ring_before("B", e, b) + NT)
                        link(dve.tensor_copy(rwe[:, :], rw[:, :, bass.ds(e, 1)].rearrange("p t a -> p (t a)")),
                             rwe_done, e)
                for i in range(2):
                    dve.wait_ge(b_hi, s * 2 + (i + 1))
                    dve.tensor_tensor(ab[:, LO, i, :], pr[:, i, :], ab[:, HI, i, :].bitcast(F32),
                                      ALU.subtract).then_inc(b_lo, 1)
                late("B", e, b)
                if isinstance(e, int) and e == 0:
                    seq(dve.tensor_copy(rwe[:, b * NT:(b + 1) * NT], rw[:, b * NT:(b + 1) * NT, 0]), "rt")
                    if b in (1, 3):
                        for j in range(2):
                            m = (b - 1) + j
                            dve.wait_ge(m_hi, m + 1)
                            dve.tensor_tensor(M[:, LO, m, :], bank[6 + j][:, :], M[:, HI, m, :].bitcast(F32),
                                              ALU.subtract).then_inc(m_lo, 1)

            def step_c(b):
                for t in range(NT):
                    tail_evac("C", 0, b, t)
                ln = layernorms("C", 0, b)
                stats(ln, range(NT))
                ln_apply(*ln)
                dve.wait_ge(y_sq, NT * (b + 1))
                seq(dve.tensor_scalar(ve[:, :], ssum[:, :], 1.0 / H, EPS_RMS, ALU.mult, ALU.add), "ln")
                inv_sqrt()
                dve.wait_ge(crow_full[2], 16 * (b + 1))
                for t in range(NT):
                    n = NT * b + t
                    if n >= 4:
                        dve.wait_ge(c_add, n - 3)
                    dve.scalar_tensor_tensor(out=yn[n % 4], in0=bank[YB[n % 6]][:, :],
                                             scalar=rstd[:, t:t + 1], in1=crow[:, 2, :], op0=ALU.mult,
                                             op1=ALU.mult).then_inc(y_read, 1)
                if gated_in("C", 0, b) is not None:
                    gated(gated_in("C", 0, b))

            def step_d(g, b):
                s = g * NB + b
                ln = layernorms("D", g, b)
                if ln and b == 0:
                    stats(ln, range(NT))
                    ln_apply(*ln)
                for r in range(4):
                    dve.wait_ge(du_full, s * 4 + (r + 1))
                    dve.wait_ge(d_silu, s * 4 + (r + 1))
                    dve.tensor_tensor(hh[:, r, :], hh[:, r, :], bank[4 + r % 2][:, :], ALU.mult).then_inc(d_h, 1)
                    if ln and b > 0 and r == 1:
                        stats(ln, range(NT))
                    if ln and b > 0 and r == 2:
                        ln_apply(*ln)
                done = [0]

                def op(ins):
                    done[0] += 1
                    ins.then_inc(d_sp, 1)

                def after(k):
                    dve.wait_ge(d_sp, s * NSP + k)

                c01, c23, fa, fb, fs, ft = (fl[:, i, :] for i in range(6))
                a = [ab4[:, r, :] for r in range(4)]
                tt = dve.tensor_tensor
                dve.wait_ge(d_abs, s * 4 + 2)
                op(tt(c01, a[0], a[1], ALU.is_ge))
                op(tt(mx[:, :], a[0], a[1], ALU.max))
                tail_evac("D", g, b, 0)
                op(tt(a[0], a[0], a[1], ALU.min))
                dve.wait_ge(d_abs, s * 4 + 4)
                op(tt(c23, a[2], a[3], ALU.is_ge))
                after(4)
                op(tt(a[1], a[2], a[3], ALU.max))
                tail_evac("D", g, b, 1)
                op(tt(a[2], a[2], a[3], ALU.min))
                after(5)
                op(tt(fb, a[0], a[1], ALU.is_ge))
                after(6)
                op(tt(fa, mx[:, :], a[2], ALU.is_ge))
                tail_evac("D", g, b, 2)
                after(8)
                op(tt(fs, fa, fb, ALU.add))
                after(9)
                op(tt(ft, fs, c01, ALU.add))
                op(tt(fa, fs, c01, ALU.subtract))
                op(tt(fb, fs, c23, ALU.subtract))
                op(tt(fs, fs, c23, ALU.add))
                tail_evac("D", g, b, 3)
                for r, (flag, bound, cmp) in enumerate(((ft, 2.0, ALU.is_ge), (fa, 1.0, ALU.is_ge),
                                                        (fb, 0.0, ALU.is_le), (fs, 1.0, ALU.is_le))):
                    after(10 + r)
                    op(dve.scalar_tensor_tensor(out=hh[:, r, :], in0=flag, scalar=bound, in1=hh[:, r, :],
                                                op0=cmp, op1=ALU.mult))
                assert done[0] == NSP
                if isinstance(g, int) and g == GD - 1 and b == NB - 1:
                    for r in range(4):
                        dve.wait_ge(d_hi, s * 4 + (r + 1))
                        dve.tensor_tensor(ad[:, r, LO, :], hh[:, r, :], ad[:, r, HI, :].bitcast(F32),
                                          ALU.subtract).then_inc(d_lo, 1)

            def epi():
                for t in range(NT):
                    tail_evac("end", GD - 1, 3, t)

            walk(dve, pro, step_a, step_b, step_c, step_d, epi)

        @block.gpsimd
        def _(pool):
            def lo_part(dst, src, hi):
                return pool.tensor_tensor(dst, src, hi.bitcast(F32), ALU.subtract)

            def wsplit(n, j, lo, hi, size):
                pool.wait_ge(split_hi, n + 1)
                if not (isinstance(n, int) and n == 0):
                    pool.wait_ge(split_done, n)
                lo_part(lo, stage[:, j % 2, 0:size], hi).then_inc(split_done, 1)

            def split_a(g, j):
                w, at = ((W1a, 0), (W1a, 1024), (W1b, 0), (W1b, 2048))[j]
                off = (2048, 2048, 1024, 1024)[j]
                wsplit(g * NSA + j, j, w[:, at + off:at + off + 1024], w[:, at:at + 1024], 1024)

            def split_b(e, j):
                n = e * NSB + (BASE_B + j)
                if j < 2:
                    wsplit(n, j, W2[:, j * 2048 + 1024:(j + 1) * 2048], W2[:, j * 2048:j * 2048 + 1024], 1024)
                else:
                    wsplit(n, j, Wd[:, LO, j - 2, :], Wd[:, HI, j - 2, :], 512)

            def split_d(g, j):
                n = g * NSD + (BASE_D + j)
                if j < 4:
                    w, at = (W1a, W1a, W1b, W1b)[j], (j % 2) * 2048
                    wsplit(n, j, w[:, at + 1024:at + 2048], w[:, at:at + 1024], 1024)
                else:
                    at = (j - 4) * 1024
                    wsplit(n, j, W2[:, 2048 + at:2048 + at + 1024], W2[:, at:at + 1024], 1024)

            def ln_out(ln, half):
                if ln is None:
                    return
                k, b = ln
                for i in range(2):
                    n, c = RING[("ln", k, b, half)] + i, 2 * half + i
                    pool.wait_ge(h_hi, ln_index(k, b) * NC + c + 1)
                    hs = slice(b * S, (b + 1) * S)
                    lo_part(hT[:, LO, c, hs], tmp[:, n % 2, :], hT[:, HI, c, hs]).then_inc(ring_done, 1)

            def gated_add(b):
                if b is not None:
                    if b == 3:
                        pool.wait_ge(c_add, NT * NB)
                    for t in range(NT):
                        pool.wait_ge(pq_sum, NT * b + t + 1)
                        xt = x[:, b * NT + t, :]
                        pool.tensor_tensor(xt, xt, xn_of(2, b)[:, t, :], ALU.add).then_inc(pq_add, 1)

            def extras(stage_, g, b):
                rt = routed(stage_, g, b)
                if rt is not None:
                    n = RING[("rt", rt)]
                    pool.wait_ge(ring_read, n + 1)
                    pool.tensor_copy(lg[:, :, :], tmp[:, n % 2, 0:NT * 8].rearrange("p (t e) -> p t e", t=NT)) \
                        .then_inc(ring_done, 1)

            def add_tail(tail, n0):
                ts, tg, tb = tail
                key = RING[("tail", ts, tg if isinstance(tg, int) else 1, tb)]
                for t in range(NT):
                    pool.wait_ge(ring_read, n0 + t + 1)
                    xt = x[:, tb * NT + t, :]
                    pool.tensor_tensor(xt, xt, tmp[:, (key + t) % 2, :], ALU.add).then_inc(ring_done, 1)

            def tails(stage_, g, b):
                tail = tail_of(stage_, g, b)
                if tail:
                    add_tail(tail, ring_before(stage_, g, b))

            def pro():
                pool.memset(ident[:, :], 0.0).then_inc(zeroed, 1)
                pool.wait_ge(zeroed, 1)
                pool.affine_select(out=ident[:, :], in_=ident[:, :], compare_op=ALU.not_equal, fill=1.0, base=0,
                                   pattern=[[-1, P]], channel_multiplier=1).then_inc(const_ready, 1)
                pool.dma_start(gwr[:, :, :], gwT).then_inc(gw_loaded, 16)
                pool.wait_ge(gw_loaded, 16)
                pool.tensor_copy(gw[:, HI, :, :], gwr[:, :, :]).then_inc(gw_hi_s, 1)
                pool.wait_ge(gw_hi_s, 1)
                lo_part(gw[:, LO, :, :], gwr[:, :, :], gw[:, HI, :, :]).then_inc(gw_ready, 1)
                split_a(0, 2)
                split_a(0, 3)

            def chained(ins):
                chain[0] += 1
                ins.then_inc(mod_chain, 1)
                pool.wait_ge(mod_chain, chain[0])

            chain = [0]

            def gate(v):
                sign = prow[:, SIGN, :]
                chained(pool.tensor_scalar(sign, v, 0.0, 2.0, ALU.is_ge, ALU.mult))
                chained(pool.tensor_scalar(sign, sign, -1.0, None, ALU.add))
                chained(pool.tensor_tensor(v, v, sign, ALU.mult))
                chained(pool.tensor_scalar(v, v, 0.25, None, ALU.max))
                chained(pool.tensor_tensor(v, v, sign, ALU.mult))

            def mod_out(g, b, place):
                for i, use in mod_uses(g, b, place):
                    n = RING[("mod", i, use)]
                    layer, part = MOD_PARTS[i]
                    pool.wait_ge(ring_read, n + 1)
                    if use == "col":
                        k, sc = 2 * layer + COL_KIND[part] // 2, COL_KIND[part] % 2
                        pool.tensor_scalar(modc[:, k, sc, :, :],
                                           tmp[:, n % 2, 0:16].rearrange("p (c b) -> p c b", c=NC),
                                           float(sc), None, ALU.add).then_inc(ring_done, 1)
                    else:
                        pool.memset(mark[:, i:i + 1], 0.0).then_inc(ring_done, 1)

            def mod_rows(g, b):
                for i in MOD_FINISH[b]:
                    kind, v = ROW_KIND[MOD_PARTS[i]], mod_row[i]
                    pool.wait_ge(ring_done, RING[("mod", i, "col" if MOD_PARTS[i][1] in COL_KIND else "row")] + 1)
                    if kind == R_GB1:
                        pool.wait_ge(row_stored[R_R1], 16)
                    if kind in (R_GA0, R_GB0, R_R1, R_GB1):
                        gate(v)
                    elif kind == R_Q1:
                        chained(pool.tensor_tensor(v, v, prow[:, GATE1, :], ALU.mult))
                    else:
                        chained(pool.tensor_scalar(v, v, 1.0, None, ALU.add))
                        chained(pool.tensor_tensor(v, v, prow[:, GATE1, :], ALU.mult))
                    if kind == R_R1:
                        v = prow[:, SIGN, :]
                        pool.dma_start(v, norm_w.partition_broadcast(NB)).then_inc(nw_loaded, 16)
                        pool.wait_ge(nw_loaded, 16)
                        chained(pool.tensor_tensor(v, v, prow[:, GATE1, :], ALU.mult))
                    pool.dma_start(rows_d[kind], v).then_inc(row_stored[kind], 16)

            def step_a(g, b):
                first = isinstance(g, int) and g == 0
                mod_out(g, b, 0)
                mod_out(g, b, 1)
                if b == 3 and not (isinstance(g, int) and g == GA - 1):
                    for j in range(2 if first else 3):
                        split_a(g + 1, j)
                if b == 3 and isinstance(g, int) and g == GA - 1:
                    split_b(0, 0)
                    split_b(0, 1)
                ln = layernorms("A", g, b)
                ln_out(ln, 0)
                if first:
                    ln_out(ln, 1)
                mod_out(g, b, 2)
                tails("A", g, b)
                if first:
                    if b == 3:
                        split_a(1, 2)
                    mod_rows(g, b)
                if b == 0 and not first:
                    split_a(g, 3)
                if not first:
                    ln_out(ln, 1)

            def step_b(e, b):
                ln = layernorms("B", e, b)
                ln_out(ln, 0)
                tails("B", e, b)
                if b == 0:
                    split_b(e, 2)
                    split_b(e, 3)
                ln_out(ln, 1)
                gated_add(gated_in("B", e, b))
                extras("B", e, b)

            def step_c(b):
                tails("C", 0, b)
                ln = layernorms("C", 0, b)
                if b == 2:
                    pool.wait_ge(pq_add, NT * 3)
                for t in range(NT):
                    n = NT * b + t
                    pool.wait_ge(y_read, n + 1)
                    xt = x[:, NT * b + t, :]
                    pool.tensor_tensor(xt, xt, yn[n % 4], ALU.add).then_inc(c_add, 1)
                ln_out(ln, 0)
                ln_out(ln, 1)
                if b < 2:
                    split_d(0, b)
                gated_add(gated_in("C", 0, b))

            def step_d(g, b):
                s = g * NB + b
                if isinstance(g, int) and g == 0 and b == 0:
                    split_d(0, 2)
                    split_d(0, 3)
                if b == 3 and not (isinstance(g, int) and g == GD - 1):
                    for j in range(4):
                        split_d(g + 1, j)
                ln = layernorms("D", g, b)
                ln_out(ln, 0)
                ln_out(ln, 1)
                tails("D", g, b)
                for r in range(4):
                    if isinstance(g, int) and g == GD - 1 and b == NB - 1:
                        break
                    pool.wait_ge(d_hi, s * 4 + (r + 1))
                    lo_part(ad[:, r, LO, :], hh[:, r, :], ad[:, r, HI, :]).then_inc(d_lo, 1)
                if b == 0:
                    split_d(g, 4)
                    split_d(g, 5)

            def epi():
                add_tail(("D", GD - 1, 3), RING[("tail", "D", GD - 1, 3)])

            walk(pool, pro, step_a, step_b, step_c, step_d, epi)


def kernel(**inputs):
    import numpy as np
    import concourse.bacc as bacc
    from concourse.bass_utils import run_bass_kernel_spmd as run

    a = {k: np.asarray(v) for k, v in inputs.items()}

    def chunks(w):
        return w.reshape(-1, P, w.shape[-1]).transpose(1, 0, 2)

    gw_ = 256
    wk, wv, wq = (chunks(a[f"L0_attn_W{n}"]).reshape(P, NC, GA, gw_) for n in "kvq")
    kv = np.concatenate([wk, wv], axis=3).transpose(2, 0, 1, 3).reshape(GA, P, 2, 1024)
    wa = np.concatenate([kv, wq.transpose(2, 0, 1, 3).reshape(GA, P, 1, 1024),
                         a["L0_attn_Wo"].reshape(GA, 2, P, H).transpose(0, 2, 1, 3).reshape(GA, P, 1, 1024)], axis=2)
    def up(w):
        return w.reshape(GE, 2, P, NC, P).transpose(0, 4, 1, 3, 2)
    gu_ = np.stack([up(a["L0_ffn_gate_proj_w"]), up(a["L0_ffn_up_proj_w"])], axis=3).reshape(GE, P, 2048)
    dn_ = a["L0_ffn_down_proj_w"].reshape(GE, H, 2, P).transpose(0, 3, 2, 1).reshape(GE, P, 1024)
    wbe = np.concatenate([gu_, dn_], axis=2)
    def cols(w):
        return w.reshape(NC, P, GD, P, 4).transpose(2, 1, 4, 0, 3)
    gud_ = np.stack([cols(a["L1_ffn_w_gate"]), cols(a["L1_ffn_w_up"])], axis=3).reshape(GD, P, 4, 1024)
    dnd_ = a["L1_ffn_w_down"].reshape(GD, P, 4, H).reshape(GD, P, 2, 1024)
    wdn = np.concatenate([gud_, dnd_], axis=2)
    winout = np.concatenate([a["L1_attn_W_in"].reshape(8, P, H),
                             a["L1_attn_W_out"].T.reshape(8, P, H)], axis=2)
    coef = np.stack([a[f"L1_attn_{n}"].reshape(8, P, DS).transpose(1, 0, 2)
                     for n in ("A_theta", "B_real", "B_imag", "C_real", "C_imag")], axis=1)
    cT = np.stack([a[f"L{i}_c"].T.reshape(NC, P, NB).transpose(1, 0, 2) for i in range(2)], axis=1)
    wmods = [a[f"L{i}_wmod"].reshape(NC, P, 6, H).transpose(2, 1, 0, 3).reshape(6, P, NC * H) for i in range(2)]
    arrays = {
        "x_in": a["L0_attn_hidden_states"], "wa": wa, "wbe": wbe, "wdn": wdn, "winout": winout, "coef": coef,
        "cT": cT, "wmod0": wmods[0], "wmod1": wmods[1],
        "gwT": chunks(a["L0_ffn_gate_w"].T), "bo": a["L0_attn_bo"], "norm_w": a["L1_attn_norm_w"],
    }
    arrays = {k: np.ascontiguousarray(v) for k, v in arrays.items()}

    nc = bacc.Bacc("TRN2", target_bir_lowering=False, num_devices=1)
    args = [nc.dram_tensor(k, v.shape, F32, kind="ExternalInput").ap() for k, v in arrays.items()]
    out = nc.dram_tensor("out", (NB, S, H), F32, kind="ExternalOutput").ap()
    rows_d = nc.dram_tensor("rows_d", (6, NB, H), F32, kind="Internal").ap()
    build(nc, *args, out, rows_d)
    r = run(nc, [arrays], core_ids=[0])
    return r.results[0]["out"]
```
